# Optimizing a Trainium2 kernel written in Bass

```python
import numpy as np
import jax
import jax.numpy as jnp

def _softmax(x, axis=-1):
    return jax.nn.softmax(x, axis=axis)

def _gelu(x):
    return jax.nn.gelu(x, approximate=True)

def _silu(x):
    return jax.nn.silu(x)

def _sigmoid(x):
    return jax.nn.sigmoid(x)

def _layernorm(x, axis=-1, eps=1e-05):
    m = jnp.mean(x, axis=axis, keepdims=True)
    v = jnp.var(x, axis=axis, keepdims=True)
    return (x - m) / jnp.sqrt(v + eps)

def _scatter_add(tgt, idx, src, axis=0):
    return tgt.at[idx].add(src)

def _segment_sum(src, seg, n):
    return jax.ops.segment_sum(src, seg, n)
kernel_name = 'mk_gnn_preln_d4_gnn_r64_beb694'

def setup_inputs(seed: int=0):
    np.random.seed(seed)
    _w = jnp.asarray

    def _rec_inputs():
        import jax
        import jax.numpy as jnp
        _gk = jax.random.key(seed)
        x = -0.0003929 + 0.9999 * jax.random.normal(jax.random.fold_in(_gk, 1), (512, 512), jnp.float32)
        src = jax.random.randint(jax.random.fold_in(_gk, 2), (8192,), 0, 512, jnp.int32)
        dst = jnp.minimum((512 * jax.random.uniform(jax.random.fold_in(_gk, 3), (8192,)) ** 2.0).astype(jnp.int32), 32767)
        _o = jnp.argsort(dst, stable=True)
        src = src[_o]
        dst = dst[_o]
        edge_attr_8 = -4.48278e-06 + 1.00019 * jax.random.normal(jax.random.fold_in(_gk, 12), (8192, 8), jnp.float32)
        return (x, src, dst, edge_attr_8)
    x, src, dst, edge_attr_8 = _rec_inputs()

    def _L0_gnn_setup():
        import jax, jax.numpy as jnp
        import numpy as np
        L, C, H, E = (512, 512, 8, 16384)
        D = C // H
        HID = 1024
        EPS = 1e-05

        def _ln(x, g, b):
            mu = jnp.mean(x, axis=-1, keepdims=True)
            var = jnp.var(x, axis=-1, keepdims=True)
            return (x - mu) * jax.lax.rsqrt(var + EPS) * g + b

        def _sparse_attention(z, row, col, bias, Wq, bq, Wk, bk, Wv, bv, Wo, bo):
            q = (z @ Wq + bq).reshape(L, H, D)
            k = (z @ Wk + bk).reshape(L, H, D)
            v = (z @ Wv + bv).reshape(L, H, D)
            scale = 1.0 / jnp.sqrt(jnp.asarray(D, z.dtype))
            scores = jnp.einsum('ehd,ehd->eh', q[row], k[col]) * scale + bias
            m = jax.ops.segment_max(scores, row, num_segments=L)
            p = jnp.exp(scores - m[row])
            ssum = jax.ops.segment_sum(p, row, num_segments=L)
            alpha = p / ssum[row]
            out = jax.ops.segment_sum(alpha[:, :, None] * v[col], row, num_segments=L)
            return out.reshape(L, C) @ Wo + bo
        key = jax.random.key(seed)
        ks = jax.random.split(key, 12)
        s = 0.02
        inp = {'x': jax.random.normal(ks[0], (L, C), jnp.float32), 'row_index': jnp.sort(jax.random.randint(ks[1], (E,), 0, L)), 'col_index': jax.random.randint(ks[2], (E,), 0, L), 'att_bias': jax.random.normal(ks[3], (E, H), jnp.float32), 'Wq': jax.random.normal(ks[4], (C, C), jnp.float32) * s, 'bq': jnp.zeros((C,), jnp.float32), 'Wk': jax.random.normal(ks[5], (C, C), jnp.float32) * s, 'bk': jnp.zeros((C,), jnp.float32), 'Wv': jax.random.normal(ks[6], (C, C), jnp.float32) * s, 'bv': jnp.zeros((C,), jnp.float32), 'Wo': jax.random.normal(ks[7], (C, C), jnp.float32) * s, 'bo': jnp.zeros((C,), jnp.float32), 'ln1_g': jnp.ones((C,), jnp.float32), 'ln1_b': jnp.zeros((C,), jnp.float32), 'ln2_g': jnp.ones((C,), jnp.float32), 'ln2_b': jnp.zeros((C,), jnp.float32), 'W1': jax.random.normal(ks[8], (C, HID), jnp.float32) * s, 'b1': jnp.zeros((HID,), jnp.float32), 'W2': jax.random.normal(ks[9], (HID, C), jnp.float32) * s, 'b2': jnp.zeros((C,), jnp.float32)}
        return inp
    _L0_gnn_all = _L0_gnn_setup()
    _L0_gnn_in = {k: v for k, v in _L0_gnn_all.items() if k in ('Wq', 'bq', 'Wk', 'bk', 'Wv', 'bv', 'Wo', 'bo', 'ln1_g', 'ln1_b', 'ln2_g', 'ln2_b', 'W1', 'b1', 'W2', 'b2')}
    del _L0_gnn_all

    def _L1_gnn_setup():
        import jax, jax.numpy as jnp
        import numpy as np
        N, E, D = (50000, 6250, 512)
        EPS = 1e-05
        key = jax.random.key(seed)
        ks = jax.random.split(key, 5)
        scale = 1.0 / np.sqrt(D)
        x = jax.random.normal(ks[0], (N, D), dtype=jnp.float32)
        edge_index = jax.random.randint(ks[1], (2, E), 0, N, dtype=jnp.int32)
        W_l = jax.random.normal(ks[2], (D, D), dtype=jnp.float32) * scale
        b_l = jnp.zeros((D,), dtype=jnp.float32)
        W_r = jax.random.normal(ks[3], (D, D), dtype=jnp.float32) * scale
        gamma = jnp.ones((D,), dtype=jnp.float32)
        beta = jnp.zeros((D,), dtype=jnp.float32)
        return {'x': x, 'edge_index': edge_index, 'W_l': W_l, 'b_l': b_l, 'W_r': W_r, 'gamma': gamma, 'beta': beta}
    _L1_gnn_all = _L1_gnn_setup()
    _L1_gnn_in = {k: v for k, v in _L1_gnn_all.items() if k in ('W_l', 'b_l', 'W_r', 'gamma', 'beta')}
    del _L1_gnn_all

    def _L2_gnn_setup():
        import jax, jax.numpy as jnp
        import numpy as np
        N_NODES = 10000

        def gcn_conv(x, edge_index, W, b):
            n = x.shape[0]
            loop = jnp.arange(n)
            src = jnp.concatenate([edge_index[0], loop])
            dst = jnp.concatenate([edge_index[1], loop])
            deg = jax.ops.segment_sum(jnp.ones_like(dst, dtype=x.dtype), dst, num_segments=n)
            dinv = jnp.where(deg > 0, jax.lax.rsqrt(deg), 0.0)
            norm = dinv[src] * dinv[dst]
            h = x @ W
            msg = h[src] * norm[:, None]
            out = jax.ops.segment_sum(msg, dst, num_segments=n)
            return out + b
        key = jax.random.key(seed)
        k1, k2, k3, k4 = jax.random.split(key, 4)
        c = [512, 1024, 512]
        x = jax.random.normal(k1, (N_NODES, c[0]), dtype=jnp.float32)
        edge_index = jax.random.randint(k2, (2, 2500), 0, N_NODES, dtype=jnp.int64)
        W1 = jax.random.normal(k3, (c[0], c[1]), dtype=jnp.float32) / np.sqrt(c[0])
        b1 = jnp.zeros((c[1],), dtype=jnp.float32)
        W2 = jax.random.normal(k4, (c[1], c[2]), dtype=jnp.float32) / np.sqrt(c[1])
        b2 = jnp.zeros((c[2],), dtype=jnp.float32)
        return {'x': x, 'edge_index': edge_index, 'W1': W1, 'b1': b1, 'W2': W2, 'b2': b2}
    _L2_gnn_all = _L2_gnn_setup()
    _L2_gnn_in = {k: v for k, v in _L2_gnn_all.items() if k in ('W1', 'b1', 'W2', 'b2')}
    del _L2_gnn_all

    def _L3_gnn_setup():
        import jax, jax.numpy as jnp
        import numpy as np
        N, D, E = (50000, 512, 6250)
        LN_EPS = 1e-05
        key = jax.random.key(seed)
        ks = jax.random.split(key, 8)
        x = jax.random.normal(ks[0], (N, D), dtype=jnp.float32)
        edge_index = jax.random.randint(ks[1], (2, E), 0, N, dtype=jnp.int64)
        s = 1.0 / np.sqrt(D)
        W1 = jax.random.uniform(ks[2], (D, D), jnp.float32, -s, s)
        b1 = jax.random.uniform(ks[3], (D,), jnp.float32, -s, s)
        W2 = jax.random.uniform(ks[4], (D, D), jnp.float32, -s, s)
        b2 = jax.random.uniform(ks[5], (D,), jnp.float32, -s, s)
        eps = jnp.zeros((), dtype=jnp.float32)
        gamma = jnp.ones((D,), dtype=jnp.float32)
        beta = jnp.zeros((D,), dtype=jnp.float32)
        return {'x': x, 'edge_index': edge_index, 'eps': eps, 'W1': W1, 'b1': b1, 'W2': W2, 'b2': b2, 'gamma': gamma, 'beta': beta}
    _L3_gnn_all = _L3_gnn_setup()
    _L3_gnn_in = {k: v for k, v in _L3_gnn_all.items() if k in ('eps', 'W1', 'b1', 'W2', 'b2', 'gamma', 'beta')}
    del _L3_gnn_all
    return {'x': x, 'src': src, 'dst': dst, 'edge_attr_8': edge_attr_8, 'L0_gnn_Wq': _L0_gnn_in['Wq'], 'L0_gnn_bq': _L0_gnn_in['bq'], 'L0_gnn_Wk': _L0_gnn_in['Wk'], 'L0_gnn_bk': _L0_gnn_in['bk'], 'L0_gnn_Wv': _L0_gnn_in['Wv'], 'L0_gnn_bv': _L0_gnn_in['bv'], 'L0_gnn_Wo': _L0_gnn_in['Wo'], 'L0_gnn_bo': _L0_gnn_in['bo'], 'L0_gnn_ln1_g': _L0_gnn_in['ln1_g'], 'L0_gnn_ln1_b': _L0_gnn_in['ln1_b'], 'L0_gnn_ln2_g': _L0_gnn_in['ln2_g'], 'L0_gnn_ln2_b': _L0_gnn_in['ln2_b'], 'L0_gnn_W1': _L0_gnn_in['W1'], 'L0_gnn_b1': _L0_gnn_in['b1'], 'L0_gnn_W2': _L0_gnn_in['W2'], 'L0_gnn_b2': _L0_gnn_in['b2'], 'L1_gnn_W_l': _L1_gnn_in['W_l'], 'L1_gnn_b_l': _L1_gnn_in['b_l'], 'L1_gnn_W_r': _L1_gnn_in['W_r'], 'L1_gnn_gamma': _L1_gnn_in['gamma'], 'L1_gnn_beta': _L1_gnn_in['beta'], 'L2_gnn_W1': _L2_gnn_in['W1'], 'L2_gnn_b1': _L2_gnn_in['b1'], 'L2_gnn_W2': _L2_gnn_in['W2'], 'L2_gnn_b2': _L2_gnn_in['b2'], 'L3_gnn_eps': _L3_gnn_in['eps'], 'L3_gnn_W1': _L3_gnn_in['W1'], 'L3_gnn_b1': _L3_gnn_in['b1'], 'L3_gnn_W2': _L3_gnn_in['W2'], 'L3_gnn_b2': _L3_gnn_in['b2'], 'L3_gnn_gamma': _L3_gnn_in['gamma'], 'L3_gnn_beta': _L3_gnn_in['beta']}

def reference(x, src, dst, edge_attr_8, L0_gnn_Wq, L0_gnn_bq, L0_gnn_Wk, L0_gnn_bk, L0_gnn_Wv, L0_gnn_bv, L0_gnn_Wo, L0_gnn_bo, L0_gnn_ln1_g, L0_gnn_ln1_b, L0_gnn_ln2_g, L0_gnn_ln2_b, L0_gnn_W1, L0_gnn_b1, L0_gnn_W2, L0_gnn_b2, L1_gnn_W_l, L1_gnn_b_l, L1_gnn_W_r, L1_gnn_gamma, L1_gnn_beta, L2_gnn_W1, L2_gnn_b1, L2_gnn_W2, L2_gnn_b2, L3_gnn_eps, L3_gnn_W1, L3_gnn_b1, L3_gnn_W2, L3_gnn_b2, L3_gnn_gamma, L3_gnn_beta):
    import jax
    import jax.numpy as jnp

    def _L0_gnn_ref(x, att_bias, Wq, bq, Wk, bk, Wv, bv, Wo, bo, ln1_g, ln1_b, ln2_g, ln2_b, W1, b1, W2, b2, row_index, col_index):
        import jax, jax.numpy as jnp
        import numpy as np
        L, C, H, E = (512, 512, 8, 16384)
        D = C // H
        HID = 1024
        EPS = 1e-05

        def _ln(x, g, b):
            mu = jnp.mean(x, axis=-1, keepdims=True)
            var = jnp.var(x, axis=-1, keepdims=True)
            return (x - mu) * jax.lax.rsqrt(var + EPS) * g + b

        def _sparse_attention(z, row, col, bias, Wq, bq, Wk, bk, Wv, bv, Wo, bo):
            q = (z @ Wq + bq).reshape(L, H, D)
            k = (z @ Wk + bk).reshape(L, H, D)
            v = (z @ Wv + bv).reshape(L, H, D)
            scale = 1.0 / jnp.sqrt(jnp.asarray(D, z.dtype))
            scores = jnp.einsum('ehd,ehd->eh', q[row], k[col]) * scale + bias
            m = jax.ops.segment_max(scores, row, num_segments=L)
            p = jnp.exp(scores - m[row])
            ssum = jax.ops.segment_sum(p, row, num_segments=L)
            alpha = p / ssum[row]
            out = jax.ops.segment_sum(alpha[:, :, None] * v[col], row, num_segments=L)
            return out.reshape(L, C) @ Wo + bo
        z = _ln(x, ln1_g, ln1_b)
        att = _sparse_attention(z, row_index, col_index, att_bias, Wq, bq, Wk, bk, Wv, bv, Wo, bo)
        x = x + att
        z = _ln(x, ln2_g, ln2_b)
        ff = jax.nn.silu(z @ W1 + b1) @ W2 + b2
        return x + ff

    def _L1_gnn_ref(x, edge_index, W_l, b_l, W_r, gamma, beta):
        import jax, jax.numpy as jnp
        import numpy as np
        N, E, D = (50000, 6250, 512)
        EPS = 1e-05
        n = x.shape[0]
        src, dst = (edge_index[0], edge_index[1])
        agg = jax.ops.segment_sum(x[src], dst, num_segments=n)
        cnt = jax.ops.segment_sum(jnp.ones((src.shape[0],), x.dtype), dst, num_segments=n)
        mean_agg = agg / jnp.maximum(cnt, 1.0)[:, None]
        h = mean_agg @ W_l.T + b_l + x @ W_r.T
        mu = jnp.mean(h, axis=0)
        var = jnp.var(h, axis=0)
        h = (h - mu) * jax.lax.rsqrt(var + EPS) * gamma + beta
        return jax.nn.relu(h) + x

    def _L2_gnn_ref(x, edge_index, W1, b1, W2, b2):
        import jax, jax.numpy as jnp
        import numpy as np
        N_NODES = 10000

        def gcn_conv(x, edge_index, W, b):
            n = x.shape[0]
            loop = jnp.arange(n)
            src = jnp.concatenate([edge_index[0], loop])
            dst = jnp.concatenate([edge_index[1], loop])
            deg = jax.ops.segment_sum(jnp.ones_like(dst, dtype=x.dtype), dst, num_segments=n)
            dinv = jnp.where(deg > 0, jax.lax.rsqrt(deg), 0.0)
            norm = dinv[src] * dinv[dst]
            h = x @ W
            msg = h[src] * norm[:, None]
            out = jax.ops.segment_sum(msg, dst, num_segments=n)
            return out + b
        h = jax.nn.relu(gcn_conv(x, edge_index, W1, b1))
        h = jax.nn.relu(gcn_conv(h, edge_index, W2, b2))
        return h

    def _L3_gnn_ref(x, edge_index, eps, W1, b1, W2, b2, gamma, beta):
        import jax, jax.numpy as jnp
        import numpy as np
        N, D, E = (50000, 512, 6250)
        LN_EPS = 1e-05
        i, j = (edge_index[0], edge_index[1])
        agg = jax.ops.segment_sum(x[j], i, num_segments=x.shape[0])
        h = (1.0 + eps) * x + agg
        h = jax.nn.relu(h @ W1.T + b1)
        h = h @ W2.T + b2
        mu = jnp.mean(h, axis=-1, keepdims=True)
        var = jnp.var(h, axis=-1, keepdims=True)
        out = (h - mu) * jax.lax.rsqrt(var + LN_EPS) * gamma + beta
        return out
    edge_index = jnp.stack([src, dst])
    h = jnp.maximum(_layernorm(x, axis=-1), 0.0)
    x = x + _L0_gnn_ref(h, edge_attr_8, L0_gnn_Wq, L0_gnn_bq, L0_gnn_Wk, L0_gnn_bk, L0_gnn_Wv, L0_gnn_bv, L0_gnn_Wo, L0_gnn_bo, L0_gnn_ln1_g, L0_gnn_ln1_b, L0_gnn_ln2_g, L0_gnn_ln2_b, L0_gnn_W1, L0_gnn_b1, L0_gnn_W2, L0_gnn_b2, src, dst)
    h = jnp.maximum(_layernorm(x, axis=-1), 0.0)
    x = x + _L1_gnn_ref(h, edge_index, L1_gnn_W_l, L1_gnn_b_l, L1_gnn_W_r, L1_gnn_gamma, L1_gnn_beta)
    h = jnp.maximum(_layernorm(x, axis=-1), 0.0)
    x = x + _L2_gnn_ref(h, edge_index, L2_gnn_W1, L2_gnn_b1, L2_gnn_W2, L2_gnn_b2)
    h = jnp.maximum(_layernorm(x, axis=-1), 0.0)
    x = x + _L3_gnn_ref(h, edge_index, L3_gnn_eps, L3_gnn_W1, L3_gnn_b1, L3_gnn_W2, L3_gnn_b2, L3_gnn_gamma, L3_gnn_beta)
    return x

_drawn_inputs = setup_inputs


def setup_inputs(seed=0):
    import zlib

    import numpy as np

    out = dict(_drawn_inputs(seed))
    spreads = {'L0_gnn_bq': (0.0, 0.8),
     'L0_gnn_bk': (0.0, 2.0),
     'L0_gnn_bv': (0.0, 0.307),
     'L0_gnn_bo': (0.0, 0.1),
     'L0_gnn_ln1_g': (1.0, 0.6),
     'L0_gnn_ln1_b': (0.0, 0.758),
     'L0_gnn_ln2_g': (1.0, 0.6),
     'L0_gnn_ln2_b': (0.0, 0.8),
     'L0_gnn_b1': (0.0, 0.429),
     'L0_gnn_b2': (0.0, 0.1),
     'L1_gnn_b_l': (0.0, 2.0),
     'L1_gnn_gamma': (1.0, 0.2),
     'L1_gnn_beta': (0.0, 0.292),
     'L2_gnn_b1': (0.0, 0.39),
     'L2_gnn_b2': (0.0, 0.306),
     'L3_gnn_gamma': (1.0, 0.2),
     'L3_gnn_beta': (0.0, 0.1)}
    factors = {'L0_gnn_Wq': 7.602,
     'L0_gnn_Wk': 7.372,
     'L3_gnn_b1': 24.412,
     'L3_gnn_b2': 8.0,
     'edge_attr_8': 2.878}
    for name, (base, spread) in spreads.items():
        noise = np.random.default_rng([zlib.crc32(name.encode()), seed]).standard_normal(out[name].shape)
        drawn = base * np.exp(spread * noise) if base else spread * noise
        out[name] = jnp.asarray(drawn.astype(out[name].dtype))
    for name, factor in factors.items():
        out[name] = (out[name] * factor).astype(out[name].dtype)
    return out
```

```python
from contextlib import ExitStack

import concourse.bass as bass
from concourse import mybir

ALU = mybir.AluOpType
ACT = mybir.ActivationFunctionType
AX = mybir.AxisListType
F32 = mybir.dt.float32
BF16 = mybir.dt.bfloat16
F16 = mybir.dt.float16
I32 = mybir.dt.int32
U32 = mybir.dt.uint32

P = 128
N = 512
D = 512
F = 1024
H = 8
DH = D // H
E = 8192
NT = N // P
FT = F // P
ET = E // P
BS = 16
NB = N // BS
GT = ET + NB
REC = 2 + H
HB = 4
LN_EPS = 1e-5
NO_EDGE = -1e30
M_FLOOR = -1e25
EXP_CAP = 80.0
W_SHIFT = 60.0
TINY = 1e-37

COLS = {}
for _name, _tiles in (("bq", NT), ("bk", NT), ("ln1_g", NT), ("ln1_b", NT), ("ln2_g", NT), ("ln2_b", NT),
                      ("b1_0", FT), ("b_l", NT), ("gamma1", NT), ("beta1", NT), ("b1_2", FT), ("b1_3", NT)):
    COLS[_name] = (sum(t for _, t in COLS.values()), _tiles)
N_COLS = sum(t for _, t in COLS.values())
ROWS = ("bv", "bo", "b2_0", "b2_2", "b2_3", "gamma3", "beta3")


def gnn_kernel(nc, x, src, dst, bias, eps, cols, rows, wq, wk, wv, wo, w1_0, w2_0,
               wl_t, wr_t, w1_2, w2_2, w1_3t, w2_3t, out):
    ctx = ExitStack()
    with ctx:
        def sb(name, shape, dt=F32):
            return ctx.enter_context(nc.sbuf_tensor(name, shape, dt))

        def sem(name):
            return ctx.enter_context(nc.semaphore(name))

        def k_major(w):
            return w.rearrange("(k p) n -> p k n", p=P)

        x_sb = sb("x_sb", [P, NT, D])
        h_sb = sb("h_sb", [P, NT, D])
        z_sb = sb("z_sb", [P, NT, D])
        t_sb = sb("t_sb", [P, NT, N])
        q_t = sb("q_t", [P, NT, N])
        k_t = sb("k_t", [P, NT, N])
        v_sb = sb("v_sb", [P, NT, H, DH + 1])
        c1 = sb("c1", [P, NT, N])
        wide = sb("wide", [P, FT, N])
        big = sb("big", [P, NT * H, N])
        wslot = sb("wslot", [P, 4, NT, D])
        row_bc = sb("row_bc", [P, len(ROWS), D])
        col = sb("col", [P, N_COLS])
        bq8 = sb("bq8", [P, NT])
        idx_src = sb("idx_src", [P, ET], I32)
        idx_dst = sb("idx_dst", [P, ET], I32)
        src_i = sb("src_i", [P, ET], I32)
        src_f = sb("src_f", [P, ET])
        dst_f = sb("dst_f", [P, ET])
        blk_f = sb("blk_f", [P, ET])
        bmax = sb("bmax", [P, H])
        bmax_all = sb("bmax_all", [P, H])
        wpart = sb("wpart", [P, GT, 3, H], BF16)
        iota_n = sb("iota_n", [P, N], F16)
        iota_b = sb("iota_b", [P, NB])
        ident = sb("ident", [P, P])
        ident_b = sb("ident_b", [P, P], BF16)
        before = sb("before", [P, P])
        ones = sb("ones", [P, P])
        pos_f = sb("pos_f", [P, ET])
        pos_i = sb("pos_i", [P, ET], I32)
        pos_lo = sb("pos_lo", [P, ET], I32)
        pos_hi = sb("pos_hi", [P, ET], I32)
        row_i = sb("row_i", [P, ET], I32)
        ntile_f = sb("ntile_f", [P, NB])
        ntile_i = sb("ntile_i", [P, NB], I32)
        blk_n = sb("blk_n", [P, NB])
        base_f = sb("base_f", [P, NB])
        tile_end = sb("tile_end", [P, NB])
        m_col = sb("m_col", [P, NT, H])
        m_neg = sb("m_neg", [P, NT, H])
        m_res = sb("m_res", [P, NT, H])
        m_hl = sb("m_hl", [P, NT, 2 * H], BF16)
        m_t = sb("m_t", [2 * H, N], BF16)
        sel = sb("sel", [2 * H, H, P], BF16)
        eps_c = sb("eps_c", [P, 1])
        gin_c = sb("gin_c", [P, 1])
        zero_b = sb("zero_b", [P, P], BF16)
        stats = sb("stats", [P, NT, 6])
        mv = sb("mv", [P, NT, 2])
        std = sb("std", [P, NT])
        rstd = sb("rstd", [P, NT])
        shift = sb("shift", [P, NT])
        rsum = sb("rsum", [P, NT, 4])
        dinv_c = sb("dinv_c", [P, NT])

        flat = big[:, :, :].rearrange("p a n -> p (a n)")
        onehot = flat[:, 0:NB * ET]
        prefix = flat[:, NB * ET:2 * NB * ET]
        keep = flat[:, 2 * NB * ET:3 * NB * ET]
        hot_ring = flat[:, 3 * NB * ET:3 * NB * ET + 2 * 2 * HB * N // 2].bitcast(BF16).rearrange(
            "p (r u s n) -> p r u s n", r=2, u=HB, s=2)
        spare = flat[:, (3 * NB * ET + 2 * 2 * HB * N // 2):]
        att_b = spare[:, 0:ET * H].rearrange("p (t h) -> p t h", h=H)
        rec = spare[:, ET * H:ET * (H + REC)].rearrange("p (t r) -> p t r", r=REC)
        iota_i = spare[:, ET * (H + REC):ET * (H + REC) + N].bitcast(I32)
        wrest = z_sb[:, :, :].rearrange("p t n -> p (t n)")[:, 0:GT * H].rearrange("p (g h) -> p g h", h=H)
        wpart_f = wpart[:, :, :, :].rearrange("p g k h -> p (g k h)").bitcast(F32)
        rcnt_bc = wpart_f[:, 0:N]
        dinv_bc = wpart_f[:, N:2 * N]
        srec = z_sb[:, :, :].rearrange("p t n -> p (t n)")[:, GT * H:GT * (H + REC)].rearrange(
            "p (g r) -> p g r", r=REC)
        wide_b = wide[:, :, :].rearrange("p a n -> p (a n)").bitcast(BF16)
        no_edge = wide_b[:, 0:NT * N].rearrange("p (t n) -> p t n", t=NT)
        w_ring = wide_b[:, 0:2 * HB * 3 * P].rearrange("p (r u k c) -> p r u k c", r=2, u=HB, k=3)
        d_ring = wide_b[:, 2 * HB * 3 * P:2 * HB * (3 * P + N)].rearrange("p (r u n) -> p r u n", r=2, u=HB)
        w1_0s = big[:, 0:8, :].rearrange("p (k a) n -> p k (a n)", a=2)
        w2_0s = big[:, 8:16, :]
        wl_s, wr_s = big[:, 16:20, :], big[:, 20:24, :]
        w1_3s, w2_3s = big[:, 24:28, :], big[:, 28:32, :]
        w1_2s = wslot[:, 0:2, :, :].rearrange("p s (k a) n -> p (s k) (a n)", a=2)
        w2_2s = wslot[:, 2:4, :, :].rearrange("p s k n -> p (s k) n")
        c1_loop, c2_loop = q_t, k_t

        def colp(name, t):
            a, _ = COLS[name]
            return col[:, a + t:a + t + 1]

        def rowp(name):
            return row_bc[:, ROWS.index(name), :]

        bank = [ctx.enter_context(nc.psum_tensor(f"bank{i}", [P, 512], F32)) for i in range(8)]

        sorted_d = nc.dram_tensor("sorted_records", [GT * P, REC], F32)

        S = {name: sem(name) for name in (
            "x_in", "src_in", "dst_in", "bias_in", "cols_in", "rows_in", "eps_in",
            "wq_in", "wk_in", "wv_in", "wo_in", "w1_0_in", "w2_0_in", "wl_in", "wr_in",
            "w1_2_in", "w2_2_in", "w1_3_in", "w2_3_in", "srec_in", "cleared", "scattered", "out_done",
            "vector_order", "scalar_order", "pool_order",
            "consts", "eps_column", "bias_col", "zeroed", "ln_var", "ln_std", "ln_coef", "h_ready", "z_ready",
            "edge_sums", "edge_bases", "bias_top", "bias_top_all", "bias_low", "rec_ready", "weights_exp",
            "rows_made", "tiles_made",
            "turned", "t_ready", "q_mm", "q_ready", "k_mm", "k_ready", "v_mm", "v_ready",
            "hot_ready", "hot_used", "c1_mm", "c1_ready", "no_edge_ready", "score_mm", "score_max",
            "shift_ready", "shift_mm", "shift_t", "wd_ready", "wd_used", "b_mm", "b_ready",
            "st_mm", "capped", "e_ready", "p_ready", "pv_mm", "att_ready", "bigfree", "wslotfree",
            "wo_mm", "x1h_ready", "ff1_mm", "ff1_ready", "ff2_mm",
            "deg_mm", "deg_std", "deg_ready", "c1i_ready", "c2_mm", "c2_ready", "h_base",
            "agg1_mm", "agg1_ready", "lin1_mm", "lin1_ready", "bn_var", "bn_std", "bn_coef", "bn_ready",
            "back_mm", "y_ready", "agg2_mm", "agg2_ready", "gcn1_mm", "gcn1_ready", "gcn2_mm", "gcn2_ready",
            "agg2b_mm", "agg3_mm", "agg3_ready", "gin1_mm", "gin1_ready", "gin2_mm", "out_ready")}
        block = ctx.enter_context(nc.Block())

        @block.sync
        def _(sp):
            sp.dma_start(x_sb[:, :, :], k_major(x)).then_inc(S["x_in"], 16)
            sp.dma_start(wslot[:, 0, :, :], k_major(wq)).then_inc(S["wq_in"], 16)
            sp.dma_start(wslot[:, 1, :, :], k_major(wk)).then_inc(S["wk_in"], 16)
            sp.dma_start(wslot[:, 2, :, :], k_major(wv)).then_inc(S["wv_in"], 16)
            for n in range(len(ROWS)):
                sp.dma_start(row_bc[:, n, :], rows[n:n + 1, :].partition_broadcast(P)
                             ).then_inc(S["rows_in"], 16)
            sp.wait_ge(S["zeroed"], 1)
            sp.dma_start(sorted_d[:, :].rearrange("(p g) r -> p (g r)", p=P),
                         srec[:, :, :].rearrange("p g r -> p (g r)")).then_inc(S["cleared"], 16)
            sp.dma_start(wslot[:, 3, :, :], k_major(wo)).then_inc(S["wo_in"], 16)
            sp.wait_ge(S["scattered"], 16 * ET)
            sp.wait_ge(S["turned"], NT)
            sp.dma_start(srec[:, :, :].rearrange("p g r -> p (g r)"),
                         sorted_d[:, :].rearrange("(p g) r -> p (g r)", p=P)).then_inc(S["srec_in"], 16)
            sp.wait_ge(S["pv_mm"], 2)
            sp.dma_start(w1_0s, k_major(w1_0)).then_inc(S["w1_0_in"], 16)
            sp.dma_start(w2_0s, k_major(w2_0)).then_inc(S["w2_0_in"], 16)
            sp.dma_start(wl_s, k_major(wl_t)).then_inc(S["wl_in"], 16)
            sp.dma_start(wr_s, k_major(wr_t)).then_inc(S["wr_in"], 16)
            sp.dma_start(w1_3s, k_major(w1_3t)).then_inc(S["w1_3_in"], 16)
            sp.dma_start(w2_3s, k_major(w2_3t)).then_inc(S["w2_3_in"], 16)
            sp.dma_start(w1_2s, k_major(w1_2)).then_inc(S["w1_2_in"], 16)
            sp.wait_ge(S["wo_mm"], NT)
            sp.dma_start(w2_2s, k_major(w2_2)).then_inc(S["w2_2_in"], 16)
            for t in range(NT):
                sp.wait_ge(S["out_ready"], t + 1)
                sp.dma_start(out[t * P:(t + 1) * P, :], z_sb[:, t, :]).then_inc(S["out_done"], 16)
            sp.wait_ge(S["out_done"], 16 * NT)

        @block.gpsimd
        def _(pool):
            nc.gpsimd.memset(srec[:, :, :], 0.0).then_inc(S["zeroed"], 1)
            nc.gpsimd.iota(iota_i[:, :], [[1, N]], base=0, channel_multiplier=0).then_inc(S["pool_order"], 1)
            nc.gpsimd.memset(ident[:, :], 0.0).then_inc(S["pool_order"], 1)
            nc.gpsimd.memset(ones[:, :], 1.0).then_inc(S["pool_order"], 1)
            nc.gpsimd.memset(sel[:, :, :], 0.0).then_inc(S["pool_order"], 1)
            pool.wait_ge(S["pool_order"], 4)
            nc.gpsimd.affine_select(out=ident[:, :], in_=ident[:, :], compare_op=ALU.not_equal, fill=1.0,
                                    base=0, pattern=[[-1, P]], channel_multiplier=1).then_inc(S["consts"], 1)
            nc.gpsimd.affine_select(out=before[:, :], in_=ones[:, :], compare_op=ALU.is_gt, fill=0.0,
                                    base=0, pattern=[[1, P]], channel_multiplier=-1).then_inc(S["consts"], 1)
            for part in range(2):
                nc.gpsimd.affine_select(out=sel[:, :, :], in_=sel[:, :, :], compare_op=ALU.not_equal, fill=1.0,
                                        base=-part * H, pattern=[[-1, H], [0, P]],
                                        channel_multiplier=1).then_inc(S["consts"], 1)
                pool.wait_ge(S["consts"], 3 + part)
            pool.wait_ge(S["bias_top"], 1)
            nc.gpsimd.partition_all_reduce(bmax_all[:, :], bmax[:, :], P,
                                           bass.bass_isa.ReduceOp.max).then_inc(S["bias_top_all"], 1)
            pool.wait_ge(S["cleared"], 16)
            pool.wait_ge(S["rec_ready"], 2)
            pool.wait_ge(S["weights_exp"], 1)
            pool.wait_ge(S["rows_made"], 1)
            for t in range(ET):
                nc.gpsimd.indirect_dma_start(
                    out=sorted_d[:, :], out_offset=bass.IndirectOffsetOnAxis(ap=row_i[:, t:t + 1], axis=0),
                    in_=rec[:, t, :], in_offset=None).then_inc(S["scattered"], 16)

        @block.scalar
        def _(act):
            act.dma_start(idx_src[:, :], src.rearrange("(p t) -> p t", p=P)).then_inc(S["src_in"], 16)
            act.dma_start(idx_dst[:, :], dst.rearrange("(p t) -> p t", p=P)).then_inc(S["dst_in"], 16)
            act.dma_start(att_b[:, :, :], bias.rearrange("(p t) h -> p t h", p=P)).then_inc(S["bias_in"], 16)
            act.dma_start(col[:, :], cols).then_inc(S["cols_in"], 16)
            act.dma_start(gin_c[:, :], eps.rearrange("(a b) -> a b", a=1).partition_broadcast(P)
                          ).then_inc(S["eps_in"], 16)

            def ln_std(n):
                act.wait_ge(S["ln_var"], n)
                if n == 1:
                    act.wait_ge(S["eps_column"], 1)
                nc.scalar.activation(std[:, :], mv[:, :, 1], ACT.Sqrt, bias=eps_c[:, 0:1]).then_inc(S["ln_std"], 1)

            def ln_relu(n, m, source):
                act.wait_ge(S["ln_coef"], n)
                for t in range(NT):
                    nc.scalar.activation(h_sb[:, t, :], source[:, t, :], ACT.Relu, bias=shift[:, t:t + 1],
                                         scale=rstd[:, t:t + 1]).then_inc(S["h_ready"], 1)

            def to_t(done, banks, gain=None, offset=None):
                for t in range(NT):
                    act.wait_ge(S["turned"], done + t + 1)
                    kw = {}
                    if gain:
                        kw = dict(bias=colp(offset, t), scale=colp(gain, t))
                    nc.scalar.activation(t_sb[:, t, :], bank[banks + t][:, :], ACT.Identity, **kw
                                         ).then_inc(S["t_ready"], 1)

            ln_std(1)
            ln_relu(1, 1, x_sb)
            ln_std(2)
            act.wait_ge(S["bias_low"], 1)
            nc.scalar.activation(rec[:, :, 2:REC], att_b[:, :, :], ACT.Exp).then_inc(S["weights_exp"], 1)
            act.wait_ge(S["cols_in"], 16)
            nc.scalar.mul(bq8[:, :], col[:, COLS["bq"][0]:COLS["bq"][0] + NT], DH ** -0.5
                          ).then_inc(S["scalar_order"], 1)
            to_t(0, 0, "ln1_g", "ln1_b")
            act.wait_ge(S["scalar_order"], 1)
            for t in range(NT):
                act.wait_ge(S["q_mm"], t + 1)
                nc.scalar.activation(q_t[:, t, :], bank[4 + t][:, :], ACT.Identity, bias=bq8[:, t:t + 1],
                                     scale=DH ** -0.5).then_inc(S["q_ready"], 1)
            for t in range(NT):
                act.wait_ge(S["k_mm"], t + 1)
                nc.scalar.activation(k_t[:, t, :], bank[t][:, :], ACT.Identity, bias=colp("bk", t)
                                     ).then_inc(S["k_ready"], 1)
            for t in range(NT):
                act.wait_ge(S["c1_mm"], t + 1)
                nc.scalar.copy(c1[:, t, :], bank[t][:, :]).then_inc(S["c1_ready"], 1)
            for b in range(NB):
                act.wait_ge(S["b_mm"], b + 1)
                nc.scalar.copy(big[:, :, b * BS:(b + 1) * BS],
                               bank[4 + b % 2][:, :].rearrange("p (a i) -> p a i", i=BS)).then_inc(S["b_ready"], 1)
            for n in range(NT * H):
                act.wait_ge(S["capped"], n + 1)
                nc.scalar.activation(t_sb[:, n % NT, :], t_sb[:, n % NT, :], ACT.Exp).then_inc(S["e_ready"], 1)
            to_t(NT, 0)
            ln_std(3)
            to_t(2 * NT, 0, "ln2_g", "ln2_b")
            for f in range(FT):
                act.wait_ge(S["ff1_mm"], f + 1)
                nc.scalar.activation(wide[:, f, :], bank[(4 + f) % 8][:, :], ACT.Silu, bias=colp("b1_0", f)
                                     ).then_inc(S["ff1_ready"], 1)
            ln_std(4)
            ln_relu(4, 2, x_sb)
            act.wait_ge(S["deg_mm"], 1 + NT)
            nc.scalar.activation(dinv_bc[:, :], bank[0][:, :], ACT.Sqrt, bias=1.0).then_inc(S["deg_std"], 1)
            nc.scalar.activation(dinv_c[:, :], bank[1][:, 0:NT], ACT.Sqrt, bias=1.0).then_inc(S["deg_std"], 1)
            to_t(3 * NT, 0)
            for t in range(NT):
                act.wait_ge(S["lin1_mm"], t + 1)
                nc.scalar.activation(z_sb[:, t, :], bank[t][:, :], ACT.Identity, bias=colp("b_l", t)
                                     ).then_inc(S["lin1_ready"], 1)
            act.wait_ge(S["bn_var"], 1)
            nc.scalar.activation(std[:, :], mv[:, :, 1], ACT.Sqrt, bias=eps_c[:, 0:1]).then_inc(S["bn_std"], 1)
            act.wait_ge(S["bn_coef"], 1)
            for t in range(NT):
                nc.scalar.activation(t_sb[:, t, :], z_sb[:, t, :], ACT.Relu, bias=shift[:, t:t + 1],
                                     scale=rstd[:, t:t + 1]).then_inc(S["bn_ready"], 1)
            ln_std(5)
            ln_relu(5, 3, x_sb)
            for f in range(FT):
                act.wait_ge(S["gcn1_mm"], f + 1)
                nc.scalar.activation(wide[:, f, :], bank[(4 + f) % 8][:, :], ACT.Relu, bias=colp("b1_2", f)
                                     ).then_inc(S["gcn1_ready"], 1)
            for t in range(NT):
                act.wait_ge(S["gcn2_mm"], t + 1)
                nc.scalar.activation(z_sb[:, t, :], bank[4 + t][:, :], ACT.Identity, scale=dinv_c[:, t:t + 1]
                                     ).then_inc(S["gcn2_ready"], 1)
            ln_std(6)
            ln_relu(6, 4, x_sb)
            for t in range(NT):
                act.wait_ge(S["agg3_mm"], t + 1)
                nc.scalar.copy(t_sb[:, t, :], bank[4 + t][:, :]).then_inc(S["agg3_ready"], 1)
            for t in range(NT):
                act.wait_ge(S["gin1_mm"], t + 1)
                nc.scalar.activation(wide[:, t, :], bank[t][:, :], ACT.Relu, bias=colp("b1_3", t)
                                     ).then_inc(S["gin1_ready"], 1)
            ln_std(7)

        @block.vector
        def _(dve):
            order = [0]

            def link(ins):
                order[0] += 1
                ins.then_inc(S["vector_order"], 1)
                dve.wait_ge(S["vector_order"], order[0])

            def mark(ins):
                order[0] += 1
                ins.then_inc(S["vector_order"], 1)

            def settle():
                dve.wait_ge(S["vector_order"], order[0])

            def statistics(source, done):
                for t in range(NT):
                    mark(nc.vector.bn_stats(stats[:, t, :], source[:, t, :]))
                settle()
                for t in range(NT):
                    last = nc.vector.bn_aggr(mv[:, t, :], stats[:, t, :])
                    if t < NT - 1:
                        mark(last)
                last.then_inc(S[done], 1)

            def ln_coef(n):
                dve.wait_ge(S["ln_std"], n)
                link(nc.vector.reciprocal(rstd[:, :], std[:, :]))
                nc.vector.scalar_tensor_tensor(out=shift[:, :], in0=mv[:, :, 0], scalar=-1.0, in1=rstd[:, :],
                                               op0=ALU.mult, op1=ALU.mult).then_inc(S["ln_coef"], 1)
                dve.wait_ge(S["ln_coef"], n)

            def ln_plain(source):
                for t in range(NT):
                    nc.vector.tensor_scalar(z_sb[:, t, :], source[:, t, :], rstd[:, t:t + 1], shift[:, t:t + 1],
                                            ALU.mult, ALU.add).then_inc(S["z_ready"], 1)

            nc.vector.memset(eps_c[:, :], LN_EPS).then_inc(S["eps_column"], 1)
            mark(nc.vector.memset(zero_b[:, :], 0.0))
            mark(nc.vector.memset(v_sb[:, :, :, DH:DH + 1], 1.0))
            mark(nc.vector.memset(keep, 1.0))
            dve.wait_ge(S["pool_order"], 1)
            mark(nc.vector.tensor_copy(iota_n[:, :], iota_i[:, :]))
            mark(nc.vector.tensor_copy(iota_b[:, :], iota_i[:, 0:NB]))
            settle()
            mark(nc.vector.memset(keep.rearrange("p (b t) -> p b t", b=NB)[:, :, 0:1], 0.0))
            dve.wait_ge(S["x_in"], 16)
            statistics(x_sb, "ln_var")
            ln_coef(1)
            dve.wait_ge(S["bias_in"], 16)
            nc.vector.tensor_reduce(bmax[:, :], att_b[:, :, :].rearrange("p t h -> p h t"), AX.X, ALU.max
                                    ).then_inc(S["bias_top"], 1)
            dve.wait_ge(S["src_in"], 16)
            mark(nc.vector.tensor_copy(src_f[:, :], idx_src[:, :]))
            link(nc.vector.tensor_single_scalar(src_i[:, :], idx_src[:, :], 4, ALU.logical_shift_right))
            link(nc.vector.tensor_copy(blk_f[:, :], src_i[:, :]))
            nc.vector.scalar_tensor_tensor(out=rec[:, :, 0], in0=blk_f[:, :], scalar=-float(BS), in1=src_f[:, :],
                                           op0=ALU.mult, op1=ALU.add).then_inc(S["rec_ready"], 1)
            dve.wait_ge(S["dst_in"], 16)
            link(nc.vector.tensor_copy(dst_f[:, :], idx_dst[:, :]))
            nc.vector.tensor_copy(rec[:, :, 1], dst_f[:, :]).then_inc(S["rec_ready"], 1)
            oh = onehot.rearrange("p (b t) -> p b t", b=NB)
            pf = prefix.rearrange("p (b t) -> p b t", b=NB)
            link(nc.vector.tensor_tensor(oh, blk_f[:, :].unsqueeze(1).broadcast_to([P, NB, ET]),
                                         iota_b[:, :].unsqueeze(2).broadcast_to([P, NB, ET]), ALU.is_equal))
            nc.vector.tensor_tensor_scan(prefix, keep, onehot, 0.0, ALU.mult, ALU.add).then_inc(S["edge_sums"], 1)
            dve.wait_ge(S["h_ready"], NT)
            statistics(h_sb, "ln_var")
            ln_coef(2)
            dve.wait_ge(S["cleared"], 16)
            ln_plain(h_sb)
            dve.wait_ge(S["bias_top_all"], 1)
            link(nc.vector.tensor_single_scalar(bmax_all[:, :], bmax_all[:, :], -W_SHIFT, ALU.add))
            nc.vector.tensor_tensor(att_b[:, :, :], att_b[:, :, :],
                                    bmax_all[:, :].unsqueeze(1).broadcast_to([P, ET, H]), ALU.subtract
                                    ).then_inc(S["bias_low"], 1)
            dve.wait_ge(S["edge_bases"], 2)
            link(nc.vector.tensor_single_scalar(ntile_i[:, :], bank[0][:, NB:2 * NB], float(P - 1), ALU.add))
            link(nc.vector.tensor_single_scalar(ntile_i[:, :], ntile_i[:, :], 7, ALU.logical_shift_right))
            link(nc.vector.tensor_single_scalar(ntile_f[:, :], ntile_i[:, :], 1.0, ALU.max))
            link(nc.vector.tensor_tensor_scan(tile_end[:, :], ones[:, 0:NB], ntile_f[:, :], 0.0, ALU.mult, ALU.add))
            nc.vector.tensor_copy(ntile_i[:, :], tile_end[:, :]).then_inc(S["tiles_made"], 1)
            link(nc.vector.tensor_tensor(base_f[:, :], tile_end[:, :], ntile_f[:, :], ALU.subtract))
            link(nc.vector.scalar_tensor_tensor(out=base_f[:, :], in0=base_f[:, :], scalar=float(P),
                                                in1=bank[0][:, 0:NB], op0=ALU.mult, op1=ALU.add))
            link(nc.vector.tensor_tensor(pf, pf, base_f[:, :].unsqueeze(2).broadcast_to([P, NB, ET]), ALU.add))
            link(nc.vector.tensor_tensor(prefix, prefix, onehot, ALU.mult))
            link(nc.vector.tensor_reduce(pos_f[:, :], prefix.rearrange("p (b t) -> p t b", b=NB), AX.X, ALU.add))
            link(nc.vector.tensor_single_scalar(pos_i[:, :], pos_f[:, :], -1.0, ALU.add))
            mark(nc.vector.tensor_single_scalar(pos_lo[:, :], pos_i[:, :], P - 1, ALU.bitwise_and))
            link(nc.vector.tensor_single_scalar(pos_hi[:, :], pos_i[:, :], 7, ALU.logical_shift_right))
            nc.vector.scalar_tensor_tensor(out=row_i[:, :], in0=pos_lo[:, :], scalar=float(GT), in1=pos_hi[:, :],
                                           op0=ALU.mult, op1=ALU.add).then_inc(S["rows_made"], 1)
            dve.wait_ge(S["consts"], 1)
            mark(nc.vector.tensor_copy(ident_b[:, :], ident[:, :]))

            def hots(b, slot):
                for u in range(HB):
                    for w, node in ((0, src_f), (1, dst_f)):
                        at = node[:, bass.ds(b * HB + u, 1)]
                        last = nc.vector.tensor_scalar(hot_ring[:, slot, u, w, :], iota_n[:, :], at, None,
                                                       ALU.is_equal)
                last.then_inc(S["hot_ready"], 1)

            dve.wait_ge(S["rows_in"], 16 * len(ROWS))
            for t in range(NT):
                dve.wait_ge(S["v_mm"], t + 1)
                nc.vector.tensor_tensor(v_sb[:, t, :, 0:DH], bank[4 + t][:, :].rearrange("p (h d) -> p h d", h=H),
                                        rowp("bv").rearrange("p (h d) -> p h d", h=H), ALU.add
                                        ).then_inc(S["v_ready"], 1)
            hots(0, 0)
            hots(1, 1)
            with nc.vector.Fori(1, ET // HB // 2) as i:
                for r in range(2):
                    dve.wait_ge(S["hot_used"], 2 * i + r - 1)
                    hots(2 * i + r, r)
            for t in range(NT):
                dve.wait_ge(S["c1_ready"], t + 1)
                nc.vector.tensor_scalar(no_edge[:, t, :], c1[:, t, :], 0.0, NO_EDGE, ALU.is_equal, ALU.mult
                                        ).then_inc(S["no_edge_ready"], 1)
            for h in range(H):
                for t in range(NT):
                    n = h * NT + t
                    dve.wait_ge(S["score_mm"], n + 1)
                    nc.vector.tensor_reduce(m_col[:, t, h:h + 1], bank[(4 + n) % 8][:, :], AX.X, ALU.max
                                            ).then_inc(S["score_max"], 1)
            dve.wait_ge(S["score_max"], NT * H)
            link(nc.vector.tensor_scalar(m_neg[:, :, :], m_col[:, :, :], M_FLOOR, -1.0, ALU.max, ALU.mult))
            link(nc.vector.tensor_copy(m_hl[:, :, 0:H], m_neg[:, :, :]))
            nc.vector.tensor_tensor(m_hl[:, :, H:2 * H], m_neg[:, :, :], m_hl[:, :, 0:H], ALU.subtract
                                    ).then_inc(S["shift_ready"], 1)
            dve.wait_ge(S["srec_in"], 16)
            link(nc.vector.tensor_copy(wpart[:, :, 0, :], srec[:, :, 2:REC]))
            link(nc.vector.tensor_tensor(wrest[:, :, :], srec[:, :, 2:REC], wpart[:, :, 0, :], ALU.subtract))
            link(nc.vector.tensor_copy(wpart[:, :, 1, :], wrest[:, :, :]))
            link(nc.vector.tensor_tensor(wpart[:, :, 2, :], wrest[:, :, :], wpart[:, :, 1, :], ALU.subtract))
            dve.wait_ge(S["shift_mm"], 1)
            nc.vector.tensor_copy(m_t[:, :], bank[3][0:2 * H, 0:N // 2].bitcast(BF16)).then_inc(S["shift_t"], 1)

            def weights(b, slot):
                for u in range(HB):
                    g = b * HB + u
                    nc.vector.scalar_tensor_tensor(
                        out=w_ring[:, slot, u, :, :].rearrange("p k (h i) -> p (k h) i", i=BS),
                        in0=iota_b[:, 0:BS].unsqueeze(1).broadcast_to([P, 3 * H, BS]),
                        scalar=srec[:, bass.ds(g, 1), 0],
                        in1=wpart[:, bass.ds(g, 1), :, :].rearrange("p g k h -> p (g k h)").unsqueeze(2)
                        .broadcast_to([P, 3 * H, BS]), op0=ALU.is_equal, op1=ALU.mult)
                    nc.vector.tensor_scalar(d_ring[:, slot, u, :], iota_n[:, :], srec[:, bass.ds(g, 1), 1], None,
                                            ALU.is_equal).then_inc(S["wd_ready"], 1)

            weights(0, 0)
            weights(1, 1)
            with nc.vector.Fori(1, GT // HB // 2) as i:
                for r in range(2):
                    dve.wait_ge(S["wd_used"], (2 * i + r - 1) * HB)
                    weights(2 * i + r, r)
            dve.wait_ge(S["b_ready"], NB)

            def cap(n):
                dve.wait_ge(S["st_mm"], n + 1)
                if n >= NT:
                    dve.wait_ge(S["p_ready"], n - NT + 1)
                nc.vector.tensor_single_scalar(t_sb[:, n % NT, :], bank[n % NT][:, :], EXP_CAP, ALU.min
                                               ).then_inc(S["capped"], 1)

            for n in range(2):
                cap(n)
            for h in range(H):
                for t in range(NT):
                    n = h * NT + t
                    if n + 2 < NT * H:
                        cap(n + 2)
                    dve.wait_ge(S["e_ready"], n + 1)
                    p = big[:, t * H + h, :]
                    nc.vector.tensor_tensor(p, t_sb[:, n % NT, :], p, ALU.mult).then_inc(S["p_ready"], 1)
                if h % 4 == 3:
                    c = h // 4
                    dve.wait_ge(S["pv_mm"], c + 1)
                    for t in range(NT):
                        o = bank[4 + t][:, 0:4 * (DH + 1)].rearrange("p (h d) -> p h d", h=4)
                        link(nc.vector.tensor_single_scalar(rsum[:, t, :], o[:, :, DH], TINY, ALU.max))
                        link(nc.vector.reciprocal(rsum[:, t, :], rsum[:, t, :]))
                        nc.vector.tensor_tensor(
                            z_sb[:, t, 4 * c * DH:4 * (c + 1) * DH].rearrange("p (h d) -> p h d", h=4),
                            o[:, :, 0:DH], rsum[:, t, :].unsqueeze(2).broadcast_to([P, 4, DH]), ALU.mult
                        ).then_inc(S["att_ready"], 1)
            for t in range(NT):
                link(nc.vector.tensor_tensor(h_sb[:, t, :], h_sb[:, t, :], rowp("bo"), ALU.add))
                dve.wait_ge(S["wo_mm"], t + 1)
                mark(nc.vector.tensor_tensor(h_sb[:, t, :], bank[4 + t][:, :], h_sb[:, t, :], ALU.add))
            settle()
            statistics(h_sb, "ln_var")
            ln_coef(3)
            ln_plain(h_sb)
            for t in range(NT):
                link(nc.vector.tensor_tensor(h_sb[:, t, :], h_sb[:, t, :], rowp("b2_0"), ALU.add))
                link(nc.vector.tensor_tensor(h_sb[:, t, :], h_sb[:, t, :], x_sb[:, t, :], ALU.add))
            for t in range(NT):
                dve.wait_ge(S["ff2_mm"], t + 1)
                mark(nc.vector.tensor_tensor(x_sb[:, t, :], bank[4 + t][:, :], h_sb[:, t, :], ALU.add))
            settle()
            statistics(x_sb, "ln_var")
            ln_coef(4)
            dve.wait_ge(S["deg_std"], 2)
            mark(nc.vector.reciprocal(dinv_bc[:, :], dinv_bc[:, :]))
            mark(nc.vector.reciprocal(dinv_c[:, :], dinv_c[:, :]))
            link(nc.vector.tensor_single_scalar(rcnt_bc[:, :], bank[0][:, :], 1.0, ALU.max))
            nc.vector.reciprocal(rcnt_bc[:, :], rcnt_bc[:, :]).then_inc(S["deg_ready"], 1)
            dve.wait_ge(S["eps_in"], 16)
            link(nc.vector.tensor_single_scalar(gin_c[:, :], gin_c[:, :], 1.0, ALU.add))
            for t in range(NT):
                dve.wait_ge(S["c2_mm"], t + 1)
                mark(nc.vector.tensor_copy(c1_loop[:, t, :], c1[:, t, :]))
                mark(nc.vector.tensor_copy(c2_loop[:, t, :], bank[4 + t][:, :]))
            settle()
            for t in range(NT):
                d = slice(t * P, (t + 1) * P)
                nc.vector.tensor_tensor(c1_loop[:, t, d], c1_loop[:, t, d], ident[:, :], ALU.add
                                        ).then_inc(S["c1i_ready"], 1)
                nc.vector.scalar_tensor_tensor(out=c2_loop[:, t, d], in0=ident[:, :], scalar=gin_c[:, 0:1],
                                               in1=c2_loop[:, t, d], op0=ALU.mult, op1=ALU.add
                                               ).then_inc(S["c2_ready"], 1)
            dve.wait_ge(S["deg_ready"], 1)
            for t in range(NT):
                dve.wait_ge(S["agg1_mm"], t + 1)
                nc.vector.tensor_tensor(wide[:, t, :], bank[4 + t][:, :], rcnt_bc[:, :], ALU.mult
                                        ).then_inc(S["agg1_ready"], 1)
            dve.wait_ge(S["lin1_ready"], NT)
            statistics(z_sb, "bn_var")
            dve.wait_ge(S["bn_std"], 1)
            link(nc.vector.reciprocal(rstd[:, :], std[:, :]))
            g1, b1 = COLS["gamma1"][0], COLS["beta1"][0]
            link(nc.vector.tensor_tensor(rstd[:, :], rstd[:, :], col[:, g1:g1 + NT], ALU.mult))
            link(nc.vector.scalar_tensor_tensor(out=shift[:, :], in0=mv[:, :, 0], scalar=-1.0, in1=rstd[:, :],
                                                op0=ALU.mult, op1=ALU.mult))
            nc.vector.tensor_tensor(shift[:, :], shift[:, :], col[:, b1:b1 + NT], ALU.add).then_inc(S["bn_coef"], 1)
            for t in range(NT):
                mark(nc.vector.tensor_tensor(x_sb[:, t, :], x_sb[:, t, :], h_sb[:, t, :], ALU.add))
            settle()
            for t in range(NT):
                dve.wait_ge(S["back_mm"], t + 1)
                mark(nc.vector.tensor_tensor(x_sb[:, t, :], bank[4 + t][:, :], x_sb[:, t, :], ALU.add))
            settle()
            statistics(x_sb, "ln_var")
            ln_coef(5)
            for t in range(NT):
                dve.wait_ge(S["h_ready"], 2 * NT + t + 1)
                nc.vector.tensor_scalar(z_sb[:, t, :], h_sb[:, t, :], dinv_c[:, t:t + 1], None, ALU.mult
                                        ).then_inc(S["y_ready"], 1)
            for t in range(NT):
                dve.wait_ge(S["agg2_mm"], t + 1)
                nc.vector.tensor_tensor(t_sb[:, t, :], bank[t][:, :], dinv_bc[:, :], ALU.mult
                                        ).then_inc(S["agg2_ready"], 1)
            for t in range(NT):
                dve.wait_ge(S["agg2b_mm"], t + 1)
                link(nc.vector.scalar_tensor_tensor(out=h_sb[:, t, :], in0=bank[t][:, :], scalar=dinv_c[:, t:t + 1],
                                                    in1=rowp("b2_2"), op0=ALU.mult, op1=ALU.add))
                mark(nc.vector.scalar_tensor_tensor(out=x_sb[:, t, :], in0=h_sb[:, t, :], scalar=0.0,
                                                    in1=x_sb[:, t, :], op0=ALU.max, op1=ALU.add))
            settle()
            statistics(x_sb, "ln_var")
            ln_coef(6)
            for t in range(NT):
                dve.wait_ge(S["gin2_mm"], t + 1)
                mark(nc.vector.tensor_tensor(h_sb[:, t, :], bank[4 + t][:, :], rowp("b2_3"), ALU.add))
            settle()
            statistics(h_sb, "ln_var")
            ln_coef(7)
            for t in range(NT):
                link(nc.vector.tensor_tensor(x_sb[:, t, :], x_sb[:, t, :], rowp("beta3"), ALU.add))
                link(nc.vector.tensor_scalar(z_sb[:, t, :], h_sb[:, t, :], rstd[:, t:t + 1], shift[:, t:t + 1],
                                             ALU.mult, ALU.add))
                link(nc.vector.tensor_tensor(z_sb[:, t, :], z_sb[:, t, :], rowp("gamma3"), ALU.mult))
                nc.vector.tensor_tensor(z_sb[:, t, :], z_sb[:, t, :], x_sb[:, t, :], ALU.add
                                        ).then_inc(S["out_ready"], 1)

        @block.tensor
        def _(pe):
            def tile(ap, t):
                return ap[:, t * P:(t + 1) * P]

            def turn(source, first, done):
                for c in range(NT):
                    for t in range(NT):
                        last = nc.tensor.transpose(tile(bank[first + c], t), tile(source[:, t, :], c), ident[:, :])
                    last.then_inc(S[done], 1)

            def product(banks, lhs, rhs, done, first=True, stop=True):
                for m, b in enumerate(banks):
                    for k, (a, r) in enumerate(zip(lhs, rhs)):
                        last = nc.tensor.matmul(bank[b][:, :], tile(a, m), r, start=(k == 0),
                                                stop=(k == len(lhs) - 1))
                    last.then_inc(S[done], 1)

            def ks(a, n=NT):
                return [a[:, k, :] for k in range(n)]

            lo, hi = (0, 1, 2, 3), (4, 5, 6, 7)
            pe.wait_ge(S["consts"], 4)
            pe.wait_ge(S["edge_sums"], 1)
            tot = prefix.rearrange("p (b t) -> p b t", b=NB)[:, :, ET - 1]
            nc.tensor.matmul(bank[0][:, 0:NB], before[:, :], tot, start=True, stop=True).then_inc(S["edge_bases"], 1)
            nc.tensor.matmul(bank[0][:, NB:2 * NB], ones[:, :], tot, start=True, stop=True
                             ).then_inc(S["edge_bases"], 1)
            pe.wait_ge(S["z_ready"], NT)
            pe.wait_ge(S["rows_made"], 1)
            turn(z_sb, 0, "turned")
            pe.wait_ge(S["t_ready"], NT)
            pe.wait_ge(S["wq_in"], 16)
            product(hi, ks(wslot[:, 0, :, :]), ks(t_sb), "q_mm")
            pe.wait_ge(S["wk_in"], 16)
            product(lo, ks(wslot[:, 1, :, :]), ks(t_sb), "k_mm")
            pe.wait_ge(S["wv_in"], 16)
            pe.wait_ge(S["q_ready"], NT)
            product(hi, ks(t_sb), ks(wslot[:, 2, :, :]), "v_mm")

            def count(slot, start, stop):
                for u in range(HB):
                    for t in range(NT):
                        last = nc.tensor.matmul(bank[t][:, :], tile(hot_ring[:, slot, u, 0, :], t),
                                                hot_ring[:, slot, u, 1, :], start=start and u == 0,
                                                stop=stop and u == HB - 1)
                        if stop and u == HB - 1:
                            last.then_inc(S["c1_mm"], 1)
                if not stop:
                    last.then_inc(S["hot_used"], 1)

            pe.wait_ge(S["k_ready"], NT)
            pe.wait_ge(S["hot_ready"], 1)
            count(0, True, False)
            pe.wait_ge(S["hot_ready"], 2)
            count(1, False, False)
            with nc.tensor.Fori(1, ET // HB // 2 - 1) as i:
                for r in range(2):
                    pe.wait_ge(S["hot_ready"], 2 * i + r + 1)
                    count(r, False, False)
            pe.wait_ge(S["hot_ready"], ET // HB - 1)
            count(0, False, False)
            pe.wait_ge(S["hot_ready"], ET // HB)
            count(1, False, True)

            pe.wait_ge(S["v_ready"], NT)
            for h in range(H):
                r = slice((h % 2) * DH, (h % 2 + 1) * DH)
                for t in range(NT):
                    n = h * NT + t
                    if h == 0:
                        pe.wait_ge(S["no_edge_ready"], t + 1)
                    if n >= 8:
                        pe.wait_ge(S["score_max"], n - 7)
                    b = bank[(4 + n) % 8][:, :]
                    nc.tensor.matmul(b, ident_b[:, :], no_edge[:, t, :], start=True, stop=False)
                    nc.tensor.matmul(b, q_t[r, h // 2, t * P:(t + 1) * P], k_t[r, h // 2, :], start=False,
                                     stop=True).then_inc(S["score_mm"], 1)
            pe.wait_ge(S["shift_ready"], 1)
            for t in range(NT):
                last = nc.tensor.transpose(bank[3][0:2 * H, t * P // 2:(t + 1) * P // 2].bitcast(BF16),
                                           m_hl[:, t, :], ident_b[:, :])
            last.then_inc(S["shift_mm"], 1)

            pe.wait_ge(S["tiles_made"], 1)
            w_flat = w_ring.rearrange("p r u k c -> p (r u) k c")
            d_flat = d_ring.rearrange("p r u n -> p (r u) n")
            start = 0
            for b in range(NB):
                if b < NB - 1:
                    end = pe.value_load(ntile_i[0:1, b:b + 1], min_val=b + 1, max_val=GT - NB + b + 1)
                else:
                    end = GT
                if b >= 2:
                    pe.wait_ge(S["b_ready"], b - 1)
                o = bank[4 + b % 2]
                nc.tensor.matmul(o[:, :], zero_b[:, :], iota_n[:, :], start=True, stop=False)
                with nc.tensor.Fori(start, end) as g:
                    pe.wait_ge(S["wd_ready"], g + 1)
                    slot = g % (2 * HB)
                    for j in range(NT):
                        for k in range(3):
                            last = nc.tensor.matmul(
                                tile(o, j), d_flat[:, bass.ds(slot, 1), tile_slice(j)],
                                w_flat[:, bass.ds(slot, 1), k, :], start=False, stop=False)
                    last.then_inc(S["wd_used"], 1)
                nc.tensor.matmul(o[:, :], zero_b[:, :], iota_n[:, :], start=False, stop=True
                                 ).then_inc(S["b_mm"], 1)
                start = end

            def scores_t(h):
                r = slice((h % 2) * DH, (h % 2 + 1) * DH)
                for t in range(NT):
                    n = h * NT + t
                    if n >= NT:
                        pe.wait_ge(S["capped"], n - NT + 1)
                    b = bank[t][:, :]
                    nc.tensor.matmul(b, sel[:, h, :], m_t[:, :], start=True, stop=False)
                    nc.tensor.matmul(b, k_t[r, h // 2, t * P:(t + 1) * P], q_t[r, h // 2, :], start=False,
                                     stop=True).then_inc(S["st_mm"], 1)

            def weighted(h):
                pe.wait_ge(S["p_ready"], (h + 1) * NT)
                if h == 4:
                    pe.wait_ge(S["att_ready"], NT)
                for m in range(NT):
                    o = bank[4 + m][:, (h % 4) * (DH + 1):(h % 4 + 1) * (DH + 1)]
                    for t in range(NT):
                        last = nc.tensor.matmul(o, tile(big[:, t * H + h, :], m), v_sb[:, t, h, :],
                                                start=(t == 0), stop=(t == NT - 1))
                if h % 4 == 3:
                    last.then_inc(S["pv_mm"], 1)

            pe.wait_ge(S["shift_t"], 1)
            pe.wait_ge(S["b_ready"], NB)
            scores_t(0)
            for h in range(H):
                if h + 1 < H:
                    scores_t(h + 1)
                weighted(h)
            pe.wait_ge(S["att_ready"], 2 * NT)
            turn(z_sb, 0, "turned")
            pe.wait_ge(S["t_ready"], 2 * NT)
            pe.wait_ge(S["wo_in"], 16)
            product(hi, ks(t_sb), ks(wslot[:, 3, :, :]), "wo_mm")
            pe.wait_ge(S["z_ready"], 2 * NT)
            turn(z_sb, 0, "turned")
            pe.wait_ge(S["t_ready"], 3 * NT)
            pe.wait_ge(S["w1_0_in"], 16)
            product(hi + lo, ks(w1_0s), ks(t_sb), "ff1_mm")
            pe.wait_ge(S["w2_0_in"], 16)
            pe.wait_ge(S["ff1_ready"], FT)
            product(hi, ks(wide, FT), ks(w2_0s, FT), "ff2_mm")
            nc.tensor.matmul(bank[0][:, :], ones[:, :], c1[:, 0, :], start=True, stop=False)
            for k in range(1, NT):
                last = nc.tensor.matmul(bank[0][:, :], ones[:, :], c1[:, k, :], start=False, stop=(k == NT - 1))
            last.then_inc(S["deg_mm"], 1)
            for m in range(NT):
                for k in range(NT):
                    last = nc.tensor.matmul(bank[1][:, m:m + 1], tile(c1[:, k, :], m), ones[:, 0:1],
                                            start=(k == 0), stop=(k == NT - 1))
                last.then_inc(S["deg_mm"], 1)
            pe.wait_ge(S["ln_coef"], 4)
            turn(c1, 4, "c2_mm")
            pe.wait_ge(S["h_ready"], 2 * NT)
            pe.wait_ge(S["deg_ready"], 1)
            turn(h_sb, 0, "turned")
            pe.wait_ge(S["c2_ready"], NT)
            product(hi, ks(h_sb), ks(c1), "agg1_mm")
            pe.wait_ge(S["agg1_ready"], NT)
            pe.wait_ge(S["t_ready"], 4 * NT)
            pe.wait_ge(S["wl_in"], 16)
            pe.wait_ge(S["wr_in"], 16)
            product(lo, ks(wl_s) + ks(wr_s), ks(wide) + ks(t_sb), "lin1_mm")
            pe.wait_ge(S["bn_ready"], NT)
            turn(t_sb, 4, "back_mm")
            pe.wait_ge(S["y_ready"], NT)
            pe.wait_ge(S["c1i_ready"], NT)
            product(lo, ks(z_sb), ks(c1_loop), "agg2_mm")
            pe.wait_ge(S["agg2_ready"], NT)
            pe.wait_ge(S["w1_2_in"], 16)
            product(hi + lo, ks(w1_2s), ks(t_sb), "gcn1_mm")
            pe.wait_ge(S["gcn1_ready"], FT)
            pe.wait_ge(S["w2_2_in"], 16)
            product(hi, ks(wide, FT), ks(w2_2s, FT), "gcn2_mm")
            pe.wait_ge(S["gcn2_ready"], NT)
            product(lo, ks(c1_loop), ks(z_sb), "agg2b_mm")
            pe.wait_ge(S["h_ready"], 4 * NT)
            product(hi, ks(h_sb), ks(c2_loop), "agg3_mm")
            pe.wait_ge(S["agg3_ready"], NT)
            pe.wait_ge(S["w1_3_in"], 16)
            product(lo, ks(w1_3s), ks(t_sb), "gin1_mm")
            pe.wait_ge(S["gin1_ready"], NT)
            pe.wait_ge(S["w2_3_in"], 16)
            product(hi, ks(wide), ks(w2_3s), "gin2_mm")


def tile_slice(t):
    return slice(t * P, (t + 1) * P)


def kernel(**inputs):
    import numpy as np
    import concourse.bacc as bacc
    from concourse.bass_utils import run_bass_kernel_spmd

    def as_cols(*vectors):
        return np.ascontiguousarray(np.concatenate([np.asarray(v).reshape(-1, P) for v in vectors]).T)

    g = {k: np.asarray(v) for k, v in inputs.items()}
    arrays = {
        "x": g["x"], "src": g["src"], "dst": g["dst"], "edge_bias": g["edge_attr_8"],
        "gin_eps": g["L3_gnn_eps"].reshape(1),
        "cols": as_cols(g["L0_gnn_bq"], g["L0_gnn_bk"], g["L0_gnn_ln1_g"], g["L0_gnn_ln1_b"], g["L0_gnn_ln2_g"],
                        g["L0_gnn_ln2_b"], g["L0_gnn_b1"], g["L1_gnn_b_l"], g["L1_gnn_gamma"], g["L1_gnn_beta"],
                        g["L2_gnn_b1"], g["L3_gnn_b1"]),
        "rows": np.stack([g["L0_gnn_bv"], g["L0_gnn_bo"], g["L0_gnn_b2"], g["L2_gnn_b2"], g["L3_gnn_b2"],
                          g["L3_gnn_gamma"], g["L3_gnn_beta"]]),
        "wq": g["L0_gnn_Wq"], "wk": g["L0_gnn_Wk"], "wv": g["L0_gnn_Wv"], "wo": g["L0_gnn_Wo"],
        "w1_0": g["L0_gnn_W1"], "w2_0": g["L0_gnn_W2"],
        "wl_t": g["L1_gnn_W_l"].T, "wr_t": g["L1_gnn_W_r"].T,
        "w1_2": g["L2_gnn_W1"], "w2_2": g["L2_gnn_W2"],
        "w1_3t": g["L3_gnn_W1"].T, "w2_3t": g["L3_gnn_W2"].T,
    }
    nc = bacc.Bacc("TRN2", target_bir_lowering=False, num_devices=1)
    feeds, args = {}, []
    for name, a in arrays.items():
        a = np.ascontiguousarray(a)
        feeds["in_" + name] = a
        args.append(nc.dram_tensor("in_" + name, a.shape, mybir.dt.from_np(a.dtype), kind="ExternalInput").ap())
    args.append(nc.dram_tensor("out_x", (N, D), F32, kind="ExternalOutput").ap())
    gnn_kernel(nc, *args)
    r = run_bass_kernel_spmd(nc, [feeds], core_ids=[0])
    return r.results[0]["out_x"]
```

```python
from contextlib import ExitStack

import concourse.bass as bass
from concourse import mybir

ALU = mybir.AluOpType
ACT = mybir.ActivationFunctionType
AX = mybir.AxisListType
F32 = mybir.dt.float32
BF16 = mybir.dt.bfloat16
F16 = mybir.dt.float16
I32 = mybir.dt.int32
U32 = mybir.dt.uint32

P = 128
N = 512
D = 512
F = 1024
H = 8
DH = D // H
E = 8192
NT = N // P
FT = F // P
ET = E // P
BS = 16
NB = N // BS
BT = 3
GT = NB * BT
CAP = BT * P
REC_SLOTS = GT * P
FAR = float(1 << 20)
REC = 2 + H
LN_EPS = 1e-5
NO_EDGE = -1e30
M_FLOOR = -1e25
W_SHIFT = 60.0
TINY = 1e-37

COLS = {}
for _name, _tiles in (("bq", NT), ("bk", NT), ("ln1_g", NT), ("ln1_b", NT), ("ln2_g", NT), ("ln2_b", NT),
                      ("b1_0", FT), ("b_l", NT), ("gamma1", NT), ("beta1", NT), ("b1_2", FT), ("b1_3", NT)):
    COLS[_name] = (sum(t for _, t in COLS.values()), _tiles)
N_COLS = sum(t for _, t in COLS.values())
ROWS = ("bv", "bo", "b2_0", "b2_2", "b2_3", "gamma3", "beta3")


def gnn_kernel(nc, x, src, dst, bias, eps, cols, rows, wq, wk, wv, wo, w1_0, w2_0,
               wl_t, wr_t, w1_2, w2_2, w1_3t, w2_3t, out):
    ctx = ExitStack()
    with ctx:
        def sb(name, shape, dt=F32):
            return ctx.enter_context(nc.sbuf_tensor(name, shape, dt))

        def sem(name):
            return ctx.enter_context(nc.semaphore(name))

        def k_major(w):
            return w.rearrange("(k p) n -> p k n", p=P)

        x_sb = sb("x_sb", [P, NT, D])
        h_sb = sb("h_sb", [P, NT, D])
        z_sb = sb("z_sb", [P, NT, D])
        t_sb = sb("t_sb", [P, NT, N])
        q_t = sb("q_t", [P, NT, N])
        k_t = sb("k_t", [P, NT, N])
        v_sb = sb("v_sb", [P, NT, H, DH + 1])
        c1 = sb("c1", [P, NT, N])
        wide = sb("wide", [P, FT, N])
        big = sb("big", [P, NT * H, N])
        wslot = sb("wslot", [P, 4, NT, D])
        row_bc = sb("row_bc", [P, len(ROWS), D])
        col = sb("col", [P, N_COLS])
        bq8 = sb("bq8", [P, NT])
        idx_src = sb("idx_src", [P, ET], I32)
        idx_dst = sb("idx_dst", [P, ET], I32)
        src_i = sb("src_i", [P, ET], I32)
        src_f = sb("src_f", [P, ET])
        dst_f = sb("dst_f", [P, ET])
        blk_f = sb("blk_f", [P, ET])
        bmax = sb("bmax", [P, H])
        bmax_all = sb("bmax_all", [P, H])
        wpart = sb("wpart", [P, GT, 3, H], BF16)
        iota_n = sb("iota_n", [P, N], F16)
        iota_b = sb("iota_b", [P, NB])
        ident = sb("ident", [P, P])
        ident_b = sb("ident_b", [P, P], BF16)
        before = sb("before", [P, P])
        ones = sb("ones", [P, P])
        row_i = sb("row_i", [P, ET], I32)
        rank_f = sb("rank_f", [P, ET])
        near_i = sb("near_i", [P, ET], I32)
        near_f = sb("near_f", [P, ET])
        slot_lo = sb("slot_lo", [P, ET], I32)
        slot_hi = sb("slot_hi", [P, ET], I32)
        earlier = sb("earlier", [P, NB])
        top = sb("top", [P, 1])
        rounds_f = sb("rounds_f", [P, 1])
        rounds_i = sb("rounds_i", [P, 1], I32)
        m_col = sb("m_col", [P, H, NT])
        deg = sb("deg", [P, NT])
        over = sb("over", [P, NB])
        eps_c = sb("eps_c", [P, 1])
        gin_c = sb("gin_c", [P, 1])
        stats = sb("stats", [P, NT, 6])
        mv = sb("mv", [P, NT, 2])
        std = sb("std", [P, NT])
        rstd = sb("rstd", [P, NT])
        shift = sb("shift", [P, NT])
        rsum = sb("rsum", [P, NT, 4])
        dinv_c = sb("dinv_c", [P, NT])

        flat = big[:, :, :].rearrange("p a n -> p (a n)")
        onehot = flat[:, 0:NB * ET]
        prefix = flat[:, NB * ET:2 * NB * ET]
        keep = flat[:, 2 * NB * ET:3 * NB * ET]
        spare = flat[:, 3 * NB * ET:]
        att_b = spare[:, 0:ET * H].rearrange("p (t h) -> p t h", h=H)
        iota_i = spare[:, ET * H:ET * H + N].bitcast(I32)
        late = row_bc[:, 1:, :].rearrange("p a n -> p (a n)")
        rec = late[:, 0:ET * REC].rearrange("p (t r) -> p t r", r=REC)
        empty = late[:, ET * REC:ET * REC + GT * REC // 4]
        own_hot = late[:, ET * REC + GT * REC // 4:ET * REC + GT * REC // 4 + GT * BS // 2].bitcast(BF16).rearrange(
            "p (g i) -> p g i", i=BS)
        c2 = wslot[:, 0, :, :]
        stage = wslot[:, 1, :, :].rearrange("p t n -> p (t n)")[:, 0:2 * NT * BS * (H + 1)].rearrange(
            "p (s c) -> p s c", s=2)
        wrest = z_sb[:, :, :].rearrange("p t n -> p (t n)")[:, 0:GT * H].rearrange("p (g h) -> p g h", h=H)
        wpart_f = wpart[:, :, :, :].rearrange("p g k h -> p (g k h)").bitcast(F32)
        rcnt_bc = wpart_f[:, 0:N]
        dinv_bc = wpart_f[:, N:2 * N]
        srec = z_sb[:, :, :].rearrange("p t n -> p (t n)")[:, GT * H:GT * (H + REC)].rearrange(
            "p (g r) -> p g r", r=REC)
        wide_b = wide[:, :, :].rearrange("p a n -> p (a n)").bitcast(BF16)
        w_ring = wide_b[:, 0:2 * BT * 3 * P].rearrange("p (s k c) -> p s k c", s=2 * BT, k=3)
        d_ring = wide_b[:, 2 * BT * 3 * P:2 * BT * (3 * P + N)].rearrange("p (s n) -> p s n", s=2 * BT)
        no_edge = wide_b[:, 0:NT * N].rearrange("p (t n) -> p t n", t=NT)
        peak = wide[:, 2:6, :]
        diag = wide[:, 6:8, :].rearrange("p s (t c) -> p s t c", t=NT)
        score = [t_sb, wslot[:, 1, :, :], wslot[:, 2, :, :]]
        w1_0s = big[:, 0:8, :].rearrange("p (k a) n -> p k (a n)", a=2)
        w2_0s = big[:, 8:16, :]
        wl_s, wr_s = big[:, 16:20, :], big[:, 20:24, :]
        w1_3s, w2_3s = big[:, 24:28, :], big[:, 28:32, :]
        w1_2s = wslot[:, 0:2, :, :].rearrange("p s (k a) n -> p (s k) (a n)", a=2)
        w2_2s = wslot[:, 2:4, :, :].rearrange("p s k n -> p (s k) n")
        c1_loop, c2_loop = q_t, k_t

        def colp(name, t):
            a, _ = COLS[name]
            return col[:, a + t:a + t + 1]

        def rowp(name):
            return row_bc[:, ROWS.index(name), :]

        bank = [ctx.enter_context(nc.psum_tensor(f"bank{i}", [P, 512], F32)) for i in range(8)]

        sorted_d = nc.dram_tensor("sorted_records", [GT * P, REC], F32)

        S = {name: sem(name) for name in (
            "x_in", "src_in", "dst_in", "bias_in", "cols_in", "rows_in", "eps_in",
            "wq_in", "wk_in", "wv_in", "wo_in", "w1_0_in", "w2_0_in", "wl_in", "wr_in",
            "w1_2_in", "w2_2_in", "w1_3_in", "w2_3_in", "srec_in", "cleared", "scattered", "out_done",
            "vector_order", "scalar_order", "pool_order",
            "consts", "eps_column", "bias_col", "empties", "ln_var", "ln_std", "ln_coef", "h_ready", "z_ready",
            "edge_sums", "edge_bases", "bias_top", "bias_top_all", "bias_low", "rec_ready", "weights_exp",
            "rows_made", "tiles_made",
            "turned", "t_ready", "q_mm", "q_ready", "k_mm", "k_ready", "v_mm", "v_ready",
            "c1_ready", "no_edge_ready", "bv_in", "earlier_ready", "index_steps", "split_steps", "round_built", "table_ready", "scatter_open", "b_out", "row_moved",
            "peak_steps", "peaks", "peak_mm", "diag_steps", "diag_ready", "floor_mm", "lowered", "wd_ready", "wd_used", "b_mm", "b_ready",
            "st_mm", "score_ready", "e_ready", "p_ready", "pv_mm", "att_ready", "bigfree", "wslotfree",
            "wo_mm", "x1h_ready", "ff1_mm", "ff1_ready", "ff2_mm",
            "deg_mm", "deg_std", "deg_ready", "c1i_ready", "c2_turned", "c2_ready", "h_base",
            "agg1_mm", "agg1_ready", "lin1_mm", "lin1_ready", "bn_var", "bn_std", "bn_coef", "bn_ready",
            "back_mm", "y_ready", "agg2_mm", "agg2_ready", "gcn1_mm", "gcn1_ready", "gcn2_mm", "gcn2_ready",
            "agg2b_mm", "agg3_mm", "agg3_ready", "gin1_mm", "gin1_ready", "gin2_mm", "out_ready")}
        block = ctx.enter_context(nc.Block())

        @block.sync
        def _(sp):
            sp.dma_start(x_sb[:, :, :], k_major(x)).then_inc(S["x_in"], 16)
            sp.dma_start(wslot[:, 0, :, :], k_major(wq)).then_inc(S["wq_in"], 16)
            sp.dma_start(wslot[:, 1, :, :], k_major(wk)).then_inc(S["wk_in"], 16)
            sp.dma_start(wslot[:, 2, :, :], k_major(wv)).then_inc(S["wv_in"], 16)
            sp.dma_start(row_bc[:, 0, :], rows[0:1, :].partition_broadcast(P)).then_inc(S["bv_in"], 16)
            sp.wait_ge(S["empties"], 1)

            def clear():
                sp.dma_start(sorted_d[:, :].rearrange("(p s g) r -> p s (g r)", p=P, s=4),
                             empty.unsqueeze(1).broadcast_to([P, 4, GT * REC // 4])).then_inc(S["cleared"], 16)

            clear()
            sp.wait_ge(S["cleared"], 16)
            sp.sem_inc(S["table_ready"], 1)
            sp.dma_start(wslot[:, 3, :, :], k_major(wo)).then_inc(S["wo_in"], 16)
            sp.wait_ge(S["turned"], NT)
            sp.wait_ge(S["earlier_ready"], 1)
            rounds = sp.value_load(rounds_i[0:1, 0:1], min_val=1, max_val=E // CAP + 1)
            with nc.sync.Fori(0, rounds) as r:
                sp.wait_ge(S["round_built"], r + 1)
                sp.wait_ge(S["scattered"], 16 * ET * r + 16 * ET)
                sp.dma_start(srec.rearrange("p g r -> p (g r)"),
                             sorted_d[:, :].rearrange("(p g) r -> p (g r)", p=P)).then_inc(S["srec_in"], 16)
                sp.wait_ge(S["srec_in"], 16 * r + 16)
                clear()
                sp.wait_ge(S["cleared"], 16 * r + 32)
                sp.sem_inc(S["table_ready"], 1)
            sp.wait_ge(S["round_built"], rounds + 1)
            sp.wait_ge(S["b_ready"], rounds * NB + 2)
            for n in range(1, len(ROWS)):
                sp.dma_start(row_bc[:, n, :], rows[n:n + 1, :].partition_broadcast(P)
                             ).then_inc(S["rows_in"], 16)
            sp.wait_ge(S["pv_mm"], H)
            sp.dma_start(w1_0s, k_major(w1_0)).then_inc(S["w1_0_in"], 16)
            sp.dma_start(w2_0s, k_major(w2_0)).then_inc(S["w2_0_in"], 16)
            sp.dma_start(wl_s, k_major(wl_t)).then_inc(S["wl_in"], 16)
            sp.dma_start(wr_s, k_major(wr_t)).then_inc(S["wr_in"], 16)
            sp.dma_start(w1_3s, k_major(w1_3t)).then_inc(S["w1_3_in"], 16)
            sp.dma_start(w2_3s, k_major(w2_3t)).then_inc(S["w2_3_in"], 16)
            sp.wait_ge(S["c2_ready"], NT)
            sp.dma_start(w1_2s, k_major(w1_2)).then_inc(S["w1_2_in"], 16)
            sp.wait_ge(S["wo_mm"], NT)
            sp.dma_start(w2_2s, k_major(w2_2)).then_inc(S["w2_2_in"], 16)
            for t in range(NT):
                sp.wait_ge(S["out_ready"], t + 1)
                sp.dma_start(out[t * P:(t + 1) * P, :], z_sb[:, t, :]).then_inc(S["out_done"], 16)
            sp.wait_ge(S["out_done"], 16 * NT)

        @block.gpsimd
        def _(pool):
            nc.gpsimd.memset(empty, -1.0).then_inc(S["empties"], 1)
            nc.gpsimd.iota(iota_i[:, :], [[1, N]], base=0, channel_multiplier=0).then_inc(S["pool_order"], 1)
            nc.gpsimd.memset(ident[:, :], 0.0).then_inc(S["pool_order"], 1)
            nc.gpsimd.memset(ones[:, :], 1.0).then_inc(S["pool_order"], 1)
            pool.wait_ge(S["pool_order"], 3)
            nc.gpsimd.affine_select(out=ident[:, :], in_=ident[:, :], compare_op=ALU.not_equal, fill=1.0,
                                    base=0, pattern=[[-1, P]], channel_multiplier=1).then_inc(S["consts"], 1)
            nc.gpsimd.affine_select(out=before[:, :], in_=ones[:, :], compare_op=ALU.is_gt, fill=0.0,
                                    base=0, pattern=[[1, P]], channel_multiplier=-1).then_inc(S["consts"], 1)
            pool.wait_ge(S["bias_top"], 1)
            nc.gpsimd.partition_all_reduce(bmax_all[:, :], bmax[:, :], P,
                                           bass.bass_isa.ReduceOp.max).then_inc(S["bias_top_all"], 1)
            pool.wait_ge(S["rec_ready"], 2)
            pool.wait_ge(S["weights_exp"], 1)
            pool.wait_ge(S["earlier_ready"], 1)
            rounds = pool.value_load(rounds_i[0:1, 0:1], min_val=1, max_val=E // CAP + 1)
            last_row = pool.to_reg(REC_SLOTS - 1)
            with nc.gpsimd.Fori(0, rounds) as r:
                pool.wait_ge(S["table_ready"], r + 1)
                pool.wait_ge(S["rows_made"], r + 1)
                pool.sem_inc(S["scatter_open"], 1)
                for t in range(ET):
                    nc.gpsimd.indirect_dma_start(
                        out=sorted_d[:, :], out_offset=bass.IndirectOffsetOnAxis(ap=row_i[:, t:t + 1], axis=0),
                        in_=rec[:, t, :], in_offset=None, bounds_check=last_row, oob_is_err=False
                    ).then_inc(S["scattered"], 16)
                with nc.gpsimd.Fori(0, NB // 2) as i:
                    for u in range(2):
                        pool.wait_ge(S["b_out"], r * NB + i * 2 + (u + 3))
                        part = stage[:, u, :]
                        at = bass.ds(i * (2 * BS) + u * BS, BS)
                        nc.gpsimd.tensor_tensor(c2[:, :, at], c2[:, :, at],
                                                part[:, NT * P:].rearrange("p (t i) -> p t i", i=BS), ALU.add)
                        nc.gpsimd.tensor_tensor(big[:, :, at], big[:, :, at],
                                                part[:, 0:NT * P].rearrange("p (a i) -> p a i", i=BS), ALU.add
                                                ).then_inc(S["b_ready"], 1)
            pool.wait_ge(S["b_ready"], rounds * NB + 2)
            for h in range(H):
                for t in range(NT):
                    pool.wait_ge(S["e_ready"], h * NT + t + 1)
                    p = big[:, t * H + h, :]
                    nc.gpsimd.tensor_tensor(p, score[h % 3][:, t, :], p, ALU.mult).then_inc(S["p_ready"], 1)

        @block.scalar
        def _(act):
            act.dma_start(idx_src[:, :], src.rearrange("(p t) -> p t", p=P)).then_inc(S["src_in"], 16)
            act.dma_start(idx_dst[:, :], dst.rearrange("(p t) -> p t", p=P)).then_inc(S["dst_in"], 16)
            act.dma_start(att_b[:, :, :], bias.rearrange("(p t) h -> p t h", p=P)).then_inc(S["bias_in"], 16)
            act.dma_start(col[:, :], cols).then_inc(S["cols_in"], 16)
            act.dma_start(gin_c[:, :], eps.rearrange("(a b) -> a b", a=1).partition_broadcast(P)
                          ).then_inc(S["eps_in"], 16)

            def ln_std(n):
                act.wait_ge(S["ln_var"], n)
                if n == 1:
                    act.wait_ge(S["eps_column"], 1)
                nc.scalar.activation(std[:, :], mv[:, :, 1], ACT.Sqrt, bias=eps_c[:, 0:1]).then_inc(S["ln_std"], 1)

            def ln_relu(n, m, source):
                act.wait_ge(S["ln_coef"], n)
                for t in range(NT):
                    nc.scalar.activation(h_sb[:, t, :], source[:, t, :], ACT.Relu, bias=shift[:, t:t + 1],
                                         scale=rstd[:, t:t + 1]).then_inc(S["h_ready"], 1)

            def to_t(done, banks, gain=None, offset=None):
                for t in range(NT):
                    act.wait_ge(S["turned"], done + t + 1)
                    kw = {}
                    if gain:
                        kw = dict(bias=colp(offset, t), scale=colp(gain, t))
                    nc.scalar.activation(t_sb[:, t, :], bank[banks + t][:, :], ACT.Identity, **kw
                                         ).then_inc(S["t_ready"], 1)

            act.wait_ge(S["bias_low"], 1)
            act.wait_ge(S["empties"], 1)
            nc.scalar.activation(rec[:, :, 2:REC], att_b[:, :, :], ACT.Exp).then_inc(S["weights_exp"], 1)
            ln_std(1)
            ln_relu(1, 1, x_sb)
            ln_std(2)
            act.wait_ge(S["cols_in"], 16)
            nc.scalar.mul(bq8[:, :], col[:, COLS["bq"][0]:COLS["bq"][0] + NT], DH ** -0.5
                          ).then_inc(S["scalar_order"], 1)
            to_t(0, 0, "ln1_g", "ln1_b")
            act.wait_ge(S["scalar_order"], 1)
            for t in range(NT):
                act.wait_ge(S["q_mm"], t + 1)
                nc.scalar.activation(q_t[:, t, :], bank[4 + t][:, :], ACT.Identity, bias=bq8[:, t:t + 1],
                                     scale=DH ** -0.5).then_inc(S["q_ready"], 1)
            for t in range(NT):
                act.wait_ge(S["k_mm"], t + 1)
                nc.scalar.activation(k_t[:, t, :], bank[t][:, :], ACT.Identity, bias=colp("bk", t)
                                     ).then_inc(S["k_ready"], 1)
            act.wait_ge(S["earlier_ready"], 1)
            rounds = act.value_load(rounds_i[0:1, 0:1], min_val=1, max_val=E // CAP + 1)
            act.wait_ge(S["v_mm"], NT)
            act.sem_inc(S["b_out"], 2)
            with nc.scalar.Fori(0, rounds) as r:
                with nc.scalar.Fori(0, NB // 2) as i:
                    for u in range(2):
                        act.wait_ge(S["b_mm"], r * NB + i * 2 + (u + 1))
                        act.wait_ge(S["b_ready"], r * NB + i * 2 + (u + 1))
                        nc.scalar.copy(stage[:, u, NT * P:], bank[6 + u][:, 0:NT * BS])
                        nc.scalar.copy(stage[:, u, 0:NT * P], bank[4 + u][:, :]).then_inc(S["b_out"], 1)
            for t in range(NT):
                act.wait_ge(S["c2_turned"], t + 1)
                nc.scalar.copy(c1[:, t, :], bank[4 + t][:, :]).then_inc(S["c1_ready"], 1)

            def exps(h):
                for t in range(NT):
                    act.wait_ge(S["lowered"], h * NT + t + 1)
                    nc.scalar.activation(score[h % 3][:, t, :], score[h % 3][:, t, :], ACT.Exp
                                         ).then_inc(S["e_ready"], 1)

            for h in range(H):
                for t in range(NT):
                    act.wait_ge(S["st_mm"], h * NT + t + 1)
                    if h >= 3:
                        act.wait_ge(S["p_ready"], (h - 3) * NT + t + 1)
                    if h == 0:
                        act.wait_ge(S["b_ready"], rounds * NB + 2)
                    nc.scalar.copy(score[h % 3][:, t, :], bank[t][:, :]).then_inc(S["score_ready"], 1)
                if h >= 2:
                    exps(h - 2)
            exps(H - 2)
            exps(H - 1)
            to_t(NT, 0)
            ln_std(3)
            to_t(2 * NT, 0, "ln2_g", "ln2_b")
            for f in range(FT):
                act.wait_ge(S["ff1_mm"], f + 1)
                nc.scalar.activation(wide[:, f, :], bank[(4 + f) % 8][:, :], ACT.Silu, bias=colp("b1_0", f)
                                     ).then_inc(S["ff1_ready"], 1)
            ln_std(4)
            ln_relu(4, 2, x_sb)
            act.wait_ge(S["deg_mm"], 1)
            nc.scalar.activation(dinv_bc[:, :], bank[0][:, :], ACT.Sqrt, bias=1.0).then_inc(S["deg_std"], 1)
            nc.scalar.activation(dinv_c[:, :], deg[:, :], ACT.Sqrt, bias=1.0).then_inc(S["deg_std"], 1)
            to_t(3 * NT, 0)
            for t in range(NT):
                act.wait_ge(S["lin1_mm"], t + 1)
                nc.scalar.activation(z_sb[:, t, :], bank[t][:, :], ACT.Identity, bias=colp("b_l", t)
                                     ).then_inc(S["lin1_ready"], 1)
            act.wait_ge(S["bn_var"], 1)
            nc.scalar.activation(std[:, :], mv[:, :, 1], ACT.Sqrt, bias=eps_c[:, 0:1]).then_inc(S["bn_std"], 1)
            act.wait_ge(S["bn_coef"], 1)
            for t in range(NT):
                nc.scalar.activation(t_sb[:, t, :], z_sb[:, t, :], ACT.Relu, bias=shift[:, t:t + 1],
                                     scale=rstd[:, t:t + 1]).then_inc(S["bn_ready"], 1)
            ln_std(5)
            ln_relu(5, 3, x_sb)
            for f in range(FT):
                act.wait_ge(S["gcn1_mm"], f + 1)
                nc.scalar.activation(wide[:, f, :], bank[(4 + f) % 8][:, :], ACT.Relu, bias=colp("b1_2", f)
                                     ).then_inc(S["gcn1_ready"], 1)
            for t in range(NT):
                act.wait_ge(S["gcn2_mm"], t + 1)
                nc.scalar.activation(z_sb[:, t, :], bank[4 + t][:, :], ACT.Identity, scale=dinv_c[:, t:t + 1]
                                     ).then_inc(S["gcn2_ready"], 1)
            ln_std(6)
            ln_relu(6, 4, x_sb)
            for t in range(NT):
                act.wait_ge(S["agg3_mm"], t + 1)
                nc.scalar.copy(t_sb[:, t, :], bank[4 + t][:, :]).then_inc(S["agg3_ready"], 1)
            for t in range(NT):
                act.wait_ge(S["gin1_mm"], t + 1)
                nc.scalar.activation(wide[:, t, :], bank[t][:, :], ACT.Relu, bias=colp("b1_3", t)
                                     ).then_inc(S["gin1_ready"], 1)
            ln_std(7)

        @block.vector
        def _(dve):
            order = [0]

            def link(ins):
                order[0] += 1
                ins.then_inc(S["vector_order"], 1)
                dve.wait_ge(S["vector_order"], order[0])

            def mark(ins):
                order[0] += 1
                ins.then_inc(S["vector_order"], 1)

            def settle():
                dve.wait_ge(S["vector_order"], order[0])

            def statistics(source, done):
                for t in range(NT):
                    mark(nc.vector.bn_stats(stats[:, t, :], source[:, t, :]))
                settle()
                for t in range(NT):
                    last = nc.vector.bn_aggr(mv[:, t, :], stats[:, t, :])
                    if t < NT - 1:
                        mark(last)
                last.then_inc(S[done], 1)

            def ln_coef(n):
                dve.wait_ge(S["ln_std"], n)
                link(nc.vector.reciprocal(rstd[:, :], std[:, :]))
                nc.vector.scalar_tensor_tensor(out=shift[:, :], in0=mv[:, :, 0], scalar=-1.0, in1=rstd[:, :],
                                               op0=ALU.mult, op1=ALU.mult).then_inc(S["ln_coef"], 1)
                dve.wait_ge(S["ln_coef"], n)

            def ln_plain(source):
                for t in range(NT):
                    nc.vector.tensor_scalar(z_sb[:, t, :], source[:, t, :], rstd[:, t:t + 1], shift[:, t:t + 1],
                                            ALU.mult, ALU.add).then_inc(S["z_ready"], 1)

            nc.vector.memset(eps_c[:, :], LN_EPS).then_inc(S["eps_column"], 1)
            mark(nc.vector.memset(v_sb[:, :, :, DH:DH + 1], 1.0))
            mark(nc.vector.memset(keep, 1.0))
            dve.wait_ge(S["pool_order"], 1)
            mark(nc.vector.tensor_copy(iota_n[:, :], iota_i[:, :]))
            mark(nc.vector.tensor_copy(iota_b[:, :], iota_i[:, 0:NB]))
            settle()
            mark(nc.vector.memset(keep.rearrange("p (b t) -> p b t", b=NB)[:, :, 0:1], 0.0))
            dve.wait_ge(S["src_in"], 16)
            mark(nc.vector.tensor_copy(src_f[:, :], idx_src[:, :]))
            link(nc.vector.tensor_single_scalar(src_i[:, :], idx_src[:, :], 4, ALU.logical_shift_right))
            link(nc.vector.tensor_copy(blk_f[:, :], src_i[:, :]))
            oh = onehot.rearrange("p (b t) -> p b t", b=NB)
            pf = prefix.rearrange("p (b t) -> p b t", b=NB)
            link(nc.vector.tensor_tensor(oh, blk_f[:, :].unsqueeze(1).broadcast_to([P, NB, ET]),
                                         iota_b[:, :].unsqueeze(2).broadcast_to([P, NB, ET]), ALU.is_equal))
            dve.wait_ge(S["bias_in"], 16)
            nc.vector.tensor_reduce(bmax[:, :], att_b[:, :, :].rearrange("p t h -> p h t"), AX.X, ALU.max
                                    ).then_inc(S["bias_top"], 1)
            nc.vector.tensor_tensor_scan(prefix, keep, onehot, 0.0, ALU.mult, ALU.add).then_inc(S["edge_sums"], 1)
            dve.wait_ge(S["empties"], 1)
            nc.vector.scalar_tensor_tensor(out=rec[:, :, 0], in0=blk_f[:, :], scalar=-float(BS), in1=src_f[:, :],
                                           op0=ALU.mult, op1=ALU.add).then_inc(S["rec_ready"], 1)
            dve.wait_ge(S["dst_in"], 16)
            link(nc.vector.tensor_copy(dst_f[:, :], idx_dst[:, :]))
            nc.vector.tensor_copy(rec[:, :, 1], dst_f[:, :]).then_inc(S["rec_ready"], 1)
            dve.wait_ge(S["bias_top_all"], 1)
            link(nc.vector.tensor_single_scalar(bmax_all[:, :], bmax_all[:, :], -W_SHIFT, ALU.add))
            nc.vector.tensor_tensor(att_b[:, :, :], att_b[:, :, :],
                                    bmax_all[:, :].unsqueeze(1).broadcast_to([P, ET, H]), ALU.subtract
                                    ).then_inc(S["bias_low"], 1)
            dve.wait_ge(S["edge_bases"], 2)
            mark(nc.vector.tensor_copy(earlier[:, :], bank[7][:, 0:NB]))
            link(nc.vector.tensor_reduce(top[:, :], bank[7][:, NB:2 * NB], AX.X, ALU.max))
            link(nc.vector.tensor_scalar(over[:, :], iota_b[:, :], float(CAP), top[:, 0:1], ALU.mult, ALU.is_lt))
            link(nc.vector.tensor_reduce(rounds_f[:, :], over[:, :], AX.X, ALU.add))
            nc.vector.tensor_copy(rounds_i[:, :], rounds_f[:, :]).then_inc(S["earlier_ready"], 1)
            link(nc.vector.tensor_tensor(pf, pf, earlier[:, :].unsqueeze(2).broadcast_to([P, NB, ET]), ALU.add))
            link(nc.vector.tensor_tensor(prefix, prefix, onehot, ALU.mult))
            link(nc.vector.tensor_reduce(rank_f[:, :], prefix.rearrange("p (b t) -> p t b", b=NB), AX.X, ALU.add))
            link(nc.vector.tensor_single_scalar(rank_f[:, :], rank_f[:, :], -1.0, ALU.add))

            INDEX_STEPS = 8

            def make_rows(base):
                at = [0]

                def step(ins):
                    at[0] += 1
                    ins.then_inc(S["index_steps"], 1)
                    dve.wait_ge(S["index_steps"], base + at[0])

                if type(base) is not int:
                    dve.wait_ge(S["index_steps"], base)
                step(nc.vector.tensor_scalar(near_i[:, :], rank_f[:, :], 0.0, float(CAP - 1), ALU.max, ALU.min))
                step(nc.vector.tensor_copy(near_f[:, :], near_i[:, :]))
                step(nc.vector.tensor_single_scalar(slot_lo[:, :], near_i[:, :], P - 1, ALU.bitwise_and))
                step(nc.vector.tensor_single_scalar(slot_hi[:, :], near_i[:, :], 7, ALU.logical_shift_right))
                step(nc.vector.tensor_tensor(near_f[:, :], near_f[:, :], rank_f[:, :], ALU.not_equal))
                step(nc.vector.scalar_tensor_tensor(out=near_i[:, :], in0=slot_lo[:, :], scalar=float(GT),
                                                    in1=slot_hi[:, :], op0=ALU.mult, op1=ALU.add))
                step(nc.vector.scalar_tensor_tensor(out=near_i[:, :], in0=blk_f[:, :], scalar=float(BT),
                                                    in1=near_i[:, :], op0=ALU.mult, op1=ALU.add))
                nc.vector.scalar_tensor_tensor(out=row_i[:, :], in0=near_f[:, :], scalar=FAR, in1=near_i[:, :],
                                               op0=ALU.mult, op1=ALU.add).then_inc(S["rows_made"], 1)
                nc.vector.tensor_single_scalar(rank_f[:, :], rank_f[:, :], -float(CAP), ALU.add
                                               ).then_inc(S["index_steps"], 1)

            make_rows(0)
            dve.wait_ge(S["x_in"], 16)
            statistics(x_sb, "ln_var")
            ln_coef(1)
            dve.wait_ge(S["h_ready"], NT)
            statistics(h_sb, "ln_var")
            ln_coef(2)
            ln_plain(h_sb)
            dve.wait_ge(S["consts"], 1)
            mark(nc.vector.tensor_copy(ident_b[:, :], ident[:, :]))
            dve.wait_ge(S["weights_exp"], 1)
            half = NT * H // 2
            nc.vector.memset(big[:, 0:half, :], 0.0).then_inc(S["b_ready"], 1)
            nc.vector.memset(big[:, half:, :], 0.0).then_inc(S["b_ready"], 1)
            dve.wait_ge(S["q_mm"], NT)
            mark(nc.vector.memset(c2, 0.0))
            dve.wait_ge(S["bv_in"], 16)
            for t in range(NT):
                dve.wait_ge(S["v_mm"], t + 1)
                nc.vector.tensor_tensor(v_sb[:, t, :, 0:DH], bank[4 + t][:, :].rearrange("p (h d) -> p h d", h=H),
                                        rowp("bv").rearrange("p (h d) -> p h d", h=H), ALU.add
                                        ).then_inc(S["v_ready"], 1)
            settle()
            dve.sem_inc(S["round_built"], 1)
            rounds = dve.value_load(rounds_i[0:1, 0:1], min_val=1, max_val=E // CAP + 1)
            with nc.vector.Fori(0, rounds) as r:
                dve.wait_ge(S["srec_in"], 16 * r + 16)

                def split(n, ins):
                    ins.then_inc(S["split_steps"], 1)
                    dve.wait_ge(S["split_steps"], r * 5 + n)

                split(1, nc.vector.tensor_copy(wpart[:, :, 0, :], srec[:, :, 2:REC]))
                split(2, nc.vector.tensor_tensor(wrest[:, :, :], srec[:, :, 2:REC], wpart[:, :, 0, :], ALU.subtract))
                split(3, nc.vector.tensor_copy(wpart[:, :, 1, :], wrest[:, :, :]))
                split(4, nc.vector.tensor_tensor(wpart[:, :, 2, :], wrest[:, :, :], wpart[:, :, 1, :], ALU.subtract))
                nc.vector.tensor_tensor(own_hot, iota_b[:, 0:BS].unsqueeze(1).broadcast_to([P, GT, BS]),
                                        srec[:, :, 0:1].broadcast_to([P, GT, BS]), ALU.is_equal
                                        ).then_inc(S["split_steps"], 1)
                dve.wait_ge(S["split_steps"], r * 5 + 5)
                make_rows(r * INDEX_STEPS + INDEX_STEPS)
                with nc.vector.Fori(0, NB // 2) as i:
                    for u in range(2):
                        dve.wait_ge(S["wd_used"], r * GT + i * (2 * BT) + (u + 1) * BT)
                        g = bass.ds(i * (2 * BT) + u * BT, BT)
                        nc.vector.tensor_tensor(
                            w_ring[:, u * BT:(u + 1) * BT, :, :].rearrange("p s k (h i) -> p s (k h) i", i=BS),
                            own_hot[:, g, :].unsqueeze(2).broadcast_to([P, BT, 3 * H, BS]),
                            wpart[:, g, :, :].rearrange("p g k h -> p g (k h)").unsqueeze(3)
                            .broadcast_to([P, BT, 3 * H, BS]), ALU.mult)
                        for q in range(BT):
                            nc.vector.tensor_scalar(d_ring[:, u * BT + q, :], iota_n[:, :],
                                                    srec[:, bass.ds(i * (2 * BT) + (u * BT + q), 1), 1], None,
                                                    ALU.is_equal).then_inc(S["wd_ready"], 1)
                dve.wait_ge(S["wd_ready"], r * GT + GT)
                dve.sem_inc(S["round_built"], 1)
            dve.wait_ge(S["b_ready"], rounds * NB + 2)
            for t in range(NT):
                nc.vector.tensor_scalar(no_edge[:, t, :], c2[:, t, :], 0.0, NO_EDGE, ALU.is_equal, ALU.mult
                                        ).then_inc(S["no_edge_ready"], 1)
            nc.vector.tensor_reduce(deg[:, :], c2, AX.X, ALU.add).then_inc(S["deg_ready"], 1)

            def peaks(h):
                s, k = score[h % 3], peak[:, 2 * (h % 2):2 * (h % 2) + 2, :]
                dve.wait_ge(S["score_ready"], h * NT + 2)
                if h >= 2:
                    dve.wait_ge(S["peak_mm"], h - 1)
                nc.vector.tensor_tensor(k[:, 0, :], s[:, 0, :], s[:, 1, :], ALU.max).then_inc(S["peak_steps"], 1)
                dve.wait_ge(S["score_ready"], h * NT + 4)
                nc.vector.tensor_tensor(k[:, 1, :], s[:, 2, :], s[:, 3, :], ALU.max).then_inc(S["peak_steps"], 1)
                dve.wait_ge(S["peak_steps"], 2 * h + 2)
                nc.vector.tensor_tensor(k[:, 0, :], k[:, 0, :], k[:, 1, :], ALU.max).then_inc(S["peaks"], 1)

            def diags(h):
                dve.wait_ge(S["peak_mm"], h + 1)
                m = m_col[:, h, :]
                nc.vector.tensor_reduce(m, bank[4][:, :].rearrange("p (t j) -> p t j", t=NT), AX.X, ALU.max
                                        ).then_inc(S["diag_steps"], 1)
                dve.wait_ge(S["diag_steps"], 2 * h + 1)
                nc.vector.tensor_single_scalar(m, m, M_FLOOR, ALU.max).then_inc(S["diag_steps"], 1)
                dve.wait_ge(S["diag_steps"], 2 * h + 2)
                if h >= 2:
                    dve.wait_ge(S["floor_mm"], h - 1)
                nc.vector.tensor_tensor(diag[:, h % 2, :, :], ident[:, :].unsqueeze(1).broadcast_to([P, NT, P]),
                                        m.unsqueeze(2).broadcast_to([P, NT, P]), ALU.mult
                                        ).then_inc(S["diag_ready"], 1)

            def lower(h):
                dve.wait_ge(S["floor_mm"], h + 1)
                for t in range(NT):
                    s = score[h % 3][:, t, :]
                    nc.vector.tensor_tensor(s, s, bank[5][:, :], ALU.subtract).then_inc(S["lowered"], 1)

            def normalise(h):
                dve.wait_ge(S["pv_mm"], h + 1)
                o = bank[6 + h % 2][:, 0:NT * (DH + 1)].rearrange("p (t d) -> p t d", t=NT)
                link(nc.vector.tensor_single_scalar(rsum[:, h % 2, :], o[:, :, DH], TINY, ALU.max))
                link(nc.vector.reciprocal(rsum[:, h % 2, :], rsum[:, h % 2, :]))
                nc.vector.tensor_tensor(z_sb[:, :, h * DH:(h + 1) * DH], o[:, :, 0:DH],
                                        rsum[:, h % 2, :].unsqueeze(2).broadcast_to([P, NT, DH]), ALU.mult
                                        ).then_inc(S["att_ready"], 1)

            for n in range(H + 3):
                if n >= 2 and n - 2 < H:
                    lower(n - 2)
                if n >= 1 and n - 1 < H:
                    diags(n - 1)
                if n < H:
                    peaks(n)
                if n >= 3:
                    normalise(n - 3)
            dve.wait_ge(S["rows_in"], 16 * (len(ROWS) - 1))
            for t in range(NT):
                link(nc.vector.tensor_tensor(h_sb[:, t, :], h_sb[:, t, :], rowp("bo"), ALU.add))
                dve.wait_ge(S["wo_mm"], t + 1)
                mark(nc.vector.tensor_tensor(h_sb[:, t, :], bank[4 + t][:, :], h_sb[:, t, :], ALU.add))
            settle()
            statistics(h_sb, "ln_var")
            ln_coef(3)
            ln_plain(h_sb)
            for t in range(NT):
                link(nc.vector.tensor_tensor(h_sb[:, t, :], h_sb[:, t, :], rowp("b2_0"), ALU.add))
                link(nc.vector.tensor_tensor(h_sb[:, t, :], h_sb[:, t, :], x_sb[:, t, :], ALU.add))
            for t in range(NT):
                dve.wait_ge(S["ff2_mm"], t + 1)
                mark(nc.vector.tensor_tensor(x_sb[:, t, :], bank[4 + t][:, :], h_sb[:, t, :], ALU.add))
            settle()
            statistics(x_sb, "ln_var")
            ln_coef(4)
            dve.wait_ge(S["deg_std"], 2)
            mark(nc.vector.reciprocal(dinv_bc[:, :], dinv_bc[:, :]))
            mark(nc.vector.reciprocal(dinv_c[:, :], dinv_c[:, :]))
            link(nc.vector.tensor_single_scalar(rcnt_bc[:, :], bank[0][:, :], 1.0, ALU.max))
            nc.vector.reciprocal(rcnt_bc[:, :], rcnt_bc[:, :]).then_inc(S["deg_ready"], 1)
            dve.wait_ge(S["eps_in"], 16)
            link(nc.vector.tensor_single_scalar(gin_c[:, :], gin_c[:, :], 1.0, ALU.add))
            for t in range(NT):
                mark(nc.vector.tensor_copy(c1_loop[:, t, :], c1[:, t, :]))
                mark(nc.vector.tensor_copy(c2_loop[:, t, :], c2[:, t, :]))
            settle()
            for t in range(NT):
                d = slice(t * P, (t + 1) * P)
                nc.vector.tensor_tensor(c1_loop[:, t, d], c1_loop[:, t, d], ident[:, :], ALU.add
                                        ).then_inc(S["c1i_ready"], 1)
                nc.vector.scalar_tensor_tensor(out=c2_loop[:, t, d], in0=ident[:, :], scalar=gin_c[:, 0:1],
                                               in1=c2_loop[:, t, d], op0=ALU.mult, op1=ALU.add
                                               ).then_inc(S["c2_ready"], 1)
            dve.wait_ge(S["deg_ready"], 2)
            for t in range(NT):
                dve.wait_ge(S["agg1_mm"], t + 1)
                nc.vector.tensor_tensor(wide[:, t, :], bank[4 + t][:, :], rcnt_bc[:, :], ALU.mult
                                        ).then_inc(S["agg1_ready"], 1)
            dve.wait_ge(S["lin1_ready"], NT)
            statistics(z_sb, "bn_var")
            dve.wait_ge(S["bn_std"], 1)
            link(nc.vector.reciprocal(rstd[:, :], std[:, :]))
            g1, b1 = COLS["gamma1"][0], COLS["beta1"][0]
            link(nc.vector.tensor_tensor(rstd[:, :], rstd[:, :], col[:, g1:g1 + NT], ALU.mult))
            link(nc.vector.scalar_tensor_tensor(out=shift[:, :], in0=mv[:, :, 0], scalar=-1.0, in1=rstd[:, :],
                                                op0=ALU.mult, op1=ALU.mult))
            nc.vector.tensor_tensor(shift[:, :], shift[:, :], col[:, b1:b1 + NT], ALU.add).then_inc(S["bn_coef"], 1)
            for t in range(NT):
                mark(nc.vector.tensor_tensor(x_sb[:, t, :], x_sb[:, t, :], h_sb[:, t, :], ALU.add))
            settle()
            for t in range(NT):
                dve.wait_ge(S["back_mm"], t + 1)
                mark(nc.vector.tensor_tensor(x_sb[:, t, :], bank[4 + t][:, :], x_sb[:, t, :], ALU.add))
            settle()
            statistics(x_sb, "ln_var")
            ln_coef(5)
            for t in range(NT):
                dve.wait_ge(S["h_ready"], 2 * NT + t + 1)
                nc.vector.tensor_scalar(z_sb[:, t, :], h_sb[:, t, :], dinv_c[:, t:t + 1], None, ALU.mult
                                        ).then_inc(S["y_ready"], 1)
            for t in range(NT):
                dve.wait_ge(S["agg2_mm"], t + 1)
                nc.vector.tensor_tensor(t_sb[:, t, :], bank[t][:, :], dinv_bc[:, :], ALU.mult
                                        ).then_inc(S["agg2_ready"], 1)
            for t in range(NT):
                dve.wait_ge(S["agg2b_mm"], t + 1)
                link(nc.vector.scalar_tensor_tensor(out=h_sb[:, t, :], in0=bank[t][:, :], scalar=dinv_c[:, t:t + 1],
                                                    in1=rowp("b2_2"), op0=ALU.mult, op1=ALU.add))
                mark(nc.vector.scalar_tensor_tensor(out=x_sb[:, t, :], in0=h_sb[:, t, :], scalar=0.0,
                                                    in1=x_sb[:, t, :], op0=ALU.max, op1=ALU.add))
            settle()
            statistics(x_sb, "ln_var")
            ln_coef(6)
            for t in range(NT):
                dve.wait_ge(S["gin2_mm"], t + 1)
                mark(nc.vector.tensor_tensor(h_sb[:, t, :], bank[4 + t][:, :], rowp("b2_3"), ALU.add))
            settle()
            statistics(h_sb, "ln_var")
            ln_coef(7)
            for t in range(NT):
                link(nc.vector.tensor_tensor(x_sb[:, t, :], x_sb[:, t, :], rowp("beta3"), ALU.add))
                link(nc.vector.tensor_scalar(z_sb[:, t, :], h_sb[:, t, :], rstd[:, t:t + 1], shift[:, t:t + 1],
                                             ALU.mult, ALU.add))
                link(nc.vector.tensor_tensor(z_sb[:, t, :], z_sb[:, t, :], rowp("gamma3"), ALU.mult))
                nc.vector.tensor_tensor(z_sb[:, t, :], z_sb[:, t, :], x_sb[:, t, :], ALU.add
                                        ).then_inc(S["out_ready"], 1)

        @block.tensor
        def _(pe):
            def tile(ap, t):
                return ap[:, t * P:(t + 1) * P]

            def turn(source, first, done):
                for c in range(NT):
                    for t in range(NT):
                        last = nc.tensor.transpose(tile(bank[first + c], t), tile(source[:, t, :], c), ident[:, :])
                    last.then_inc(S[done], 1)

            def product(banks, lhs, rhs, done, first=True, stop=True):
                for m, b in enumerate(banks):
                    for k, (a, r) in enumerate(zip(lhs, rhs)):
                        last = nc.tensor.matmul(bank[b][:, :], tile(a, m), r, start=(k == 0),
                                                stop=(k == len(lhs) - 1))
                    last.then_inc(S[done], 1)

            def ks(a, n=NT):
                return [a[:, k, :] for k in range(n)]

            lo, hi = (0, 1, 2, 3), (4, 5, 6, 7)
            pe.wait_ge(S["consts"], 2)
            pe.wait_ge(S["edge_sums"], 1)
            tot = prefix.rearrange("p (b t) -> p b t", b=NB)[:, :, ET - 1]
            nc.tensor.matmul(bank[7][:, 0:NB], before[:, :], tot, start=True, stop=True).then_inc(S["edge_bases"], 1)
            nc.tensor.matmul(bank[7][:, NB:2 * NB], ones[:, :], tot, start=True, stop=True
                             ).then_inc(S["edge_bases"], 1)
            pe.wait_ge(S["z_ready"], NT)
            turn(z_sb, 0, "turned")
            pe.wait_ge(S["t_ready"], NT)
            pe.wait_ge(S["wq_in"], 16)
            pe.wait_ge(S["earlier_ready"], 1)
            product(hi, ks(wslot[:, 0, :, :]), ks(t_sb), "q_mm")
            pe.wait_ge(S["wk_in"], 16)
            product(lo, ks(wslot[:, 1, :, :]), ks(t_sb), "k_mm")
            pe.wait_ge(S["wv_in"], 16)
            pe.wait_ge(S["q_ready"], NT)
            product(hi, ks(t_sb), ks(wslot[:, 2, :, :]), "v_mm")

            pe.wait_ge(S["v_ready"], NT)
            pe.sem_inc(S["wd_used"], 2 * BT)
            rounds = pe.value_load(rounds_i[0:1, 0:1], min_val=1, max_val=E // CAP + 1)
            with nc.tensor.Fori(0, rounds) as r:
                with nc.tensor.Fori(0, NB // 2) as i:
                    for u in range(2):
                        pe.wait_ge(S["b_out"], r * NB + i * 2 + (u + 1))
                        for q in range(BT):
                            slot = u * BT + q
                            pe.wait_ge(S["wd_ready"], r * GT + i * (2 * BT) + (slot + 1))
                            for j in range(NT):
                                to = tile(d_ring[:, slot, :], j)
                                for k in range(3):
                                    nc.tensor.matmul(tile(bank[4 + u], j), to, w_ring[:, slot, k, :],
                                                     start=(q == j == k == 0),
                                                     stop=(q == BT - 1 and j == NT - 1 and k == 2))
                                last = nc.tensor.matmul(bank[6 + u][:, j * BS:(j + 1) * BS], to, own_hot[:, bass.ds(i * (2 * BT) + slot, 1), :],
                                                        start=(q == j == 0), stop=False)
                            last.then_inc(S["wd_used"], 1)
                        nc.tensor.matmul(bank[6 + u][:, NT * BS:NT * BS + BS], ident_b[:, :], ident_b[:, 0:BS],
                                         start=False, stop=True).then_inc(S["b_mm"], 1)

            pe.wait_ge(S["b_ready"], rounds * NB + 2)
            turn(c2, 4, "c2_turned")

            def scores(h):
                r = slice((h % 2) * DH, (h % 2 + 1) * DH)
                for t in range(NT):
                    if h == 0:
                        pe.wait_ge(S["no_edge_ready"], t + 1)
                    else:
                        pe.wait_ge(S["score_ready"], (h - 1) * NT + t + 1)
                    b = bank[t][:, :]
                    nc.tensor.matmul(b, ident_b[:, :], no_edge[:, t, :], start=True, stop=False)
                    nc.tensor.matmul(b, k_t[r, h // 2, t * P:(t + 1) * P], q_t[r, h // 2, :], start=False,
                                     stop=True).then_inc(S["st_mm"], 1)

            def peaks_turned(h):
                pe.wait_ge(S["peaks"], h + 1)
                if h >= 1:
                    pe.wait_ge(S["diag_ready"], h)
                for t in range(NT):
                    last = nc.tensor.transpose(tile(bank[4], t), tile(peak[:, 2 * (h % 2), :], t), ident[:, :])
                last.then_inc(S["peak_mm"], 1)

            def floor_row(h):
                pe.wait_ge(S["diag_ready"], h + 1)
                if h >= 1:
                    pe.wait_ge(S["lowered"], h * NT)
                nc.tensor.matmul(bank[5][:, :], ones[:, :], diag[:, h % 2, :, :].rearrange("p t c -> p (t c)"),
                                 start=True, stop=True).then_inc(S["floor_mm"], 1)

            def weighted(h):
                pe.wait_ge(S["p_ready"], (h + 1) * NT)
                if h >= 2:
                    pe.wait_ge(S["att_ready"], h - 1)
                for m in range(NT):
                    o = bank[6 + h % 2][:, m * (DH + 1):(m + 1) * (DH + 1)]
                    for t in range(NT):
                        last = nc.tensor.matmul(o, tile(big[:, t * H + h, :], m), v_sb[:, t, h, :],
                                                start=(t == 0), stop=(t == NT - 1))
                last.then_inc(S["pv_mm"], 1)

            pe.wait_ge(S["c1_ready"], NT)
            for n in range(H + 3):
                if n < H:
                    scores(n)
                if n >= 1 and n - 1 < H:
                    peaks_turned(n - 1)
                if n >= 3:
                    weighted(n - 3)
                if n >= 1 and n - 1 < H:
                    floor_row(n - 1)
            pe.wait_ge(S["att_ready"], H)
            turn(z_sb, 0, "turned")
            pe.wait_ge(S["t_ready"], 2 * NT)
            pe.wait_ge(S["wo_in"], 16)
            product(hi, ks(t_sb), ks(wslot[:, 3, :, :]), "wo_mm")
            pe.wait_ge(S["z_ready"], 2 * NT)
            turn(z_sb, 0, "turned")
            pe.wait_ge(S["t_ready"], 3 * NT)
            pe.wait_ge(S["w1_0_in"], 16)
            product(hi + lo, ks(w1_0s), ks(t_sb), "ff1_mm")
            pe.wait_ge(S["w2_0_in"], 16)
            pe.wait_ge(S["ff1_ready"], FT)
            product(hi, ks(wide, FT), ks(w2_0s, FT), "ff2_mm")
            nc.tensor.matmul(bank[0][:, :], ones[:, :], c1[:, 0, :], start=True, stop=False)
            for k in range(1, NT):
                last = nc.tensor.matmul(bank[0][:, :], ones[:, :], c1[:, k, :], start=False, stop=(k == NT - 1))
            last.then_inc(S["deg_mm"], 1)
            pe.wait_ge(S["h_ready"], 2 * NT)
            pe.wait_ge(S["deg_ready"], 2)
            turn(h_sb, 0, "turned")
            pe.wait_ge(S["ln_coef"], 4)
            product(hi, ks(h_sb), ks(c1), "agg1_mm")
            pe.wait_ge(S["agg1_ready"], NT)
            pe.wait_ge(S["t_ready"], 4 * NT)
            pe.wait_ge(S["wl_in"], 16)
            pe.wait_ge(S["wr_in"], 16)
            product(lo, ks(wl_s) + ks(wr_s), ks(wide) + ks(t_sb), "lin1_mm")
            pe.wait_ge(S["bn_ready"], NT)
            turn(t_sb, 4, "back_mm")
            pe.wait_ge(S["y_ready"], NT)
            pe.wait_ge(S["c1i_ready"], NT)
            product(lo, ks(z_sb), ks(c1_loop), "agg2_mm")
            pe.wait_ge(S["agg2_ready"], NT)
            pe.wait_ge(S["w1_2_in"], 16)
            product(hi + lo, ks(w1_2s), ks(t_sb), "gcn1_mm")
            pe.wait_ge(S["gcn1_ready"], FT)
            pe.wait_ge(S["w2_2_in"], 16)
            product(hi, ks(wide, FT), ks(w2_2s, FT), "gcn2_mm")
            pe.wait_ge(S["gcn2_ready"], NT)
            product(lo, ks(c1_loop), ks(z_sb), "agg2b_mm")
            pe.wait_ge(S["h_ready"], 4 * NT)
            product(hi, ks(h_sb), ks(c2_loop), "agg3_mm")
            pe.wait_ge(S["agg3_ready"], NT)
            pe.wait_ge(S["w1_3_in"], 16)
            product(lo, ks(w1_3s), ks(t_sb), "gin1_mm")
            pe.wait_ge(S["gin1_ready"], NT)
            pe.wait_ge(S["w2_3_in"], 16)
            product(hi, ks(wide), ks(w2_3s), "gin2_mm")


def kernel(**inputs):
    import numpy as np
    import concourse.bacc as bacc
    from concourse.bass_utils import run_bass_kernel_spmd

    def as_cols(*vectors):
        return np.ascontiguousarray(np.concatenate([np.asarray(v).reshape(-1, P) for v in vectors]).T)

    g = {k: np.asarray(v) for k, v in inputs.items()}
    arrays = {
        "x": g["x"], "src": g["src"], "dst": g["dst"], "edge_bias": g["edge_attr_8"],
        "gin_eps": g["L3_gnn_eps"].reshape(1),
        "cols": as_cols(g["L0_gnn_bq"], g["L0_gnn_bk"], g["L0_gnn_ln1_g"], g["L0_gnn_ln1_b"], g["L0_gnn_ln2_g"],
                        g["L0_gnn_ln2_b"], g["L0_gnn_b1"], g["L1_gnn_b_l"], g["L1_gnn_gamma"], g["L1_gnn_beta"],
                        g["L2_gnn_b1"], g["L3_gnn_b1"]),
        "rows": np.stack([g["L0_gnn_bv"], g["L0_gnn_bo"], g["L0_gnn_b2"], g["L2_gnn_b2"], g["L3_gnn_b2"],
                          g["L3_gnn_gamma"], g["L3_gnn_beta"]]),
        "wq": g["L0_gnn_Wq"], "wk": g["L0_gnn_Wk"], "wv": g["L0_gnn_Wv"], "wo": g["L0_gnn_Wo"],
        "w1_0": g["L0_gnn_W1"], "w2_0": g["L0_gnn_W2"],
        "wl_t": g["L1_gnn_W_l"].T, "wr_t": g["L1_gnn_W_r"].T,
        "w1_2": g["L2_gnn_W1"], "w2_2": g["L2_gnn_W2"],
        "w1_3t": g["L3_gnn_W1"].T, "w2_3t": g["L3_gnn_W2"].T,
    }
    nc = bacc.Bacc("TRN2", target_bir_lowering=False, num_devices=1)
    feeds, args = {}, []
    for name, a in arrays.items():
        a = np.ascontiguousarray(a)
        feeds["in_" + name] = a
        args.append(nc.dram_tensor("in_" + name, a.shape, mybir.dt.from_np(a.dtype), kind="ExternalInput").ap())
    args.append(nc.dram_tensor("out_x", (N, D), F32, kind="ExternalOutput").ap())
    gnn_kernel(nc, *args)
    r = run_bass_kernel_spmd(nc, [feeds], core_ids=[0])
    return r.results[0]["out_x"]
```

```python
from collections import namedtuple
from contextlib import ExitStack

import concourse.bass as bass
from concourse import mybir

ALU = mybir.AluOpType
ACT = mybir.ActivationFunctionType
AX = mybir.AxisListType
F32 = mybir.dt.float32
F32R = mybir.dt.float32r
BF16 = mybir.dt.bfloat16
F16 = mybir.dt.float16
I32 = mybir.dt.int32

P = 128
N = 512
D = 512
F = 1024
H = 8
DH = D // H
E = 8192
NT = N // P
FT = F // P
ET = E // P
BS = 16
NB = N // BS
BT = 3
GT = NB * BT
FIRST = 4 * BT
CAP = BT * P
REC_SLOTS = GT * P
FAR = float(1 << 20)
WC = 1 + 3 * H
SC = (1 + H) * BS
REC = 2 + H
EARLY = ET // 4
LN_EPS = 1e-5
NO_EDGE = -1e30
M_FLOOR = -1e25
W_SHIFT = 60.0
TINY = 1e-37

COLS = {}
for _name, _tiles in (("bq", NT), ("bk", NT), ("ln1_g", NT), ("ln1_b", NT), ("ln2_g", NT), ("ln2_b", NT),
                      ("b1_0", FT), ("b_l", NT), ("gamma1", NT), ("beta1", NT), ("b1_2", FT), ("b1_3", NT)):
    COLS[_name] = (sum(t for _, t in COLS.values()), _tiles)
N_COLS = sum(t for _, t in COLS.values())
ROWS = ("bv", "bo", "b2_0", "b2_2", "b2_3", "gamma3", "beta3")

Place = namedtuple("Place", ("full", "rounded"))


def gnn_kernel(nc, x, src, dst, bias, eps, cols, rows, wq, wk, wv, wo, w1_0, w2_0,
               wl_t, wr_t, w1_2, w2_2, w1_3t, w2_3t, out):
    ctx = ExitStack()
    with ctx:
        def sb(name, shape, dt=F32):
            return ctx.enter_context(nc.sbuf_tensor(name, shape, dt))

        def sb_rounded(name, shape):
            at = nc.sbuf_base
            assert at % 32 == 0
            return sb(name, shape), nc.alloc_sbuf_tensor_at(name + "_rounded", shape, F32R, offset=at)

        def sem(name):
            return ctx.enter_context(nc.semaphore(name))

        def k_major(w):
            return w.rearrange("(k p) n -> p k n", p=P)

        x_sb = sb("x_sb", [P, NT, D])
        h_sb, h_sb_r = sb_rounded("h_sb", [P, NT, D])
        z_sb, z_sb_r = sb_rounded("z_sb", [P, NT, D])
        t_sb, t_sb_r = sb_rounded("t_sb", [P, NT, N])
        q_t, q_t_r = sb_rounded("q_t", [P, NT, N])
        k_t, k_t_r = sb_rounded("k_t", [P, NT, N])
        v_sb, v_sb_r = sb_rounded("v_sb", [P, NT, H, DH + 1])
        c1 = sb("c1", [P, NT, N])
        wide, wide_r = sb_rounded("wide", [P, FT, N])
        big, big_r = sb_rounded("big", [P, NT * H, N])
        wslot, wslot_r = sb_rounded("wslot", [P, 4, NT, D])
        row_bc = sb("row_bc", [P, len(ROWS), D])
        col = sb("col", [P, N_COLS])
        bq8 = sb("bq8", [P, NT])
        idx_src = sb("idx_src", [P, ET], I32)
        idx_dst = sb("idx_dst", [P, ET], I32)
        src_i = sb("src_i", [P, ET], I32)
        src_f = sb("src_f", [P, ET])
        dst_f = sb("dst_f", [P, ET])
        blk_f = sb("blk_f", [P, ET])
        bmax = sb("bmax", [P, H])
        bmax_all = sb("bmax_all", [P, H])
        wpart_all = sb("wpart", [P, GT * WC], BF16)
        iota_n = sb("iota_n", [P, N], F16)
        iota_b = sb("iota_b", [P, NB])
        ident = sb("ident", [P, P])
        ident_b = sb("ident_b", [P, P], BF16)
        before = sb("before", [P, P])
        loop_i = sb("loop_i", [P, P])
        ones = sb("ones", [P, P])
        row_i = sb("row_i", [P, ET], I32)
        rank_f = sb("rank_f", [P, ET])
        near_i_all = sb("near_i", [P, ET], I32)
        near_f_all = sb("near_f", [P, ET])
        slot_lo = sb("slot_lo", [P, ET], I32)
        slot_hi = sb("slot_hi", [P, ET], I32)
        earlier = sb("earlier", [P, NB])
        top = sb("top", [P, 1])
        rounds_f = sb("rounds_f", [P, 1])
        rounds_i = sb("rounds_i", [P, 1], I32)
        m_col = sb("m_col", [P, H, NT])
        deg = sb("deg", [P, NT])
        over = sb("over", [P, NB])
        eps_c = sb("eps_c", [P, 1])
        gin_c = sb("gin_c", [P, 1])
        stats = sb("stats", [P, NT, 6])
        mv = sb("mv", [P, NT, 2])
        std = sb("std", [P, NT])
        rstd = sb("rstd", [P, NT])
        shift = sb("shift", [P, NT])
        rsum = sb("rsum", [P, NT, 4])
        dinv_c = sb("dinv_c", [P, NT])

        flat = big[:, :, :].rearrange("p a n -> p (a n)")
        onehot = flat[:, 0:NB * ET]
        prefix = flat[:, NB * ET:2 * NB * ET]
        keep = flat[:, 2 * NB * ET:3 * NB * ET]
        spare = flat[:, 3 * NB * ET:]
        att_b = spare[:, 0:ET * H].rearrange("p (t h) -> p t h", h=H)
        iota_i = spare[:, ET * H:ET * H + N].bitcast(I32)
        late = row_bc[:, 1:, :].rearrange("p a n -> p (a n)")
        rec = late[:, 0:ET * REC].rearrange("p (t r) -> p t r", r=REC)
        empty = late[:, ET * REC:ET * REC + GT * REC // 4]
        own_hot = late[:, ET * REC + GT * REC // 4:ET * REC + GT * REC // 4 + GT * BS // 2].bitcast(BF16).rearrange(
            "p (g i) -> p g i", i=BS)
        c2 = wslot[:, 0, :, :]
        stage = wslot[:, 1, :, :].rearrange("p t n -> p (t n)")[:, 0:2 * NT * SC].rearrange(
            "p (s c) -> p s c", s=2)
        wrest = z_sb[:, :, :].rearrange("p t n -> p (t n)")[:, 0:GT * H].rearrange("p (g h) -> p g h", h=H)
        wpart = wpart_all[:, :].rearrange("p (g k) -> p g k", k=WC)
        wpart_f = wpart_all[:, :].bitcast(F32)
        rcnt_bc = wpart_f[:, 0:N]
        dinv_bc = wpart_f[:, N:2 * N]
        b_sums = big[:, :, :].rearrange("p (t h) n -> p t h n", h=H)
        srec = z_sb[:, :, :].rearrange("p t n -> p (t n)")[:, GT * H:GT * (H + REC)].rearrange(
            "p (g r) -> p g r", r=REC)
        wide_b = wide[:, :, :].rearrange("p a n -> p (a n)").bitcast(BF16)
        w_ring = wide_b[:, 0:2 * BT * WC * BS].rearrange("p (s c) -> p s c", s=2 * BT)
        d_ring = wide_b[:, 2 * BT * WC * BS:2 * BT * (WC * BS + N)].rearrange("p (s n) -> p s n", s=2 * BT)
        no_edge = wide_b[:, 0:NT * N].rearrange("p (t n) -> p t n", t=NT)
        peak = wide[:, 2:6, :]
        diag = wide[:, 6:8, :].rearrange("p s (t c) -> p s t c", t=NT)
        score = [t_sb, wslot[:, 1, :, :], wslot[:, 2, :, :]]
        bn_t = wide[:, NT:, :]
        def both(view, full, rounded):
            return Place(view(full), view(rounded))

        h_at = both(lambda a: a[:, :, :], h_sb, h_sb_r)
        z_at = both(lambda a: a[:, :, :], z_sb, z_sb_r)
        t_at = both(lambda a: a[:, :, :], t_sb, t_sb_r)
        spare_at = both(lambda a: a[:, :, :, :].rearrange("p t h d -> p (t h d)")[:, 0:NT * D].rearrange(
            "p (t n) -> p t n", t=NT), v_sb, v_sb_r)
        t_lo = both(lambda a: a[:, 3, :, :], wslot, wslot_r)
        wide_at = both(lambda a: a[:, :, :], wide, wide_r)
        wide_lo = both(lambda a: a[:, 1:3, :, :].rearrange("p s t n -> p (s t) n"), wslot, wslot_r)
        c1_hi, c1_lo = both(lambda a: a[:, :, :], q_t, q_t_r), both(lambda a: a[:, :, :], k_t, k_t_r)
        c2_hi = both(lambda a: a[:, NT:, :], wide, wide_r)
        c2_lo = both(lambda a: a[:, 0, :, :], wslot, wslot_r)

        def unit(n):
            return both(lambda a: a[:, n * FT:(n + 1) * FT, :], big, big_r)

        weights = {"w1_0": (unit(0), unit(1)), "w2_0": (unit(2), unit(3)), "w_lr": (unit(0), unit(1)),
                   "w1_2": (unit(2), unit(3)), "w2_2": (unit(0), unit(1)), "w_3": (unit(2), unit(3))}

        def colp(name, t):
            a, _ = COLS[name]
            return col[:, a + t:a + t + 1]

        def rowp(name):
            return row_bc[:, ROWS.index(name), :]

        bank = [ctx.enter_context(nc.psum_tensor(f"bank{i}", [P, 512], F32)) for i in range(8)]

        sorted_d = nc.dram_tensor("sorted_records", [GT * P, REC], F32)

        S = {name: sem(name) for name in (
            "x_in", "src_in", "dst_in", "bias_in", "cols_in", "rows_in", "eps_in", "wq_in", "wk_in", "wv_in",
            "wo_in", "w1_0_in", "w1_0_hi", "w1_0_lo", "w2_0_in", "w2_0_hi", "w2_0_lo", "w_lr_in", "w_lr_hi",
            "w_lr_lo", "w1_2_in", "w1_2_hi", "w1_2_lo", "w2_2_in", "w2_2_hi", "w2_2_lo", "w_3_in", "w_3_hi",
            "w_3_lo", "hi_vector", "hi_scalar", "lo_vector", "lo_pool", "wo_hi", "wo_lo", "base_ready",
            "rcnt_ready", "dinv_ready", "mean_c1_ready", "gcn_c1_ready", "c2_hi_ready", "mean_ready", "srec_in",
            "cleared", "scattered", "out_done", "vector_order", "scalar_order", "pool_order", "consts", "kept",
            "eps_column", "empties", "ln_var", "ln_std", "ln_coef", "h_ready", "z_ready", "edge_sums",
            "edge_bases", "bias_top", "bias_top_all", "bias_low", "rec_ready", "weights_exp", "rows_made",
            "rest_rows_made", "turned", "t_ready", "q_mm", "q_ready", "k_mm", "k_ready", "v_mm", "v_ready",
            "c1_ready", "no_edge_ready", "bv_in", "earlier_ready", "index_steps", "split_steps", "round_built",
            "table_ready", "scatter_open", "b_out", "peak_steps", "peaks", "peak_mm", "diag_steps", "diag_ready",
            "floor_mm", "lowered", "wd_ready", "wd_used", "b_mm", "b_ready", "st_mm", "score_ready", "e_ready",
            "p_ready", "last_p_ready", "rest_steps", "rest_split", "pv_mm", "att_ready", "wo_mm", "ff1_mm",
            "ff1_ready", "ff2_mm", "deg_mm", "deg_diag", "deg_std", "deg_ready", "loop_steps", "c2_turned", "c2_ready",
            "agg1_mm", "lin1_mm", "lin1_ready", "bn_var", "bn_std", "bn_coef", "bn_ready", "back_mm", "y_ready",
            "agg2_mm", "agg2_ready", "gcn1_mm", "gcn1_ready", "gcn2_mm", "gcn2_ready", "agg2b_mm", "agg3_mm",
            "agg3_ready", "gin1_mm", "gin1_ready", "gin2_mm", "out_ready")}
        parts, made = {}, {"hi_vector": 0, "hi_scalar": 0, "lo_vector": 0, "lo_pool": 0}
        for name, tiles, hi_by, lo_by in (
                ("att", NT, "vector", "vector"), ("ff_in", NT, "vector", "vector"), ("ff_mid", FT, "scalar", "vector"),
                ("h1", NT, "scalar", "vector"), ("mean", NT, "vector", "pool"), ("h1_t", NT, "vector", "vector"),
                ("y", NT, "scalar", "pool"), ("gcn_in", NT, "vector", "pool"), ("gcn_mid", FT, "scalar", "vector"),
                ("gcn_out", NT, "scalar", "vector"), ("h3", NT, "scalar", "pool"),
                ("gin_in", NT, "vector", "pool"), ("gin_mid", NT, "scalar", "vector")):
            hi_by, lo_by = "hi_" + hi_by, "lo_" + lo_by
            parts[name] = (hi_by, made[hi_by], lo_by, made[lo_by])
            made[hi_by] += tiles
            made[lo_by] += tiles
        block = ctx.enter_context(nc.Block())

        @block.sync
        def _(sp):
            sp.wait_ge(S["empties"], 1)

            def clear():
                sp.dma_start(sorted_d[:, :].rearrange("(p s g) r -> p s (g r)", p=P, s=4),
                             empty.unsqueeze(1).broadcast_to([P, 4, GT * REC // 4])).then_inc(S["cleared"], 16)

            clear()
            sp.wait_ge(S["bias_in"], 16)
            sp.dma_start(x_sb[:, :, :], k_major(x)).then_inc(S["x_in"], 16)
            sp.dma_start(wslot[:, 0, :, :], k_major(wq)).then_inc(S["wq_in"], 16)
            sp.dma_start(wslot[:, 1, :, :], k_major(wk)).then_inc(S["wk_in"], 16)
            sp.dma_start(wslot[:, 2, :, :], k_major(wv)).then_inc(S["wv_in"], 16)
            sp.dma_start(row_bc[:, 0, :], rows[0:1, :].partition_broadcast(P)).then_inc(S["bv_in"], 16)
            sp.wait_ge(S["cleared"], 16)
            sp.sem_inc(S["table_ready"], 1)
            sp.dma_start(wslot[:, 3, :, :], k_major(wo)).then_inc(S["wo_in"], 16)
            sp.wait_ge(S["turned"], NT)
            sp.wait_ge(S["earlier_ready"], 1)
            rounds = sp.value_load(rounds_i[0:1, 0:1], min_val=1, max_val=E // CAP + 1)
            with nc.sync.Fori(0, rounds) as r:
                sp.wait_ge(S["round_built"], r + 1)
                sp.wait_ge(S["scattered"], 16 * ET * r + 16 * ET)
                sp.dma_start(srec.rearrange("p g r -> p (g r)"),
                             sorted_d[:, :].rearrange("(p g) r -> p (g r)", p=P)).then_inc(S["srec_in"], 16)
                sp.wait_ge(S["srec_in"], 16 * r + 16)
                clear()
                sp.wait_ge(S["cleared"], 16 * r + 32)
                sp.sem_inc(S["table_ready"], 1)
            sp.wait_ge(S["round_built"], rounds + 1)
            sp.wait_ge(S["b_ready"], rounds * NB + 2)
            for n in range(1, len(ROWS)):
                sp.dma_start(row_bc[:, n, :], rows[n:n + 1, :].partition_broadcast(P)
                             ).then_inc(S["rows_in"], 16)
            sp.wait_ge(S["pv_mm"], H)

            def load(name, matrix, half=None):
                to = weights[name][0].full
                if half is not None:
                    to = to[:, half * NT:(half + 1) * NT, :]
                elif matrix.shape[1] == F:
                    to = to.rearrange("p (k a) n -> p k (a n)", a=2)
                sp.dma_start(to, k_major(matrix)).then_inc(S[name + "_in"], 16)

            load("w1_0", w1_0)
            load("w2_0", w2_0)
            sp.wait_ge(S["ff1_mm"], FT)
            load("w_lr", wl_t, 0)
            load("w_lr", wr_t, 1)
            sp.wait_ge(S["ff2_mm"], NT)
            load("w1_2", w1_2)
            sp.wait_ge(S["lin1_mm"], NT)
            load("w2_2", w2_2)
            sp.wait_ge(S["gcn1_mm"], FT)
            load("w_3", w1_3t, 0)
            load("w_3", w2_3t, 1)
            for t in range(NT):
                sp.wait_ge(S["out_ready"], t + 1)
                sp.dma_start(out[t * P:(t + 1) * P, :], z_sb[:, t, :]).then_inc(S["out_done"], 16)
            sp.wait_ge(S["out_done"], 16 * NT)

        @block.gpsimd
        def _(pool):
            nc.gpsimd.memset(empty, -1.0).then_inc(S["empties"], 1)
            nc.gpsimd.iota(iota_i[:, :], [[1, N]], base=0, channel_multiplier=0).then_inc(S["pool_order"], 1)
            nc.gpsimd.memset(keep, 1.0).then_inc(S["kept"], 1)
            nc.gpsimd.memset(ident[:, :], 0.0).then_inc(S["pool_order"], 1)
            nc.gpsimd.memset(ones[:, :], 1.0).then_inc(S["pool_order"], 1)
            pool.wait_ge(S["pool_order"], 3)
            nc.gpsimd.affine_select(out=ident[:, :], in_=ident[:, :], compare_op=ALU.not_equal, fill=1.0,
                                    base=0, pattern=[[-1, P]], channel_multiplier=1).then_inc(S["consts"], 1)
            nc.gpsimd.affine_select(out=before[:, :], in_=ones[:, :], compare_op=ALU.is_gt, fill=0.0,
                                    base=0, pattern=[[1, P]], channel_multiplier=-1).then_inc(S["consts"], 1)
            pool.wait_ge(S["bias_top"], 1)
            nc.gpsimd.partition_all_reduce(bmax_all[:, :], bmax[:, :], P,
                                           bass.bass_isa.ReduceOp.max).then_inc(S["bias_top_all"], 1)
            pool.wait_ge(S["rec_ready"], 2)
            pool.wait_ge(S["weights_exp"], 1)
            pool.wait_ge(S["earlier_ready"], 1)
            rounds = pool.value_load(rounds_i[0:1, 0:1], min_val=1, max_val=E // CAP + 1)
            last_row = pool.to_reg(REC_SLOTS - 1)
            with nc.gpsimd.Fori(0, rounds) as r:
                pool.wait_ge(S["table_ready"], r + 1)
                pool.wait_ge(S["rows_made"], r + 1)
                pool.sem_inc(S["scatter_open"], 1)
                for t in range(ET):
                    if t == EARLY:
                        pool.wait_ge(S["rest_rows_made"], r + 1)
                        pool.sem_inc(S["scatter_open"], 1)
                    nc.gpsimd.indirect_dma_start(
                        out=sorted_d[:, :], out_offset=bass.IndirectOffsetOnAxis(ap=row_i[:, t:t + 1], axis=0),
                        in_=rec[:, t, :], in_offset=None, bounds_check=last_row, oob_is_err=False
                    ).then_inc(S["scattered"], 16)
                pool.wait_ge(S["srec_in"], 16 * r + 16)
                pool.sem_inc(S["rest_steps"], 1)

                def split(n, ins):
                    ins.then_inc(S["rest_steps"], 1)
                    pool.wait_ge(S["rest_steps"], r * 7 + 2 * n)
                    pool.sem_inc(S["rest_steps"], 1)

                f = slice(FIRST, GT)
                split(1, nc.gpsimd.tensor_copy(wpart[:, f, 1:1 + H], srec[:, f, 2:REC]))
                split(2, nc.gpsimd.tensor_tensor(wrest[:, f, :], srec[:, f, 2:REC], wpart[:, f, 1:1 + H], ALU.subtract))
                split(3, nc.gpsimd.tensor_copy(wpart[:, f, 1 + H:1 + 2 * H], wrest[:, f, :]))
                nc.gpsimd.tensor_tensor(wpart[:, f, 1 + 2 * H:], wrest[:, f, :],
                                        wpart[:, f, 1 + H:1 + 2 * H], ALU.subtract
                                        ).then_inc(S["rest_split"], 1)
                with nc.gpsimd.Fori(0, NB // 2) as i:
                    for u in range(2):
                        pool.wait_ge(S["b_out"], r * NB + i * 2 + (u + 3))
                        part = stage[:, u, :].rearrange("p (t c) -> p t c", c=SC)
                        at = bass.ds(i * (2 * BS) + u * BS, BS)
                        nc.gpsimd.tensor_tensor(c2[:, :, at], c2[:, :, at], part[:, :, 0:BS], ALU.add)
                        nc.gpsimd.tensor_tensor(b_sums[:, :, :, at], b_sums[:, :, :, at],
                                                part[:, :, BS:].rearrange("p t (h i) -> p t h i", i=BS), ALU.add
                                                ).then_inc(S["b_ready"], 1)
            pool.wait_ge(S["b_ready"], rounds * NB + 2)
            for h in range(H):
                for t in range(NT if h < H - 1 else NT // 2):
                    pool.wait_ge(S["e_ready"], h * NT + t + 1)
                    p = big[:, t * H + h, :]
                    nc.gpsimd.tensor_tensor(p, score[h % 3][:, t, :], p, ALU.mult).then_inc(S["p_ready"], 1)
            order = [0]

            def link(ins):
                order[0] += 1
                ins.then_inc(S["loop_steps"], 1)
                pool.wait_ge(S["loop_steps"], order[0])

            def weight_lo(name):
                lo, hi = weights[name]
                for q in range(4):
                    part = slice(q * FT // 4, (q + 1) * FT // 4)
                    pool.wait_ge(S[name + "_hi"], q + 1)
                    nc.gpsimd.tensor_tensor(lo.rounded[:, part, :], lo.full[:, part, :],
                                            hi.rounded[:, part, :].bitcast(F32),
                                            ALU.subtract).then_inc(S[name + "_lo"], 1)

            def split_lo(name, t, whole, hi, ready=None, before=0):
                hi_by, before_hi, lo_by, _ = parts[name]
                if ready:
                    pool.wait_ge(S[ready], before + t + 1)
                pool.wait_ge(S[hi_by], before_hi + t + 1)
                nc.gpsimd.tensor_tensor(whole.rounded[:, t, :], whole.full[:, t, :],
                                        hi.rounded[:, t, :].bitcast(F32), ALU.subtract).then_inc(S[lo_by], 1)

            def c1_parts(row, done):
                for t in range(NT):
                    link(nc.gpsimd.tensor_tensor(c1_lo.full[:, t, :], c1[:, t, :], row[:, :], ALU.mult))
                    link(nc.gpsimd.tensor_scalar(c1_hi.rounded[:, t, :], c1_lo.full[:, t, :], 1.0, None, ALU.mult))
                    nc.gpsimd.tensor_tensor(c1_lo.rounded[:, t, :], c1_lo.full[:, t, :],
                                            c1_hi.rounded[:, t, :].bitcast(F32),
                                            ALU.subtract).then_inc(S[done], 1)

            pool.wait_ge(S["eps_in"], 16)
            link(nc.gpsimd.tensor_scalar(gin_c[:, :], gin_c[:, :], 1.0, None, ALU.add))
            link(nc.gpsimd.tensor_scalar(loop_i[:, :], ident[:, :], gin_c[:, 0:1], None, ALU.mult))
            for t in range(NT):
                pool.wait_ge(S["wo_hi"], t + 1)
                nc.gpsimd.tensor_tensor(t_lo.rounded[:, t, :], t_lo.full[:, t, :],
                                        c1_hi.rounded[:, t, :].bitcast(F32), ALU.subtract).then_inc(S["wo_lo"], 1)
            pool.wait_ge(S["c1_ready"], NT)
            for t in range(NT):
                d = slice(t * P, (t + 1) * P)
                nc.gpsimd.tensor_tensor(c2[:, t, d], c2[:, t, d], loop_i[:, :], ALU.add
                                        ).then_inc(S["c2_ready"], 1)
            weight_lo("w1_0")
            pool.wait_ge(S["z_ready"], 2 * NT)
            for t in range(NT):
                link(nc.gpsimd.tensor_tensor(h_sb[:, t, :], h_sb[:, t, :], rowp("b2_0"), ALU.add))
                nc.gpsimd.tensor_tensor(h_sb[:, t, :], h_sb[:, t, :], x_sb[:, t, :], ALU.add
                                        ).then_inc(S["base_ready"], 1)
            weight_lo("w2_0")
            pool.wait_ge(S["wo_mm"], NT)
            pool.wait_ge(S["rcnt_ready"], 1)
            c1_parts(rcnt_bc, "mean_c1_ready")
            weight_lo("w_lr")
            for t in range(NT):
                split_lo("mean", t, wide_lo, wide_at)
            pool.wait_ge(S["agg1_mm"], NT)
            for t in range(NT):
                d = slice(t * P, (t + 1) * P)
                link(nc.gpsimd.tensor_tensor(c1[:, t, d], c1[:, t, d], ident[:, :], ALU.add))
            pool.wait_ge(S["dinv_ready"], 2)
            c1_parts(dinv_bc, "gcn_c1_ready")
            weight_lo("w1_2")
            for t in range(NT):
                split_lo("y", t, z_at, spare_at, "y_ready")
            for t in range(NT):
                split_lo("gcn_in", t, t_lo, t_at)
            weight_lo("w2_2")
            weight_lo("w_3")
            pool.wait_ge(S["c2_hi_ready"], NT)
            for t in range(NT):
                nc.gpsimd.tensor_tensor(c2_lo.rounded[:, t, :], c2[:, t, :], c2_hi.rounded[:, t, :].bitcast(F32),
                                        ALU.subtract).then_inc(S["c2_ready"], 1)
            for t in range(NT):
                split_lo("h3", t, h_at, t_at, "h_ready", 2 * NT)
            for t in range(NT):
                split_lo("gin_in", t, z_at, spare_at)

        @block.scalar
        def _(act):
            act.dma_start(idx_src[:, :], src.rearrange("(p t) -> p t", p=P)).then_inc(S["src_in"], 16)
            act.dma_start(idx_dst[:, :], dst.rearrange("(p t) -> p t", p=P)).then_inc(S["dst_in"], 16)
            act.dma_start(att_b[:, :, :], bias.rearrange("(p t) h -> p t h", p=P)).then_inc(S["bias_in"], 16)
            act.dma_start(col[:, :], cols).then_inc(S["cols_in"], 16)
            act.dma_start(gin_c[:, :], eps.rearrange("(a b) -> a b", a=1).partition_broadcast(P)
                          ).then_inc(S["eps_in"], 16)

            def ln_std(n, t):
                act.wait_ge(S["ln_var"], n * NT + t + 1)
                nc.scalar.activation(std[:, t:t + 1], mv[:, t, 1:2], ACT.Sqrt, bias=eps_c[:, 0:1]
                                     ).then_inc(S["ln_std"], 1)

            def twice(name, t, whole, hi, source, function, done, between=None, **kw):
                nc.scalar.activation(hi.rounded[:, t, :], source, function, **kw).then_inc(S[parts[name][0]], 1)
                if between:
                    between()
                nc.scalar.activation(whole.full[:, t, :], source, function, **kw).then_inc(S[done], 1)

            def ln_relu_parts(n, name, whole, hi, done, ahead=False):
                for t in range(NT):
                    if t == 0 or not ahead:
                        ln_std(n, t)
                    act.wait_ge(S["ln_coef"], n * NT + t + 1)
                    twice(name, t, whole, hi, x_sb[:, t, :], ACT.Relu, done,
                          between=(lambda: ln_std(n, t + 1)) if ahead and t < NT - 1 else None,
                          bias=shift[:, t:t + 1], scale=rstd[:, t:t + 1])

            def ln_relu(n, to, done):
                for t in range(NT):
                    ln_std(n, t)
                    act.wait_ge(S["ln_coef"], n * NT + t + 1)
                    nc.scalar.activation(to[:, t, :], x_sb[:, t, :], ACT.Relu, bias=shift[:, t:t + 1],
                                         scale=rstd[:, t:t + 1]).then_inc(S[done], 1)

            def weight_hi(name, q):
                part = slice(q * FT // 4, (q + 1) * FT // 4)
                lo, hi = weights[name]
                nc.scalar.copy(hi.rounded[:, part, :], lo.full[:, part, :]).then_inc(S[name + "_hi"], 1)

            def to_t(done, banks, to=t_sb, gain=None, offset=None):
                for t in range(NT):
                    act.wait_ge(S["turned"], done + t + 1)
                    kw = {}
                    if gain:
                        kw = dict(bias=colp(offset, t), scale=colp(gain, t))
                    nc.scalar.activation(to[:, t, :], bank[banks + t][:, :], ACT.Identity, **kw
                                         ).then_inc(S["t_ready"], 1)

            act.wait_ge(S["bias_low"], 1)
            act.wait_ge(S["empties"], 1)
            nc.scalar.activation(rec[:, :, 2:REC], att_b[:, :, :], ACT.Exp).then_inc(S["weights_exp"], 1)
            act.wait_ge(S["eps_column"], 1)
            ln_relu(0, h_sb, "h_ready")
            for t in range(NT):
                ln_std(1, t)
            act.wait_ge(S["cols_in"], 16)
            nc.scalar.mul(bq8[:, :], col[:, COLS["bq"][0]:COLS["bq"][0] + NT], DH ** -0.5
                          ).then_inc(S["scalar_order"], 1)
            to_t(0, 0, t_sb, "ln1_g", "ln1_b")
            act.wait_ge(S["scalar_order"], 1)
            for t in range(NT):
                act.wait_ge(S["q_mm"], t + 1)
                nc.scalar.activation(q_t[:, t, :], bank[4 + t][:, :], ACT.Identity, bias=bq8[:, t:t + 1],
                                     scale=DH ** -0.5).then_inc(S["q_ready"], 1)
            for t in range(NT):
                act.wait_ge(S["k_mm"], t + 1)
                nc.scalar.activation(k_t[:, t, :], bank[t][:, :], ACT.Identity, bias=colp("bk", t)
                                     ).then_inc(S["k_ready"], 1)
            act.wait_ge(S["earlier_ready"], 1)
            rounds = act.value_load(rounds_i[0:1, 0:1], min_val=1, max_val=E // CAP + 1)
            act.wait_ge(S["v_mm"], NT)
            act.sem_inc(S["b_out"], 2)
            with nc.scalar.Fori(0, rounds) as r:
                with nc.scalar.Fori(0, NB // 2) as i:
                    for u in range(2):
                        act.wait_ge(S["b_mm"], r * NB + i * 2 + (u + 1))
                        act.wait_ge(S["b_ready"], r * NB + i * 2 + (u + 1))
                        nc.scalar.copy(stage[:, u, 0:2 * SC], bank[4 + 2 * u][:, 0:2 * SC])
                        nc.scalar.copy(stage[:, u, 2 * SC:], bank[5 + 2 * u][:, 0:2 * SC]).then_inc(S["b_out"], 1)

            def exps(h):
                for t in range(NT):
                    act.wait_ge(S["lowered"], h * NT + t + 1)
                    nc.scalar.activation(score[h % 3][:, t, :], score[h % 3][:, t, :], ACT.Exp
                                         ).then_inc(S["e_ready"], 1)

            for h in range(H):
                for t in range(NT):
                    act.wait_ge(S["st_mm"], h * NT + t + 1)
                    if h >= 3:
                        act.wait_ge(S["p_ready"], (h - 3) * NT + t + 1)
                    if h == 0:
                        act.wait_ge(S["b_ready"], rounds * NB + 2)
                    nc.scalar.copy(score[h % 3][:, t, :], bank[t][:, :]).then_inc(S["score_ready"], 1)
                if h == 0:
                    for t in range(NT):
                        act.wait_ge(S["c2_turned"], t + 1)
                        nc.scalar.copy(c1[:, t, :], bank[4 + t][:, :]).then_inc(S["c1_ready"], 1)
                if h >= 2:
                    exps(h - 2)
            exps(H - 2)
            exps(H - 1)
            act.wait_ge(S["wo_in"], 16)
            for t in range(NT):
                nc.scalar.copy(c1_hi.rounded[:, t, :], t_lo.full[:, t, :]).then_inc(S["wo_hi"], 1)
            to_t(NT, 0, c1_lo.full)
            for t in range(NT):
                ln_std(2, t)
                if t == 0:
                    act.wait_ge(S["w1_0_in"], 16)
                    weight_hi("w1_0", 0)
                if t < NT - 1:
                    weight_hi("w1_0", t + 1)
            nc.scalar.activation(dinv_c[:, :], deg[:, :], ACT.Sqrt, bias=1.0).then_inc(S["deg_std"], 1)
            to_t(2 * NT, 0, t_lo.full, "ln2_g", "ln2_b")
            act.wait_ge(S["deg_ready"], 3)
            nc.scalar.activation(dinv_bc[:, :], dinv_bc[:, :], ACT.Sqrt, bias=1.0).then_inc(S["deg_std"], 1)
            for f in range(FT):
                act.wait_ge(S["ff1_mm"], f + 1)
                twice("ff_mid", f, wide_lo, wide_at, bank[(4 + f) % 8][:, :], ACT.Silu, "ff1_ready",
                      bias=colp("b1_0", f))
                if f == 0:
                    act.wait_ge(S["w2_0_in"], 16)
                if f < 4:
                    weight_hi("w2_0", f)
            ln_relu_parts(3, "h1", h_at, z_at, "h_ready")
            for t in range(NT):
                act.wait_ge(S["agg1_mm"], t + 1)
                nc.scalar.copy(wide_lo.full[:, t, :], bank[t][:, :]).then_inc(S["mean_ready"], 1)
            to_t(3 * NT, 4, t_lo.full)
            for t in range(NT):
                act.wait_ge(S["lin1_mm"], t + 1)
                nc.scalar.activation(z_sb[:, t, :], bank[t][:, :], ACT.Identity, bias=colp("b_l", t)
                                     ).then_inc(S["lin1_ready"], 1)
                act.wait_ge(S["bn_var"], t + 1)
                nc.scalar.activation(std[:, t:t + 1], mv[:, t, 1:2], ACT.Sqrt, bias=eps_c[:, 0:1]
                                     ).then_inc(S["bn_std"], 1)
                act.wait_ge(S["bn_coef"], t + 1)
                nc.scalar.activation(bn_t[:, t, :], z_sb[:, t, :], ACT.Relu, bias=shift[:, t:t + 1],
                                     scale=rstd[:, t:t + 1]).then_inc(S["bn_ready"], 1)
            ln_relu_parts(4, "y", z_at, spare_at, "y_ready", ahead=True)
            for t in range(NT):
                act.wait_ge(S["agg2_mm"], t + 1)
                nc.scalar.copy(t_lo.full[:, t, :], bank[t][:, :]).then_inc(S["agg2_ready"], 1)
            for f in range(FT):
                act.wait_ge(S["gcn1_mm"], f + 1)
                twice("gcn_mid", f, wide_lo, wide_at, bank[(4 + f) % 8][:, :], ACT.Relu, "gcn1_ready",
                      bias=colp("b1_2", f))
            for t in range(NT):
                act.wait_ge(S["gcn2_mm"], t + 1)
                twice("gcn_out", t, z_at, spare_at, bank[4 + t][:, :], ACT.Identity, "gcn2_ready",
                      scale=dinv_c[:, t:t + 1])
            ln_relu_parts(5, "h3", h_at, t_at, "h_ready", ahead=True)
            for t in range(NT):
                act.wait_ge(S["agg3_mm"], t + 1)
                nc.scalar.copy(z_sb[:, t, :], bank[4 + t][:, :]).then_inc(S["agg3_ready"], 1)
            for t in range(NT):
                act.wait_ge(S["gin1_mm"], t + 1)
                twice("gin_mid", t, wide_lo, wide_at, bank[t][:, :], ACT.Relu, "gin1_ready", bias=colp("b1_3", t))
            for t in range(NT):
                ln_std(6, t)

        @block.vector
        def _(dve):
            order = [0]

            def link(ins):
                order[0] += 1
                ins.then_inc(S["vector_order"], 1)
                dve.wait_ge(S["vector_order"], order[0])

            def mark(ins):
                order[0] += 1
                ins.then_inc(S["vector_order"], 1)

            def settle():
                dve.wait_ge(S["vector_order"], order[0])

            def split_hi(name, t, whole, hi):
                nc.vector.tensor_copy(hi.rounded[:, t, :], whole.full[:, t, :]).then_inc(S[parts[name][0]], 1)

            def split_lo(name, t, whole, hi, lo=None):
                hi_by, before_hi, lo_by, _ = parts[name]
                dve.wait_ge(S[hi_by], before_hi + t + 1)
                to = whole if lo is None else lo
                nc.vector.tensor_tensor(to.rounded[:, t, :], whole.full[:, t, :], hi.rounded[:, t, :].bitcast(F32),
                                        ALU.subtract).then_inc(S[lo_by], 1)

            def weight_hi(name, loaded=16):
                lo, hi = weights[name]
                dve.wait_ge(S[name + "_in"], loaded)
                for q in range(4):
                    part = slice(q * FT // 4, (q + 1) * FT // 4)
                    nc.vector.tensor_copy(hi.rounded[:, part, :], lo.full[:, part, :]
                                          ).then_inc(S[name + "_hi"], 1)

            def moments(t, source, done):
                link(nc.vector.bn_stats(stats[:, t, :], source[:, t, :]))
                nc.vector.bn_aggr(mv[:, t, :], stats[:, t, :]).then_inc(S[done], 1)

            def ln_coef(n, t, divided=False):
                c = slice(t, t + 1)
                dve.wait_ge(S["ln_std"], n * NT + t + 1)
                link(nc.vector.reciprocal(rstd[:, c], std[:, c]))
                if divided:
                    link(nc.vector.tensor_tensor(rstd[:, c], rstd[:, c], dinv_c[:, c], ALU.mult))
                nc.vector.scalar_tensor_tensor(out=shift[:, c], in0=mv[:, t, 0:1], scalar=-1.0, in1=rstd[:, c],
                                               op0=ALU.mult, op1=ALU.mult).then_inc(S["ln_coef"], 1)

            def ln_plain(n, t, source):
                dve.wait_ge(S["ln_coef"], n * NT + t + 1)
                nc.vector.tensor_scalar(z_sb[:, t, :], source[:, t, :], rstd[:, t:t + 1], shift[:, t:t + 1],
                                        ALU.mult, ALU.add).then_inc(S["z_ready"], 1)

            nc.vector.memset(eps_c[:, :], LN_EPS).then_inc(S["eps_column"], 1)
            mark(nc.vector.memset(v_sb[:, :, :, DH:DH + 1], 1.0))
            mark(nc.vector.memset(wpart[:, :, 0:1], 1.0))
            dve.wait_ge(S["pool_order"], 1)
            mark(nc.vector.tensor_copy(iota_n[:, :], iota_i[:, :]))
            mark(nc.vector.tensor_copy(iota_b[:, :], iota_i[:, 0:NB]))
            settle()
            dve.wait_ge(S["kept"], 1)
            mark(nc.vector.memset(keep.rearrange("p (b t) -> p b t", b=NB)[:, :, 0:1], 0.0))
            dve.wait_ge(S["src_in"], 16)
            mark(nc.vector.tensor_copy(src_f[:, :], idx_src[:, :]))
            link(nc.vector.tensor_single_scalar(src_i[:, :], idx_src[:, :], 4, ALU.logical_shift_right))
            link(nc.vector.tensor_copy(blk_f[:, :], src_i[:, :]))
            oh = onehot.rearrange("p (b t) -> p b t", b=NB)
            pf = prefix.rearrange("p (b t) -> p b t", b=NB)
            link(nc.vector.tensor_tensor(oh, blk_f[:, :].unsqueeze(1).broadcast_to([P, NB, ET]),
                                         iota_b[:, :].unsqueeze(2).broadcast_to([P, NB, ET]), ALU.is_equal))
            nc.vector.tensor_tensor_scan(prefix, keep, onehot, 0.0, ALU.mult, ALU.add).then_inc(S["edge_sums"], 1)
            dve.wait_ge(S["empties"], 1)
            nc.vector.scalar_tensor_tensor(out=rec[:, :, 0], in0=blk_f[:, :], scalar=-float(BS), in1=src_f[:, :],
                                           op0=ALU.mult, op1=ALU.add).then_inc(S["rec_ready"], 1)
            dve.wait_ge(S["dst_in"], 16)
            link(nc.vector.tensor_copy(dst_f[:, :], idx_dst[:, :]))
            nc.vector.tensor_copy(rec[:, :, 1], dst_f[:, :]).then_inc(S["rec_ready"], 1)
            dve.wait_ge(S["edge_bases"], 2)
            mark(nc.vector.tensor_copy(earlier[:, :], bank[7][:, 0:NB]))
            link(nc.vector.tensor_reduce(top[:, :], bank[7][:, NB:2 * NB], AX.X, ALU.max))
            link(nc.vector.tensor_scalar(over[:, :], iota_b[:, :], float(CAP), top[:, 0:1], ALU.mult, ALU.is_lt))
            link(nc.vector.tensor_reduce(rounds_f[:, :], over[:, :], AX.X, ALU.add))
            nc.vector.tensor_copy(rounds_i[:, :], rounds_f[:, :]).then_inc(S["earlier_ready"], 1)
            dve.wait_ge(S["bias_in"], 16)
            nc.vector.tensor_reduce(bmax[:, :], att_b[:, :, :].rearrange("p t h -> p h t"), AX.X, ALU.max
                                    ).then_inc(S["bias_top"], 1)

            def ranks(c):
                n = c.stop - c.start
                link(nc.vector.tensor_tensor(pf[:, :, c], pf[:, :, c],
                                             earlier[:, :].unsqueeze(2).broadcast_to([P, NB, n]), ALU.add))
                link(nc.vector.tensor_tensor(pf[:, :, c], pf[:, :, c], oh[:, :, c], ALU.mult))
                link(nc.vector.tensor_reduce(rank_f[:, c], pf[:, :, c].rearrange("p b t -> p t b"), AX.X, ALU.add))
                link(nc.vector.tensor_single_scalar(rank_f[:, c], rank_f[:, c], -1.0, ALU.add))

            INDEX_STEPS = 8

            def make_rows(base, c, done):
                at = [0]

                def step(ins):
                    at[0] += 1
                    ins.then_inc(S["index_steps"], 1)
                    dve.wait_ge(S["index_steps"], base + at[0])

                if type(base) is not int:
                    dve.wait_ge(S["index_steps"], base)
                near_i, near_f, rank = near_i_all[:, c], near_f_all[:, c], rank_f[:, c]
                step(nc.vector.tensor_scalar(near_i, rank, 0.0, float(CAP - 1), ALU.max, ALU.min))
                step(nc.vector.tensor_copy(near_f, near_i))
                step(nc.vector.tensor_single_scalar(slot_lo[:, c], near_i, P - 1, ALU.bitwise_and))
                step(nc.vector.tensor_single_scalar(slot_hi[:, c], near_i, 7, ALU.logical_shift_right))
                step(nc.vector.tensor_tensor(near_f, near_f, rank, ALU.not_equal))
                step(nc.vector.scalar_tensor_tensor(out=near_i, in0=slot_lo[:, c], scalar=float(GT),
                                                    in1=slot_hi[:, c], op0=ALU.mult, op1=ALU.add))
                step(nc.vector.scalar_tensor_tensor(out=near_i, in0=blk_f[:, c], scalar=float(BT),
                                                    in1=near_i, op0=ALU.mult, op1=ALU.add))
                nc.vector.scalar_tensor_tensor(out=row_i[:, c], in0=near_f, scalar=FAR, in1=near_i,
                                               op0=ALU.mult, op1=ALU.add).then_inc(S[done], 1)
                nc.vector.tensor_single_scalar(rank, rank, -float(CAP), ALU.add).then_inc(S["index_steps"], 1)

            ranks(slice(0, EARLY))
            dve.wait_ge(S["bias_top_all"], 1)
            link(nc.vector.tensor_single_scalar(bmax_all[:, :], bmax_all[:, :], -W_SHIFT, ALU.add))
            nc.vector.tensor_tensor(att_b[:, :, :], att_b[:, :, :],
                                    bmax_all[:, :].unsqueeze(1).broadcast_to([P, ET, H]), ALU.subtract
                                    ).then_inc(S["bias_low"], 1)
            make_rows(0, slice(0, EARLY), "rows_made")
            ranks(slice(EARLY, ET))
            make_rows(INDEX_STEPS, slice(EARLY, ET), "rest_rows_made")
            dve.wait_ge(S["x_in"], 16)
            for t in range(NT):
                moments(t, x_sb, "ln_var")
            for t in range(NT):
                ln_coef(0, t)
            for t in range(NT):
                dve.wait_ge(S["h_ready"], t + 1)
                moments(t, h_sb, "ln_var")
            for t in range(NT):
                ln_coef(1, t)
                ln_plain(1, t, h_sb)
            dve.wait_ge(S["consts"], 1)
            mark(nc.vector.tensor_copy(ident_b[:, :], ident[:, :]))
            dve.wait_ge(S["weights_exp"], 1)
            half = NT * H // 2
            nc.vector.memset(big[:, 0:half, :], 0.0).then_inc(S["b_ready"], 1)
            nc.vector.memset(big[:, half:, :], 0.0).then_inc(S["b_ready"], 1)
            dve.wait_ge(S["q_mm"], NT)
            mark(nc.vector.memset(c2, 0.0))
            dve.wait_ge(S["bv_in"], 16)
            for t in range(NT):
                dve.wait_ge(S["v_mm"], t + 1)
                nc.vector.tensor_tensor(v_sb[:, t, :, 0:DH], bank[4 + t][:, :].rearrange("p (h d) -> p h d", h=H),
                                        rowp("bv").rearrange("p (h d) -> p h d", h=H), ALU.add
                                        ).then_inc(S["v_ready"], 1)
            settle()
            dve.sem_inc(S["round_built"], 1)
            rounds = dve.value_load(rounds_i[0:1, 0:1], min_val=1, max_val=E // CAP + 1)
            with nc.vector.Fori(0, rounds) as r:
                dve.wait_ge(S["srec_in"], 16 * r + 16)

                def split(n, ins):
                    ins.then_inc(S["split_steps"], 1)
                    dve.wait_ge(S["split_steps"], r * 7 + n)

                f = slice(0, FIRST)
                split(1, nc.vector.tensor_copy(wpart[:, f, 1:1 + H], srec[:, f, 2:REC]))
                split(2, nc.vector.tensor_tensor(wrest[:, f, :], srec[:, f, 2:REC], wpart[:, f, 1:1 + H], ALU.subtract))
                split(3, nc.vector.tensor_copy(wpart[:, f, 1 + H:1 + 2 * H], wrest[:, f, :]))
                split(4, nc.vector.tensor_tensor(wpart[:, f, 1 + 2 * H:], wrest[:, f, :],
                                                 wpart[:, f, 1 + H:1 + 2 * H], ALU.subtract))
                nc.vector.tensor_tensor(own_hot, iota_b[:, 0:BS].unsqueeze(1).broadcast_to([P, GT, BS]),
                                        srec[:, :, 0:1].broadcast_to([P, GT, BS]), ALU.is_equal
                                        ).then_inc(S["split_steps"], 1)
                dve.wait_ge(S["split_steps"], r * 7 + 5)
                dve.sem_inc(S["split_steps"], 1)

                def two_blocks(i):
                    for u in range(2):
                        for q in range(BT):
                            dve.wait_ge(S["wd_used"], r * GT + i * (2 * BT) + (u * BT + q + 1))
                            nc.vector.tensor_scalar(d_ring[:, u * BT + q, :], iota_n[:, :],
                                                    srec[:, bass.ds(i * (2 * BT) + (u * BT + q), 1), 1], None,
                                                    ALU.is_equal)
                        g = bass.ds(i * (2 * BT) + u * BT, BT)
                        nc.vector.tensor_tensor(
                            w_ring[:, u * BT:(u + 1) * BT, :].rearrange("p s (k i) -> p s k i", i=BS),
                            own_hot[:, g, :].unsqueeze(2).broadcast_to([P, BT, WC, BS]),
                            wpart[:, g, :].unsqueeze(3).broadcast_to([P, BT, WC, BS]), ALU.mult
                        ).then_inc(S["wd_ready"], 1)

                with nc.vector.Fori(0, FIRST // (2 * BT)) as i:
                    two_blocks(i)
                dve.wait_ge(S["rest_split"], r + 1)
                dve.sem_inc(S["split_steps"], 1)
                with nc.vector.Fori(FIRST // (2 * BT), NB // 2) as i:
                    two_blocks(i)
                make_rows(r * INDEX_STEPS + 2 * INDEX_STEPS, slice(0, ET), "rows_made")
                dve.wait_ge(S["rows_made"], r + 2)
                dve.sem_inc(S["rest_rows_made"], 1)
                dve.wait_ge(S["wd_ready"], r * NB + NB)
                dve.sem_inc(S["round_built"], 1)
            dve.wait_ge(S["b_ready"], rounds * NB + 2)
            for t in range(NT):
                nc.vector.tensor_scalar(no_edge[:, t, :], c2[:, t, :], 0.0, NO_EDGE, ALU.is_equal, ALU.mult
                                        ).then_inc(S["no_edge_ready"], 1)
            nc.vector.tensor_reduce(deg[:, :], c2, AX.X, ALU.add).then_inc(S["deg_ready"], 1)

            def peaks(h):
                s, k = score[h % 3], peak[:, 2 * (h % 2):2 * (h % 2) + 2, :]
                dve.wait_ge(S["score_ready"], h * NT + 2)
                if h >= 2:
                    dve.wait_ge(S["peak_mm"], h - 1)
                nc.vector.tensor_tensor(k[:, 0, :], s[:, 0, :], s[:, 1, :], ALU.max).then_inc(S["peak_steps"], 1)
                dve.wait_ge(S["score_ready"], h * NT + 4)
                nc.vector.tensor_tensor(k[:, 1, :], s[:, 2, :], s[:, 3, :], ALU.max).then_inc(S["peak_steps"], 1)
                dve.wait_ge(S["peak_steps"], 2 * h + 2)
                nc.vector.tensor_tensor(k[:, 0, :], k[:, 0, :], k[:, 1, :], ALU.max).then_inc(S["peaks"], 1)

            def diags(h):
                dve.wait_ge(S["peak_mm"], h + 1)
                m = m_col[:, h, :]
                nc.vector.tensor_reduce(m, bank[4][:, :].rearrange("p (t j) -> p t j", t=NT), AX.X, ALU.max
                                        ).then_inc(S["diag_steps"], 1)
                dve.wait_ge(S["diag_steps"], 2 * h + 1)
                nc.vector.tensor_single_scalar(m, m, M_FLOOR, ALU.max).then_inc(S["diag_steps"], 1)
                dve.wait_ge(S["diag_steps"], 2 * h + 2)
                if h >= 2:
                    dve.wait_ge(S["floor_mm"], h - 1)
                nc.vector.tensor_tensor(diag[:, h % 2, :, :], ident[:, :].unsqueeze(1).broadcast_to([P, NT, P]),
                                        m.unsqueeze(2).broadcast_to([P, NT, P]), ALU.mult
                                        ).then_inc(S["diag_ready"], 1)

            def lower(h):
                dve.wait_ge(S["floor_mm"], h + 1)
                for t in range(NT):
                    s = score[h % 3][:, t, :]
                    nc.vector.tensor_tensor(s, s, bank[5][:, :], ALU.subtract).then_inc(S["lowered"], 1)

            def normalise(h):
                dve.wait_ge(S["pv_mm"], h + 1)
                o = bank[6 + h % 2][:, 0:NT * (DH + 1)].rearrange("p (t d) -> p t d", t=NT)
                link(nc.vector.tensor_single_scalar(rsum[:, h % 2, :], o[:, :, DH], TINY, ALU.max))
                link(nc.vector.reciprocal(rsum[:, h % 2, :], rsum[:, h % 2, :]))
                nc.vector.tensor_tensor(z_sb[:, :, h * DH:(h + 1) * DH], o[:, :, 0:DH],
                                        rsum[:, h % 2, :].unsqueeze(2).broadcast_to([P, NT, DH]), ALU.mult
                                        ).then_inc(S["att_ready"], 1)

            for n in range(H + 3):
                if n >= 2 and n - 2 < H:
                    lower(n - 2)
                if n == H:
                    dve.wait_ge(S["deg_ready"], 1)
                    nc.vector.tensor_tensor(diag[:, 0, :, :], ident[:, :].unsqueeze(1).broadcast_to([P, NT, P]),
                                            deg[:, :].unsqueeze(2).broadcast_to([P, NT, P]), ALU.mult
                                            ).then_inc(S["deg_diag"], 1)
                if n >= 1 and n - 1 < H:
                    diags(n - 1)
                if n < H:
                    peaks(n)
                if n == H + 1:
                    for t in range(NT // 2, NT):
                        dve.wait_ge(S["e_ready"], (H - 1) * NT + t + 1)
                        p = big[:, t * H + H - 1, :]
                        nc.vector.tensor_tensor(p, score[(H - 1) % 3][:, t, :], p, ALU.mult
                                                ).then_inc(S["last_p_ready"], 1)
                if n == H + 1:
                    dve.wait_ge(S["deg_mm"], 1)
                    nc.vector.tensor_copy(dinv_bc[:, :], bank[0][:, :]).then_inc(S["deg_ready"], 1)
                if n >= 3:
                    normalise(n - 3)
                if n == NT:
                    dve.wait_ge(S["rows_in"], 16 * (len(ROWS) - 1))
                if NT <= n < 2 * NT:
                    mark(nc.vector.tensor_tensor(h_sb[:, n - NT, :], h_sb[:, n - NT, :], rowp("bo"), ALU.add))
            settle()
            for t in range(NT):
                dve.wait_ge(S["t_ready"], NT + t + 1)
                split_hi("att", t, c1_lo, t_at)
            for t in range(NT):
                split_lo("att", t, c1_lo, t_at)
            for t in range(NT + 1):
                if t < NT:
                    dve.wait_ge(S["wo_mm"], t + 1)
                    link(nc.vector.tensor_tensor(h_sb[:, t, :], bank[4 + t][:, :], h_sb[:, t, :], ALU.add))
                    moments(t, h_sb, "ln_var")
                if t >= 1:
                    ln_coef(2, t - 1)
                    ln_plain(2, t - 1, h_sb)
            for t in range(NT):
                dve.wait_ge(S["t_ready"], 2 * NT + t + 1)
                split_hi("ff_in", t, t_lo, t_at)
            for t in range(NT):
                split_lo("ff_in", t, t_lo, t_at)
            dve.wait_ge(S["deg_ready"], 2)
            nc.vector.tensor_single_scalar(rcnt_bc[:, :], dinv_bc[:, :], 1.0, ALU.max).then_inc(S["deg_ready"], 1)
            dve.wait_ge(S["deg_ready"], 3)
            nc.vector.reciprocal(rcnt_bc[:, :], rcnt_bc[:, :]).then_inc(S["rcnt_ready"], 1)
            for f in range(FT):
                dve.wait_ge(S["ff1_ready"], f + 1)
                split_lo("ff_mid", f, wide_lo, wide_at)
            dve.wait_ge(S["deg_std"], 2)
            nc.vector.reciprocal(dinv_bc[:, :], dinv_bc[:, :]).then_inc(S["dinv_ready"], 1)
            nc.vector.reciprocal(dinv_c[:, :], dinv_c[:, :]).then_inc(S["dinv_ready"], 1)
            for t in range(NT):
                dve.wait_ge(S["base_ready"], t + 1)
                dve.wait_ge(S["ff2_mm"], t + 1)
                link(nc.vector.tensor_tensor(x_sb[:, t, :], bank[4 + t][:, :], h_sb[:, t, :], ALU.add))
                moments(t, x_sb, "ln_var")
                ln_coef(3, t)
                dve.wait_ge(S["h_ready"], NT + t + 1)
                split_lo("h1", t, h_at, z_at, spare_at)
                if t == NT - 2:
                    weight_hi("w_lr", 32)
            for t in range(NT):
                dve.wait_ge(S["mean_ready"], t + 1)
                split_hi("mean", t, wide_lo, wide_at)
            for t in range(NT):
                dve.wait_ge(S["t_ready"], 3 * NT + t + 1)
                split_hi("h1_t", t, t_lo, t_at)
            for t in range(NT):
                split_lo("h1_t", t, t_lo, t_at)
            for t in range(NT):
                mark(nc.vector.tensor_tensor(x_sb[:, t, :], x_sb[:, t, :], h_sb[:, t, :], ALU.add))
            settle()
            weight_hi("w1_2")
            for t in range(NT):
                c = slice(t, t + 1)
                dve.wait_ge(S["lin1_ready"], t + 1)
                moments(t, z_sb, "bn_var")
                dve.wait_ge(S["bn_std"], t + 1)
                link(nc.vector.reciprocal(rstd[:, c], std[:, c]))
                link(nc.vector.tensor_tensor(rstd[:, c], rstd[:, c], colp("gamma1", t), ALU.mult))
                link(nc.vector.scalar_tensor_tensor(out=shift[:, c], in0=mv[:, t, 0:1], scalar=-1.0,
                                                    in1=rstd[:, c], op0=ALU.mult, op1=ALU.mult))
                nc.vector.tensor_tensor(shift[:, c], shift[:, c], colp("beta1", t), ALU.add
                                        ).then_inc(S["bn_coef"], 1)
            for t in range(NT + 1):
                if t < NT:
                    dve.wait_ge(S["back_mm"], t + 1)
                    link(nc.vector.tensor_tensor(x_sb[:, t, :], bank[4 + t][:, :], x_sb[:, t, :], ALU.add))
                    moments(t, x_sb, "ln_var")
                if t >= 1:
                    ln_coef(4, t - 1, divided=True)
            for t in range(NT):
                dve.wait_ge(S["agg2_ready"], t + 1)
                split_hi("gcn_in", t, t_lo, t_at)
            weight_hi("w2_2")
            for f in range(FT):
                dve.wait_ge(S["gcn1_ready"], f + 1)
                split_lo("gcn_mid", f, wide_lo, wide_at)
            weight_hi("w_3", 32)
            for t in range(NT):
                dve.wait_ge(S["gcn2_ready"], t + 1)
                split_lo("gcn_out", t, z_at, spare_at)
            dve.wait_ge(S["c2_ready"], NT)
            for t in range(NT):
                nc.vector.tensor_copy(c2_hi.rounded[:, t, :], c2[:, t, :]).then_inc(S["c2_hi_ready"], 1)
            for t in range(NT + 1):
                if t < NT:
                    dve.wait_ge(S["agg2b_mm"], t + 1)
                    link(nc.vector.tensor_tensor(h_sb[:, t, :], bank[t][:, :], rowp("b2_2"), ALU.add))
                    link(nc.vector.scalar_tensor_tensor(out=x_sb[:, t, :], in0=h_sb[:, t, :], scalar=0.0,
                                                        in1=x_sb[:, t, :], op0=ALU.max, op1=ALU.add))
                    moments(t, x_sb, "ln_var")
                if t >= 1:
                    ln_coef(5, t - 1)
            for t in range(NT):
                dve.wait_ge(S["agg3_ready"], t + 1)
                split_hi("gin_in", t, z_at, spare_at)
            dve.wait_ge(S["h_ready"], 3 * NT)
            for t in range(NT):
                mark(nc.vector.tensor_tensor(x_sb[:, t, :], x_sb[:, t, :], rowp("beta3"), ALU.add))
            settle()
            for t in range(NT):
                dve.wait_ge(S["gin1_ready"], t + 1)
                split_lo("gin_mid", t, wide_lo, wide_at)
            for t in range(NT):
                c = slice(t, t + 1)
                dve.wait_ge(S["gin2_mm"], t + 1)
                link(nc.vector.tensor_tensor(h_sb[:, t, :], bank[4 + t][:, :], rowp("b2_3"), ALU.add))
                moments(t, h_sb, "ln_var")
                dve.wait_ge(S["ln_var"], 6 * NT + t + 1)
                mark(nc.vector.scalar_tensor_tensor(out=z_sb[:, t, :], in0=h_sb[:, t, :], scalar=mv[:, t, 0:1],
                                                    in1=rowp("gamma3"), op0=ALU.subtract, op1=ALU.mult))
                dve.wait_ge(S["ln_std"], 6 * NT + t + 1)
                link(nc.vector.reciprocal(rstd[:, c], std[:, c]))
                nc.vector.scalar_tensor_tensor(out=z_sb[:, t, :], in0=z_sb[:, t, :], scalar=rstd[:, c],
                                               in1=x_sb[:, t, :], op0=ALU.mult, op1=ALU.add
                                               ).then_inc(S["out_ready"], 1)

        @block.tensor
        def _(pe):
            def tile(ap, t):
                return ap[:, t * P:(t + 1) * P]

            def turn(source, first, done):
                for c in range(NT):
                    for t in range(NT):
                        last = nc.tensor.transpose(tile(bank[first + c], t), tile(source[:, t, :], c), ident[:, :])
                    last.then_inc(S[done], 1)

            def turn_by_row(source, first, ready, base, done, warm=None):
                for t in range(NT):
                    if warm and t == NT // 2:
                        keep_warm(warm, 7)
                    pe.wait_ge(S[ready], base + t + 1)
                    for c in range(NT):
                        last = nc.tensor.transpose(tile(bank[first + c], t), tile(source[:, t, :], c), ident[:, :])
                        if t == NT - 1:
                            last.then_inc(S[done], 1)

            def halves(hi, lo, n=NT):
                return [(hi.rounded[:, k, :], lo.rounded[:, k, :]) for k in range(n)]

            def reads(name, n=NT):
                hi_by, before_hi, lo_by, before_lo = parts[name]
                return [((S[hi_by], before_hi + k + 1), (S[lo_by], before_lo + k + 1)) for k in range(n)]

            def product_by_row(banks, lhs, rhs, ready, done):
                terms = list(zip(lhs, rhs))
                for n in range(len(terms) + 1):
                    if n < len(terms):
                        a, r = terms[n]
                        pe.wait_ge(*ready[n][0])
                        for m, b in enumerate(banks):
                            nc.tensor.matmul(bank[b][:, :], tile(a[0], m), r[0], start=(n == 0), stop=False)
                    if n >= 1:
                        a, r = terms[n - 1]
                        pe.wait_ge(*ready[n - 1][1])
                        for m, b in enumerate(banks):
                            nc.tensor.matmul(bank[b][:, :], tile(a[0], m), r[1], start=False, stop=False)
                            last = nc.tensor.matmul(bank[b][:, :], tile(a[1], m), r[0], start=False,
                                                    stop=(n == len(terms)))
                            if n == len(terms):
                                last.then_inc(S[done], 1)

            def product_in_parts(banks, lhs, rhs, ready, done, group=1, weight_lo=None):
                terms = list(zip(lhs, rhs))

                def highs(m):
                    for k, (a, r) in enumerate(terms):
                        if ready and m == 0:
                            pe.wait_ge(*ready[k][0])
                        nc.tensor.matmul(bank[banks[m]][:, :], tile(a[0], m), r[0], start=(k == 0), stop=False)

                for m in range(group):
                    highs(m)
                for m, b in enumerate(banks):
                    if m >= group:
                        highs(m)
                    if m == 0 and weight_lo:
                        pe.wait_ge(S[weight_lo], 4)
                    for k, (a, r) in enumerate(terms):
                        if ready and m == 0:
                            pe.wait_ge(*ready[k][1])
                        nc.tensor.matmul(bank[b][:, :], tile(a[0], m), r[1], start=False, stop=False)
                        last = nc.tensor.matmul(bank[b][:, :], tile(a[1], m), r[0], start=False,
                                                stop=(k == len(terms) - 1))
                    last.then_inc(S[done], 1)

            def keep_warm(b, n):
                for _ in range(n):
                    nc.tensor.matmul(bank[b][:, :], iota_n[:, 0:P], iota_n[:, :], start=True, stop=True)

            def weight(name, n=FT):
                pe.wait_ge(S[name + "_hi"], 4)
                lo, hi = weights[name]
                if n == NT:
                    lo, hi = (Place(*(v.rearrange("p (k a) n -> p k (a n)", a=2) for v in a)) for a in (lo, hi))
                return halves(hi, lo, n)

            def product(banks, lhs, rhs, done, ready=None, base=0):
                for m, b in enumerate(banks):
                    for k, (a, r) in enumerate(zip(lhs, rhs)):
                        if ready and m == 0:
                            pe.wait_ge(S[ready], base + k + 1)
                        last = nc.tensor.matmul(bank[b][:, :], tile(a, m), r, start=(k == 0),
                                                stop=(k == len(lhs) - 1))
                    last.then_inc(S[done], 1)

            def ks(a, n=NT):
                return [a[:, k, :] for k in range(n)]

            lo, hi = (0, 1, 2, 3), (4, 5, 6, 7)
            pe.wait_ge(S["consts"], 2)
            pe.wait_ge(S["edge_sums"], 1)
            tot = prefix.rearrange("p (b t) -> p b t", b=NB)[:, :, ET - 1]
            nc.tensor.matmul(bank[7][:, 0:NB], before[:, :], tot, start=True, stop=True).then_inc(S["edge_bases"], 1)
            nc.tensor.matmul(bank[7][:, NB:2 * NB], ones[:, :], tot, start=True, stop=True
                             ).then_inc(S["edge_bases"], 1)
            turn_by_row(z_sb, 0, "z_ready", 0, "turned")
            pe.wait_ge(S["wq_in"], 16)
            pe.wait_ge(S["earlier_ready"], 1)
            product(hi, ks(wslot[:, 0, :, :]), ks(t_sb), "q_mm", "t_ready")
            pe.wait_ge(S["wk_in"], 16)
            product(lo, ks(wslot[:, 1, :, :]), ks(t_sb), "k_mm")
            pe.wait_ge(S["wv_in"], 16)
            pe.wait_ge(S["q_ready"], NT)
            product(hi, ks(t_sb), ks(wslot[:, 2, :, :]), "v_mm")

            pe.wait_ge(S["v_ready"], NT)
            pe.sem_inc(S["wd_used"], 2 * BT)
            pe.wait_ge(S["srec_in"], 16)
            pe.wait_ge(S["k_ready"], NT)
            keep_warm(0, 8)
            rounds = pe.value_load(rounds_i[0:1, 0:1], min_val=1, max_val=E // CAP + 1)
            with nc.tensor.Fori(0, rounds) as r:
                with nc.tensor.Fori(0, NB // 2) as i:
                    for u in range(2):
                        pe.wait_ge(S["b_out"], r * NB + i * 2 + (u + 1))
                        pe.wait_ge(S["wd_ready"], r * NB + i * 2 + (u + 1))
                        for q in range(BT):
                            slot = u * BT + q
                            for j in range(NT):
                                to = tile(d_ring[:, slot, :], j)
                                sums = bank[4 + 2 * u + j // 2][:, j % 2 * SC:(j % 2 + 1) * SC]
                                nc.tensor.matmul(sums, to, w_ring[:, slot, 0:SC],
                                                 start=(q == 0 and j % 2 == 0), stop=False)
                                for k in (1, 2):
                                    last = nc.tensor.matmul(
                                        sums[:, BS:], to, w_ring[:, slot, SC + (k - 1) * P:SC + k * P],
                                        start=False, stop=(q == BT - 1 and j == 1 and k == 2))
                            last.then_inc(S["wd_used"], 1)
                        nc.tensor.matmul(bank[5 + 2 * u][:, 2 * SC:2 * SC + BS], ident_b[:, :], ident_b[:, 0:BS],
                                         start=False, stop=True).then_inc(S["b_mm"], 1)

            keep_warm(0, 11)
            pe.wait_ge(S["b_ready"], rounds * NB + 2)
            turn(c2, 4, "c2_turned")

            def scores(h):
                r = slice((h % 2) * DH, (h % 2 + 1) * DH)
                for t in range(NT):
                    if h == 0:
                        pe.wait_ge(S["no_edge_ready"], t + 1)
                    else:
                        pe.wait_ge(S["score_ready"], (h - 1) * NT + t + 1)
                    b = bank[t][:, :]
                    nc.tensor.matmul(b, ident_b[:, :], no_edge[:, t, :], start=True, stop=False)
                    nc.tensor.matmul(b, k_t[r, h // 2, t * P:(t + 1) * P], q_t[r, h // 2, :], start=False,
                                     stop=True).then_inc(S["st_mm"], 1)

            def peaks_turned(h):
                pe.wait_ge(S["peaks"], h + 1)
                if h == 0:
                    pe.wait_ge(S["c1_ready"], NT)
                if h >= 1:
                    pe.wait_ge(S["diag_ready"], h)
                for t in range(NT):
                    last = nc.tensor.transpose(tile(bank[4], t), tile(peak[:, 2 * (h % 2), :], t), ident[:, :])
                last.then_inc(S["peak_mm"], 1)

            def floor_row(h):
                pe.wait_ge(S["diag_ready"], h + 1)
                if h >= 1:
                    pe.wait_ge(S["lowered"], h * NT)
                nc.tensor.matmul(bank[5][:, :], ones[:, :], diag[:, h % 2, :, :].rearrange("p t c -> p (t c)"),
                                 start=True, stop=True).then_inc(S["floor_mm"], 1)

            def weighted(h):
                pe.wait_ge(S["p_ready"], (h + 1) * NT - (NT // 2 if h == H - 1 else 0))
                if h == H - 1:
                    pe.wait_ge(S["last_p_ready"], NT // 2)
                if h >= 2:
                    pe.wait_ge(S["att_ready"], h - 1)
                for m in range(NT):
                    o = bank[6 + h % 2][:, m * (DH + 1):(m + 1) * (DH + 1)]
                    for t in range(NT):
                        last = nc.tensor.matmul(o, tile(big[:, t * H + h, :], m), v_sb[:, t, h, :],
                                                start=(t == 0), stop=(t == NT - 1))
                last.then_inc(S["pv_mm"], 1)

            for n in range(H + 3):
                if n < H:
                    scores(n)
                if n >= 1 and n - 1 < H:
                    peaks_turned(n - 1)
                if n >= 3:
                    weighted(n - 3)
                elif n >= 1:
                    keep_warm(7, 8)
                if n >= 1 and n - 1 < H:
                    floor_row(n - 1)
                if n == H:
                    pe.wait_ge(S["score_ready"], H * NT)
                    pe.wait_ge(S["deg_diag"], 1)
                    nc.tensor.matmul(bank[0][:, :], ones[:, :], diag[:, 0, :, :].rearrange("p t c -> p (t c)"),
                                     start=True, stop=True).then_inc(S["deg_mm"], 1)
            pe.wait_ge(S["deg_ready"], 2)
            pe.wait_ge(S["att_ready"], H)
            turn(z_sb, 0, "turned")
            pe.wait_ge(S["wo_in"], 16)
            pe.wait_ge(S["wo_hi"], NT)
            pe.wait_ge(S["wo_lo"], NT)
            product_in_parts(hi, halves(t_at, c1_lo), halves(c1_hi, t_lo), reads("att"), "wo_mm", group=2)
            turn_by_row(z_sb, 0, "z_ready", NT, "turned", warm=4)
            product_in_parts(hi + lo, weight("w1_0", NT), halves(t_at, t_lo), reads("ff_in"), "ff1_mm",
                             group=NT, weight_lo="w1_0_lo")
            pe.wait_ge(S["ff1_ready"], NT)
            product_in_parts(hi, halves(wide_at, wide_lo, FT), weight("w2_0"), reads("ff_mid", FT), "ff2_mm",
                             weight_lo="w2_0_lo")
            pe.wait_ge(S["mean_c1_ready"], NT)
            product_by_row(lo, halves(z_at, spare_at), halves(c1_hi, c1_lo), reads("h1"), "agg1_mm")
            pe.wait_ge(S["ln_coef"], 4 * NT)
            turn(h_sb, 4, "turned")
            w_lr = weight("w_lr")

            def back(t):
                pe.wait_ge(S["bn_ready"], t + 1)
                for c in range(NT):
                    last = nc.tensor.transpose(tile(bank[4 + c], t), tile(bn_t[:, t, :], c), ident[:, :])
                    if t == NT - 1:
                        last.then_inc(S["back_mm"], 1)

            for m in range(NT):
                if m == 0:
                    pe.wait_ge(S["mean_ready"], NT)
                product_in_parts([m], [(tile(a, m), tile(b, m)) for a, b in w_lr],
                                 halves(wide_at, wide_lo) + halves(t_at, t_lo),
                                 reads("mean") + reads("h1_t") if m == 0 else None, "lin1_mm",
                                 weight_lo="w_lr_lo")
                if m >= 1:
                    back(m - 1)
            back(NT - 1)
            keep_warm(0, 18)
            pe.wait_ge(S["gcn_c1_ready"], NT)
            product_by_row(lo, halves(spare_at, z_at), halves(c1_hi, c1_lo), reads("y"), "agg2_mm")
            product_in_parts(hi + lo, weight("w1_2", NT), halves(t_at, t_lo), reads("gcn_in"), "gcn1_mm",
                             group=NT, weight_lo="w1_2_lo")
            pe.wait_ge(S["gcn1_ready"], NT)
            product_in_parts(hi, halves(wide_at, wide_lo, FT), weight("w2_2"), reads("gcn_mid", FT), "gcn2_mm",
                             weight_lo="w2_2_lo")
            product_in_parts(lo, halves(c1_hi, c1_lo), halves(spare_at, z_at), reads("gcn_out"), "agg2b_mm")
            pe.wait_ge(S["c2_hi_ready"], NT)
            pe.wait_ge(S["c2_ready"], 2 * NT)
            product_by_row(hi, halves(t_at, h_at), halves(c2_hi, c2_lo), reads("h3"), "agg3_mm")
            w_3 = weight("w_3")
            product_in_parts(lo, w_3[:NT], halves(spare_at, z_at), reads("gin_in"), "gin1_mm",
                             group=NT, weight_lo="w_3_lo")
            product_in_parts(hi, halves(wide_at, wide_lo), w_3[NT:], reads("gin_mid"), "gin2_mm")


def kernel(**inputs):
    import numpy as np
    import concourse.bacc as bacc
    from concourse.bass_utils import run_bass_kernel_spmd

    def as_cols(*vectors):
        return np.ascontiguousarray(np.concatenate([np.asarray(v).reshape(-1, P) for v in vectors]).T)

    g = {k: np.asarray(v) for k, v in inputs.items()}
    arrays = {
        "x": g["x"], "src": g["src"], "dst": g["dst"], "edge_bias": g["edge_attr_8"],
        "gin_eps": g["L3_gnn_eps"].reshape(1),
        "cols": as_cols(g["L0_gnn_bq"], g["L0_gnn_bk"], g["L0_gnn_ln1_g"], g["L0_gnn_ln1_b"], g["L0_gnn_ln2_g"],
                        g["L0_gnn_ln2_b"], g["L0_gnn_b1"], g["L1_gnn_b_l"], g["L1_gnn_gamma"], g["L1_gnn_beta"],
                        g["L2_gnn_b1"], g["L3_gnn_b1"]),
        "rows": np.stack([g["L0_gnn_bv"], g["L0_gnn_bo"], g["L0_gnn_b2"], g["L2_gnn_b2"], g["L3_gnn_b2"],
                          g["L3_gnn_gamma"], g["L3_gnn_beta"]]),
        "wq": g["L0_gnn_Wq"], "wk": g["L0_gnn_Wk"], "wv": g["L0_gnn_Wv"], "wo": g["L0_gnn_Wo"],
        "w1_0": g["L0_gnn_W1"], "w2_0": g["L0_gnn_W2"],
        "wl_t": g["L1_gnn_W_l"].T, "wr_t": g["L1_gnn_W_r"].T,
        "w1_2": g["L2_gnn_W1"], "w2_2": g["L2_gnn_W2"],
        "w1_3t": g["L3_gnn_W1"].T, "w2_3t": g["L3_gnn_W2"].T,
    }
    nc = bacc.Bacc("TRN2", target_bir_lowering=False, num_devices=1)
    feeds, args = {}, []
    for name, a in arrays.items():
        a = np.ascontiguousarray(a)
        feeds["in_" + name] = a
        args.append(nc.dram_tensor("in_" + name, a.shape, mybir.dt.from_np(a.dtype), kind="ExternalInput").ap())
    args.append(nc.dram_tensor("out_x", (N, D), F32, kind="ExternalOutput").ap())
    gnn_kernel(nc, *args)
    r = run_bass_kernel_spmd(nc, [feeds], core_ids=[0])
    return r.results[0]["out_x"]
```
